# Optimizing a Trainium2 kernel written in Bass

```python
import numpy as np
import jax
import jax.numpy as jnp

def _softmax(x, axis=-1):
    return jax.nn.softmax(x, axis=axis)

def _gelu(x):
    return jax.nn.gelu(x, approximate=True)

def _silu(x):
    return jax.nn.silu(x)

def _sigmoid(x):
    return jax.nn.sigmoid(x)

def _layernorm(x, axis=-1, eps=1e-05):
    m = jnp.mean(x, axis=axis, keepdims=True)
    v = jnp.var(x, axis=axis, keepdims=True)
    return (x - m) / jnp.sqrt(v + eps)

def _scatter_add(tgt, idx, src, axis=0):
    return tgt.at[idx].add(src)

def _segment_sum(src, seg, n):
    return jax.ops.segment_sum(src, seg, n)
kernel_name = 'mk_gnn_resnorm_d2_gnn_r32_de09c1'

def setup_inputs(seed: int=0):
    np.random.seed(seed)
    _w = jnp.asarray

    def _rec_inputs():
        import jax
        import jax.numpy as jnp
        _gk = jax.random.key(seed)
        x = -0.0003713 + 1 * jax.random.normal(jax.random.fold_in(_gk, 1), (3125, 128), jnp.float32)
        src = jax.random.randint(jax.random.fold_in(_gk, 2), (100000,), 0, 3125, jnp.int32)
        dst = jax.random.randint(jax.random.fold_in(_gk, 3), (100000,), 0, 3125, jnp.int32)
        _o = jnp.argsort(dst, stable=True)
        src = src[_o]
        dst = dst[_o]
        edge_attr_4 = jax.random.uniform(jax.random.fold_in(_gk, 11), (100000, 4), jnp.float32, 0.0, 1)
        return (x, src, dst, edge_attr_4)
    x, src, dst, edge_attr_4 = _rec_inputs()

    def _L0_gnn_setup():
        import jax, jax.numpy as jnp
        import numpy as np
        N_NODES = 3125
        N_EDGES = 50000
        D = 128
        L = 4
        H = 32
        BN_EPS = 1e-05

        def _bn(x, g, b):
            m = jnp.mean(x, axis=0)
            v = jnp.var(x, axis=0)
            return g * (x - m) * jax.lax.rsqrt(v + BN_EPS) + b
        key = jax.random.key(seed)
        ks = jax.random.split(key, 8)
        X = jax.random.normal(ks[0], (N_NODES, D), dtype=jnp.float32)
        edge_index = jax.random.randint(ks[1], (2, N_EDGES), 0, N_NODES, dtype=jnp.int64)
        eps = jax.random.normal(ks[2], (L,), dtype=jnp.float32)
        W1 = jax.random.normal(ks[3], (L, H, D), dtype=jnp.float32) * 0.1
        W2 = jax.random.normal(ks[4], (L, H, H), dtype=jnp.float32) * 0.1
        W3 = jax.random.normal(ks[5], (L, D, H), dtype=jnp.float32) * 0.1
        return {'X': X, 'edge_index': edge_index, 'eps': eps, 'W1': W1, 'b1': jnp.zeros((L, H), jnp.float32), 'g1': jnp.ones((L, H), jnp.float32), 'bt1': jnp.zeros((L, H), jnp.float32), 'W2': W2, 'b2': jnp.zeros((L, H), jnp.float32), 'g2': jnp.ones((L, H), jnp.float32), 'bt2': jnp.zeros((L, H), jnp.float32), 'W3': W3, 'b3': jnp.zeros((L, D), jnp.float32)}
    _L0_gnn_all = _L0_gnn_setup()
    _L0_gnn_in = {k: v for k, v in _L0_gnn_all.items() if k in ('eps', 'W1', 'b1', 'g1', 'bt1', 'W2', 'b2', 'g2', 'bt2', 'W3', 'b3')}
    del _L0_gnn_all

    def _L1_gnn_setup():
        import jax, jax.numpy as jnp
        import numpy as np
        N_NODES = 3125
        N_EDGES = 50000
        HIDDEN = 128
        N_ETYPES = 4
        N_STEPS = 4

        def _gru_cell(x, h, W_ih, W_hh, b_ih, b_hh):
            gi = x @ W_ih.T + b_ih
            gh = h @ W_hh.T + b_hh
            ir, iz, inn = jnp.split(gi, 3, axis=1)
            hr, hz, hn = jnp.split(gh, 3, axis=1)
            r = jax.nn.sigmoid(ir + hr)
            z = jax.nn.sigmoid(iz + hz)
            n = jnp.tanh(inn + r * hn)
            return (1.0 - z) * n + z * h
        key = jax.random.key(seed)
        ks = jax.random.split(key, 10)
        s = 1.0 / np.sqrt(HIDDEN)
        node_feat = jax.random.normal(ks[0], (N_NODES, HIDDEN), dtype=jnp.float32)
        edge_index = jax.random.randint(ks[1], (2, N_EDGES), 0, N_NODES)
        edge_feat = jax.random.uniform(ks[2], (N_EDGES, N_ETYPES), dtype=jnp.float32)
        W_edge = jax.random.uniform(ks[3], (N_ETYPES, HIDDEN, HIDDEN), minval=-s, maxval=s, dtype=jnp.float32)
        b_edge = jax.random.uniform(ks[4], (N_ETYPES, HIDDEN), minval=-s, maxval=s, dtype=jnp.float32)
        W_ih = jax.random.uniform(ks[5], (3 * HIDDEN, HIDDEN), minval=-s, maxval=s, dtype=jnp.float32)
        W_hh = jax.random.uniform(ks[6], (3 * HIDDEN, HIDDEN), minval=-s, maxval=s, dtype=jnp.float32)
        b_ih = jax.random.uniform(ks[7], (3 * HIDDEN,), minval=-s, maxval=s, dtype=jnp.float32)
        b_hh = jax.random.uniform(ks[8], (3 * HIDDEN,), minval=-s, maxval=s, dtype=jnp.float32)
        return {'node_feat': node_feat, 'edge_index': edge_index, 'edge_feat': edge_feat, 'W_edge': W_edge, 'b_edge': b_edge, 'W_ih': W_ih, 'W_hh': W_hh, 'b_ih': b_ih, 'b_hh': b_hh}
    _L1_gnn_all = _L1_gnn_setup()
    _L1_gnn_in = {k: v for k, v in _L1_gnn_all.items() if k in ('W_edge', 'b_edge', 'W_ih', 'W_hh', 'b_ih', 'b_hh')}
    del _L1_gnn_all
    return {'x': x, 'src': src, 'dst': dst, 'edge_attr_4': edge_attr_4, 'L0_gnn_eps': _L0_gnn_in['eps'], 'L0_gnn_W1': _L0_gnn_in['W1'], 'L0_gnn_b1': _L0_gnn_in['b1'], 'L0_gnn_g1': _L0_gnn_in['g1'], 'L0_gnn_bt1': _L0_gnn_in['bt1'], 'L0_gnn_W2': _L0_gnn_in['W2'], 'L0_gnn_b2': _L0_gnn_in['b2'], 'L0_gnn_g2': _L0_gnn_in['g2'], 'L0_gnn_bt2': _L0_gnn_in['bt2'], 'L0_gnn_W3': _L0_gnn_in['W3'], 'L0_gnn_b3': _L0_gnn_in['b3'], 'L1_gnn_W_edge': _L1_gnn_in['W_edge'], 'L1_gnn_b_edge': _L1_gnn_in['b_edge'], 'L1_gnn_W_ih': _L1_gnn_in['W_ih'], 'L1_gnn_W_hh': _L1_gnn_in['W_hh'], 'L1_gnn_b_ih': _L1_gnn_in['b_ih'], 'L1_gnn_b_hh': _L1_gnn_in['b_hh']}

def reference(x, src, dst, edge_attr_4, L0_gnn_eps, L0_gnn_W1, L0_gnn_b1, L0_gnn_g1, L0_gnn_bt1, L0_gnn_W2, L0_gnn_b2, L0_gnn_g2, L0_gnn_bt2, L0_gnn_W3, L0_gnn_b3, L1_gnn_W_edge, L1_gnn_b_edge, L1_gnn_W_ih, L1_gnn_W_hh, L1_gnn_b_ih, L1_gnn_b_hh):
    import jax
    import jax.numpy as jnp

    def _L0_gnn_ref(X, edge_index, eps, W1, b1, g1, bt1, W2, b2, g2, bt2, W3, b3):
        import jax, jax.numpy as jnp
        import numpy as np
        N_NODES = 3125
        N_EDGES = 50000
        D = 128
        L = 4
        H = 32
        BN_EPS = 1e-05

        def _bn(x, g, b):
            m = jnp.mean(x, axis=0)
            v = jnp.var(x, axis=0)
            return g * (x - m) * jax.lax.rsqrt(v + BN_EPS) + b
        src, dst = (edge_index[0], edge_index[1])
        for l in range(L):
            S = jax.ops.segment_sum(X[src], dst, num_segments=N_NODES)
            Z = (1.0 + eps[l]) * X + S
            h = jax.nn.relu(_bn(Z @ W1[l].T + b1[l], g1[l], bt1[l]))
            h = jax.nn.relu(_bn(h @ W2[l].T + b2[l], g2[l], bt2[l]))
            X = h @ W3[l].T + b3[l]
        return X

    def _L1_gnn_ref(node_feat, edge_index, edge_feat, W_edge, b_edge, W_ih, W_hh, b_ih, b_hh):
        import jax, jax.numpy as jnp
        import numpy as np
        N_NODES = 3125
        N_EDGES = 50000
        HIDDEN = 128
        N_ETYPES = 4
        N_STEPS = 4

        def _gru_cell(x, h, W_ih, W_hh, b_ih, b_hh):
            gi = x @ W_ih.T + b_ih
            gh = h @ W_hh.T + b_hh
            ir, iz, inn = jnp.split(gi, 3, axis=1)
            hr, hz, hn = jnp.split(gh, 3, axis=1)
            r = jax.nn.sigmoid(ir + hr)
            z = jax.nn.sigmoid(iz + hz)
            n = jnp.tanh(inn + r * hn)
            return (1.0 - z) * n + z * h
        etypes = jnp.argmax(edge_feat, axis=1)
        src, dst = (edge_index[0], edge_index[1])
        N = node_feat.shape[0]
        h = node_feat
        for _ in range(N_STEPS):
            trans = jnp.einsum('nd,tod->tno', h, W_edge) + b_edge[:, None, :]
            msg = trans[etypes, src]
            a = jax.ops.segment_sum(msg, dst, num_segments=N)
            h = _gru_cell(a, h, W_ih, W_hh, b_ih, b_hh)
        return h
    edge_index = jnp.stack([src, dst])
    x = _layernorm(x + _L0_gnn_ref(x, edge_index, L0_gnn_eps, L0_gnn_W1, L0_gnn_b1, L0_gnn_g1, L0_gnn_bt1, L0_gnn_W2, L0_gnn_b2, L0_gnn_g2, L0_gnn_bt2, L0_gnn_W3, L0_gnn_b3), axis=-1)
    x = _layernorm(x + _L1_gnn_ref(x, edge_index, edge_attr_4, L1_gnn_W_edge, L1_gnn_b_edge, L1_gnn_W_ih, L1_gnn_W_hh, L1_gnn_b_ih, L1_gnn_b_hh), axis=-1)
    return x

_drawn_inputs = setup_inputs


def setup_inputs(seed=0):
    import zlib

    import numpy as np

    out = dict(_drawn_inputs(seed))
    spreads = {'L0_gnn_b1': (0.0, 0.1),
     'L0_gnn_g1': (1.0, 0.2),
     'L0_gnn_bt1': (0.0, 0.1),
     'L0_gnn_b2': (0.0, 0.1),
     'L0_gnn_g2': (1.0, 0.2),
     'L0_gnn_bt2': (0.0, 0.1),
     'L0_gnn_b3': (0.0, 0.1)}
    factors = {}
    for name, (base, spread) in spreads.items():
        noise = np.random.default_rng([zlib.crc32(name.encode()), seed]).standard_normal(out[name].shape)
        drawn = base * np.exp(spread * noise) if base else spread * noise
        out[name] = jnp.asarray(drawn.astype(out[name].dtype))
    for name, factor in factors.items():
        out[name] = (out[name] * factor).astype(out[name].dtype)
    return out
```

```python
from contextlib import ExitStack, nullcontext

import concourse.bass as bass
from concourse import mybir

F32 = mybir.dt.float32
F16 = mybir.dt.float16
BF16 = mybir.dt.bfloat16
F8 = mybir.dt.float8e4
I32 = mybir.dt.int32
U32 = mybir.dt.uint32
ALU = mybir.AluOpType
ACT = mybir.ActivationFunctionType
AX = mybir.AxisListType

P = 128
N = 3125
E = 100000
D = 128
H = 32
L = 4
T = 4
STEPS = 4
EPS = 1e-5

NB = (N + P - 1) // P
LAST = N - (NB - 1) * P
UD = 64
NU = (N + UD - 1) // UD
NPAD = NU * UD
NCOL = NB * P
WD = 8
WPU = UD // WD
WC = T * WD
NWG = 4
TPW = 3
EB = 32
BPW = TPW * P // EB
NEB = E // EB
EP = 125
EF = E // EP
BPP = EF // EB
TYW = NB * WD
CH = 512
UPC = CH // UD
NCH = (NPAD + CH - 1) // CH
TAIL = NPAD - (NCH - 1) * CH
SPLIT = 1024.0
assert NEB * EB == E and EP * EF == E and TAIL == UD and NCH * 4 >= NB


def chunk_width(c):
    return CH if not isinstance(c, int) or c < NCH - 1 else TAIL


class Memory:

    def __init__(self, nc, ctx, prefix=""):
        self.nc, self.ctx, self.prefix = nc, ctx, prefix

    def sb(self, name, shape, dt):
        return self.ctx.enter_context(self.nc.sbuf_tensor(self.prefix + name, shape, dt))

    def ps(self, name, shape, dt=F32):
        return self.ctx.enter_context(self.nc.psum_tensor(self.prefix + name, shape, dt))

    def sem(self, name):
        return self.ctx.enter_context(self.nc.semaphore(self.prefix + name))


class Chain:

    def __init__(self, engine, sem):
        self.engine, self.sem, self.n, self.base = engine, sem, 0, 0

    def step(self, instruction):
        self.n += 1
        instruction.then_inc(self.sem, 1)
        self.engine.wait_ge(self.sem, self.base + self.n)
        if not isinstance(self.base, int):
            self.engine.nop(nofuse=True)


def prepare(nc, ins, keep, scratch):
    with ExitStack() as ctx:
        m = Memory(nc, ctx)
        src_i = m.sb("src_i", [EP, EF], I32)
        dst_i = m.sb("dst_i", [EP, EF], I32)
        hi_i = m.sb("hi_i", [EP, EF], I32)
        lo_i = m.sb("lo_i", [EP, EF], I32)
        attr = m.sb("attr", [EP, EF, T], F32)
        dst_f = m.sb("dst_f", [EP, EF], F32)
        top01 = m.sb("top01", [EP, EF], F32)
        top = m.sb("top", [EP, EF], F32)
        not0 = m.sb("not0", [EP, EF], F32)
        not1 = m.sb("not1", [EP, EF], F32)
        not2 = top01
        fields = m.sb("fields", [EP, BPP, 4, EB], F32)
        filler = m.sb("filler", [BPW - 1, 4 * EB], F32)
        iota_i = m.sb("iota_i", [P, T * TYW], I32)
        thr = m.sb("thr", [EP, NWG * P], F16)
        below = m.sb("below", [EP, BPP, NWG * P], BF16)
        ones = m.sb("ones", [EP, 1], BF16)
        start = m.sb("start", [P, NWG], F32)
        step_i = m.sb("step_i", [P, NWG, BPW], I32)
        step_f = m.sb("step_f", [P, NWG, BPW], F32)
        row = m.sb("row", [P, NWG, BPW], U32)
        w8_i = m.sb("w8_i", [P, NWG], I32)
        w8 = m.sb("w8", [P, NWG], F32)
        got = m.sb("got", [P, NWG, BPW, 4 * EB], F32)
        dl = m.sb("dl", [P, NWG, BPW, EB], F32)
        inside = m.sb("inside", [P, NWG, BPW, EB], F32)
        wkey = m.sb("wkey", [P, 3, NWG, BPW, EB], F32)
        w1_raw = m.sb("w1_raw", [L * H, D], F32)
        w2_raw = m.sb("w2_raw", [H, L, H], F32)
        w3_raw = m.sb("w3_raw", [D, L, H], F32)
        we_raw = m.sb("we_raw", [D, T, D], F32)
        wi_raw = m.sb("wi_raw", [D, 3, D], F32)
        wh_raw = m.sb("wh_raw", [D, 3, D], F32)
        count_ps = m.ps("count_ps", [P, NWG])
        turn_ps = m.ps("turn_ps", [P, 2, 512])
        key_ps = m.ps("key_ps", [P, 2, 512])

        edges_in = m.sem("edges_in")
        weights_in = m.sem("weights_in")
        small_in = m.sem("small_in")
        iotas = m.sem("iotas")
        ident_set = m.sem("ident_set")
        dve_chain = m.sem("dve_chain")
        fields_ready = m.sem("fields_ready")
        filler_ready = m.sem("filler_ready")
        fields_out = m.sem("fields_out")
        compared = m.sem("compared")
        counted = m.sem("counted")
        rows_ready = m.sem("rows_ready")
        gathered = m.sem("gathered")
        wkeys_ready = m.sem("wkeys_ready")
        keys_turned = m.sem("keys_turned")
        keys_out = m.sem("keys_out")
        turned = m.sem("turned")
        turned_out = m.sem("turned_out")
        block = ctx.enter_context(nc.Block())

        turns = [(w1_raw[:, :], keep.w1t[:, :])]
        turns += [(w2_raw[:, l, :], keep.w2t[:, l, :]) for l in range(L)]
        turns += [(w3_raw[:, l, :], keep.w3t[:, l, :]) for l in range(L)]
        turns += [(we_raw[:, t, :], keep.wet[:, t, :]) for t in range(T)]
        turns += [(wi_raw[:, g, :], keep.wit[:, g, :]) for g in range(3)]
        turns += [(wh_raw[:, g, :], keep.wht[:, g, :]) for g in range(3)]

        @block.sync
        def _(sp):
            sp.dma_start(dst_i[:, :], ins["dst"].rearrange("(p f) -> p f", p=EP)).then_inc(edges_in, 16)
            sp.dma_start(src_i[:, :], ins["src"].rearrange("(p f) -> p f", p=EP)).then_inc(edges_in, 16)
            sp.dma_start(attr[:, :, :], ins["edge_attr_4"].rearrange("(p f) t -> p f t", p=EP)).then_inc(edges_in, 16)
            sp.wait_ge(fields_ready, 1)
            sp.dma_start(scratch.fields[0:NEB, :].rearrange("(p b) f -> p b f", p=EP),
                         fields[:, :, :, :].rearrange("p b a e -> p b (a e)")).then_inc(fields_out, 16)
            sp.wait_ge(filler_ready, 1)
            sp.dma_start(scratch.fields[NEB:NEB + BPW - 1, :], filler[:, :]).then_inc(fields_out, 16)
            sp.wait_ge(fields_out, 32)

        @block.scalar
        def _(act):
            act.dma_start(w1_raw[:, :], ins["L0_gnn_W1"].rearrange("l h d -> (l h) d")).then_inc(weights_in, 16)
            act.dma_start(w2_raw[:, :, :], ins["L0_gnn_W2"].rearrange("l o i -> o l i")).then_inc(weights_in, 16)
            act.dma_start(w3_raw[:, :, :], ins["L0_gnn_W3"].rearrange("l o i -> o l i")).then_inc(weights_in, 16)
            act.dma_start(we_raw[:, :, :], ins["L1_gnn_W_edge"].rearrange("t o i -> o t i")).then_inc(weights_in, 16)
            act.dma_start(wi_raw[:, :, :], ins["L1_gnn_W_ih"].rearrange("(g o) i -> o g i", g=3)).then_inc(weights_in, 16)
            act.dma_start(wh_raw[:, :, :], ins["L1_gnn_W_hh"].rearrange("(g o) i -> o g i", g=3)).then_inc(weights_in, 16)
            small = [(keep.x_nm[:, 0:NB - 1, :], ins["x"][0:(NB - 1) * P, :].rearrange("(b p) d -> p b d", p=P)),
                     (keep.b_edge[:, :], ins["L1_gnn_b_edge"]),
                     (keep.b_ih[:, :], ins["L1_gnn_b_ih"].rearrange("(g o) -> o g", g=3)),
                     (keep.b_hh[:, :], ins["L1_gnn_b_hh"].rearrange("(g o) -> o g", g=3)),
                     (keep.eps[:, :], ins["L0_gnn_eps"].rearrange("(o l) -> o l", o=1).broadcast_to((P, L)))]
            for kept, name in ((keep.b1, "b1"), (keep.g1, "g1"), (keep.bt1, "bt1"),
                               (keep.b2, "b2"), (keep.g2, "g2"), (keep.bt2, "bt2"), (keep.b3, "b3")):
                small.append((kept[:, :], ins["L0_gnn_" + name].rearrange("l h -> h l")))
            for to, of in small:
                act.dma_start(to, of, allow_slow_non_contiguous=True).then_inc(small_in, 16)
            act.wait_ge(iotas, 1)
            act.dma_start(keep.x_nm[0:LAST, NB - 1, :], ins["x"][(NB - 1) * P:N, :]).then_inc(small_in, 16)
            for i, (raw, kept) in enumerate(turns):
                act.wait_ge(turned, i + 1)
                o, k = kept.shape[0], kept.shape[-1]
                nc.scalar.activation(kept, turn_ps[0:o, i % 2, 0:k], ACT.Copy).then_inc(turned_out, 1)
            for i in range(3 * TPW):
                act.wait_ge(keys_turned, i + 1)
                nc.scalar.activation(keep.key[:, i // TPW, i % TPW, :], key_ps[:, i % 2, :], ACT.Copy).then_inc(keys_out, 1)
            act.wait_ge(small_in, 16 * (len(small) + 1))

        @block.gpsimd
        def _(pool):
            nc.gpsimd.memset(keep.x_nm[:, NB - 1, :], 0.0).then_inc(iotas, 1)
            nc.gpsimd.iota(w8_i[:, :], [[P * WD, NWG]], base=0, channel_multiplier=WD).then_inc(iotas, 1)
            nc.gpsimd.iota(step_i[:, :, :], [[0, NWG], [1, BPW]], base=0, channel_multiplier=0).then_inc(iotas, 1)
            nc.gpsimd.iota(iota_i[:, :], [[1, T * TYW]], base=0, channel_multiplier=0).then_inc(iotas, 1)
            nc.gpsimd.memset(keep.ident[:, :], 0.0).then_inc(ident_set, 1)
            nc.gpsimd.memset(keep.sum3[:, :], 0.0).then_inc(ident_set, 1)
            pool.wait_ge(ident_set, 2)
            nc.gpsimd.affine_select(out=keep.ident[:, :], in_=keep.ident[:, :], compare_op=ALU.not_equal, fill=1.0,
                                    base=0, pattern=[[-1, P]], channel_multiplier=1).then_inc(ident_set, 1)
            for s in range(3):
                pool.wait_ge(ident_set, 3 + s)
                nc.gpsimd.affine_select(out=keep.sum3[:, :], in_=keep.sum3[:, :], compare_op=ALU.not_equal, fill=1.0,
                                        base=-H * s, pattern=[[-1, H]], channel_multiplier=1).then_inc(ident_set, 1)
            pool.wait_ge(rows_ready, 1)
            pool.wait_ge(fields_out, 32)
            for g in range(NWG):
                for k in range(BPW):
                    nc.gpsimd.indirect_dma_start(
                        got[:, g, k, :], None, scratch.fields,
                        bass.IndirectOffsetOnAxis(ap=row[:, g, k:k + 1], axis=0)).then_inc(gathered, 16)

        @block.vector
        def _(dve):
            c = Chain(dve, dve_chain)
            nc.vector.memset(filler[:, :], -1.0).then_inc(filler_ready, 1)
            c.step(nc.vector.memset(ones[:, :], 1.0))
            dve.wait_ge(iotas, 4)
            nc.vector.tensor_scalar(thr[:, :], iota_i[0:EP, 0:NWG * P], float(WD), None, ALU.mult).then_inc(dve_chain, 1)
            nc.vector.tensor_copy(keep.iota[:, :], iota_i[:, :]).then_inc(dve_chain, 1)
            nc.vector.tensor_scalar(keep.iota1[:, :], iota_i[:, 0:P], 1.0, None, ALU.add).then_inc(dve_chain, 1)
            nc.vector.tensor_copy(step_f[:, :, :], step_i[:, :, :]).then_inc(dve_chain, 1)
            nc.vector.tensor_copy(w8[:, :], w8_i[:, :]).then_inc(dve_chain, 1)
            c.n += 5
            dve.wait_ge(edges_in, 48)
            c.step(nc.vector.tensor_copy(dst_f[:, :], dst_i[:, :]))
            for j in range(BPP):
                last = nc.vector.tensor_scalar(below[:, j, :], thr[:, :], dst_f[:, j * EB:j * EB + 1], None, ALU.is_gt)
            last.then_inc(compared, 1)
            nc.vector.tensor_tensor(top01[:, :], attr[:, :, 0], attr[:, :, 1], ALU.max).then_inc(dve_chain, 1)
            nc.vector.tensor_tensor(top[:, :], attr[:, :, 2], attr[:, :, 3], ALU.max).then_inc(dve_chain, 1)
            c.n += 2
            dve.wait_ge(dve_chain, c.n)
            c.step(nc.vector.tensor_tensor(top[:, :], top[:, :], top01[:, :], ALU.max))
            for i, (to) in enumerate((not0, not1, not2)):
                nc.vector.tensor_tensor(to[:, :], attr[:, :, i], top[:, :], ALU.not_equal).then_inc(dve_chain, 1)
            c.n += 3
            dve.wait_ge(dve_chain, c.n)
            c.step(nc.vector.scalar_tensor_tensor(out=not1[:, :], in0=not2[:, :], scalar=1.0, in1=not1[:, :], op0=ALU.add, op1=ALU.mult))
            c.step(nc.vector.scalar_tensor_tensor(out=not0[:, :], in0=not1[:, :], scalar=1.0, in1=not0[:, :], op0=ALU.add, op1=ALU.mult))
            nc.vector.tensor_scalar(hi_i[:, :], src_i[:, :], 7, None, ALU.arith_shift_right).then_inc(dve_chain, 1)
            nc.vector.tensor_scalar(lo_i[:, :], src_i[:, :], P - 1, None, ALU.bitwise_and).then_inc(dve_chain, 1)
            c.n += 2
            dve.wait_ge(dve_chain, c.n)

            def field(a):
                return fields[:, :, a, :]

            def blocks(a):
                return a[:, :].rearrange("p (b e) -> p b e", e=EB)

            nc.vector.tensor_copy(field(0), blocks(dst_f))
            nc.vector.tensor_scalar(field(1), blocks(hi_i), float(WD), None, ALU.mult)
            nc.vector.tensor_scalar(field(2), blocks(not0), float(TYW), None, ALU.mult)
            nc.vector.tensor_copy(field(3), blocks(lo_i)).then_inc(fields_ready, 1)
            dve.wait_ge(counted, 1)
            c.step(nc.vector.tensor_scalar(start[:, :], count_ps[:, :], -1.0, 0.0, ALU.add, ALU.max))
            for g in range(NWG):
                last = nc.vector.tensor_scalar(row[:, g, :], step_f[:, g, :], start[:, g:g + 1], None, ALU.add)
            last.then_inc(rows_ready, 1)
            dve.wait_ge(gathered, 16 * NWG * BPW)
            v = got[:, :, :, :].rearrange("p g b (a e) -> p g b a e", a=4)
            for g in range(NWG):
                nc.vector.tensor_scalar(dl[:, g, :, :], v[:, g, :, 0, :], w8[:, g:g + 1], None, ALU.subtract).then_inc(dve_chain, 1)
            c.n += NWG
            dve.wait_ge(dve_chain, c.n)

            def flat(a):
                return a.rearrange("p g b e -> p (g b) e")

            vf = got[:, :, :, :].rearrange("p g b (a e) -> p (g b) a e", a=4)
            dlf, inf = flat(dl[:, :, :, :]), flat(inside[:, :, :, :])
            c.step(nc.vector.tensor_scalar(inf, dlf, 0.0, None, ALU.is_ge))
            c.step(nc.vector.scalar_tensor_tensor(out=inf, in0=dlf, scalar=float(WD), in1=inf, op0=ALU.is_lt, op1=ALU.mult))
            c.step(nc.vector.tensor_tensor(flat(wkey[:, 2, :, :, :]), vf[:, :, 1, :], dlf, ALU.add))
            c.step(nc.vector.tensor_tensor(flat(wkey[:, 1, :, :, :]), flat(wkey[:, 2, :, :, :]), vf[:, :, 2, :], ALU.add))
            nc.vector.scalar_tensor_tensor(out=flat(wkey[:, 0, :, :, :]), in0=vf[:, :, 3, :], scalar=1.0, in1=inf,
                                           op0=ALU.add, op1=ALU.mult).then_inc(wkeys_ready, 1)
            c.step(nc.vector.tensor_scalar(dlf, dlf, 1.0, None, ALU.add))
            kt = keep.dkey[:, :, :].rearrange("p g (b e) -> p (g b) e", e=EB)
            c.step(nc.vector.scalar_tensor_tensor(out=kt, in0=vf[:, :, 2, :], scalar=float(WD) / TYW, in1=dlf,
                                                  op0=ALU.mult, op1=ALU.add))
            c.step(nc.vector.tensor_tensor(kt, kt, inf, ALU.mult))

        @block.tensor
        def _(pe):
            pe.wait_ge(ident_set, 3)
            pe.wait_ge(weights_in, 96)
            for i, (raw, kept) in enumerate(turns):
                if i >= 2:
                    pe.wait_ge(turned_out, i - 1)
                k, o = raw.shape[0], raw.shape[-1]
                nc.tensor.transpose(turn_ps[0:o, i % 2, 0:k], raw, keep.ident[0:k, 0:k]).then_inc(turned, 1)
            pe.wait_ge(compared, 1)
            for g in range(NWG):
                for j in range(BPP):
                    last = nc.tensor.matmul(count_ps[:, g:g + 1], below[:, j, g * P:(g + 1) * P], ones[:, :],
                                            start=(j == 0), stop=(j == BPP - 1))
            last.then_inc(counted, 1)
            pe.wait_ge(wkeys_ready, 1)
            for i in range(3 * TPW):
                a, j = i // TPW, i % TPW
                if i >= 2:
                    pe.wait_ge(keys_out, i - 1)
                for g in range(NWG):
                    seen = wkey[:, a, g, :, :].rearrange("p b e -> p (b e)")[:, j * P:(j + 1) * P]
                    last = nc.tensor.transpose(key_ps[:, i % 2, g * P:(g + 1) * P], seen, keep.ident[:, :])
                last.then_inc(keys_turned, 1)


def build(nc, keep, scratch):
    R = 6
    with ExitStack() as ctx:
        m = Memory(nc, ctx)
        which = m.sb("which", [P, R, P], BF16)
        where = m.sb("where", [P, R, T * TYW], BF16)
        anyt = m.sb("anyt", [P, R, TYW], BF16)
        unit = m.sb("unit", [P, 2, T, NB, UD], F8)
        unit_all = m.sb("unit_all", [P, 2, NB, UD], F8)
        by_type = m.ps("by_type", [P, 2, 2, 512])
        all_types = m.ps("all_types", [P, 2, 512])

        hot = m.sem("hot")
        hot_free = m.sem("hot_free")
        window_free = m.sem("window_free")
        unit_out = [m.sem("unit_out0"), m.sem("unit_out1")]
        block = ctx.enter_context(nc.Block())
        V = WPU * TPW

        @block.vector
        def _(dve):
            def fill(u, parity):
                for i in range(WPU):
                    for j in range(TPW):
                        v = i * TPW + j
                        r = (parity * V + v) % R
                        dve.wait_ge(hot_free, (u * V + v) + 1)
                        w = u * WPU + i
                        nc.vector.tensor_scalar(which[:, r, :], keep.iota1[:, :], keep.key[:, 0, j, bass.ds(w, 1)], None, ALU.is_equal)
                        nc.vector.tensor_scalar(where[:, r, :], keep.iota[:, :], keep.key[:, 1, j, bass.ds(w, 1)], None, ALU.is_equal)
                        nc.vector.tensor_scalar(anyt[:, r, :], keep.iota[:, 0:TYW], keep.key[:, 2, j, bass.ds(w, 1)], None,
                                                ALU.is_equal).then_inc(hot, 1)

            with dve.Fori(0, NU - 1, 2) as u:
                fill(u, 0)
                fill(u + 1, 1)
            fill(NU - 1, 0)

        @block.tensor
        def _(pe):
            pe.sem_inc(hot_free, R)

            def count(u, parity):
                for i in range(WPU):
                    pe.wait_ge(window_free, (u * WPU + i) + 1)
                    for j in range(TPW):
                        v = i * TPW + j
                        r = (parity * V + v) % R
                        pe.wait_ge(hot, (u * V + v) + 1)
                        first, last = j == 0, j == TPW - 1
                        for h in range(2):
                            nc.tensor.matmul(by_type[:, i % 2, h, 0:2 * TYW], which[:, r, :],
                                             where[:, r, h * 2 * TYW:(h + 1) * 2 * TYW], start=first, stop=last)
                        nc.tensor.matmul(all_types[:, i % 2, 0:TYW], which[:, r, :], anyt[:, r, :],
                                         start=first, stop=last).then_inc(hot_free, 1)

            with pe.Fori(0, NU - 1, 2) as u:
                count(u, 0)
                count(u + 1, 1)
            count(NU - 1, 0)

        @block.scalar
        def _(act):
            act.sem_inc(window_free, 2)

            def leave(u, parity, before):
                act.wait_ge(unit_out[parity], before)
                act.nop(nofuse=True)
                for i in range(WPU):
                    act.wait_ge(hot_free, (u * WPU + i) * TPW + TPW + R)
                    act.nop(nofuse=True)
                    for h in range(2):
                        to = unit[:, parity, 2 * h:2 * h + 2, :, i * WD:(i + 1) * WD].rearrange("p t b d -> p (t b) d")
                        nc.scalar.activation(to, by_type[:, i % 2, h, 0:2 * TYW].rearrange("p (a d) -> p a d", d=WD), ACT.Copy, saturate=False)
                    to = unit_all[:, parity, :, i * WD:(i + 1) * WD]
                    nc.scalar.activation(to, all_types[:, i % 2, 0:TYW].rearrange("p (b d) -> p b d", d=WD), ACT.Copy,
                                         saturate=False).then_inc(window_free, 1)

            act.sem_inc(unit_out[0], 32)
            act.sem_inc(unit_out[1], 32)
            with act.Fori(0, NU - 1, 2) as u:
                leave(u, 0, u * 16 + 32)
                leave(u + 1, 1, u * 16 + 32)
            leave(NU - 1, 0, (NU - 1) * 16 + 32)

        @block.sync
        def _(sp):
            def store(u, parity):
                sp.wait_ge(window_free, u * WPU + WPU + 2)
                sp.nop(nofuse=True)
                sp.dma_start(scratch.adj[bass.ds(u, 1), :, :].rearrange("u p f -> p (u f)"),
                             unit[:, parity, :, :, :].rearrange("p t b d -> p (t b d)").bitcast(F32)).then_inc(unit_out[parity], 16)
                sp.dma_start(keep.adj_words[:, bass.ds(u, 1), :].rearrange("p u f -> p (u f)"),
                             unit_all[:, parity, :, :].rearrange("p b d -> p (b d)").bitcast(F32)).then_inc(unit_out[parity], 16)

            with sp.Fori(0, NU - 1, 2) as u:
                store(u, 0)
                store(u + 1, 1)
            store(NU - 1, 0)
            sp.wait_ge(unit_out[0], 32 * ((NU + 1) // 2 + 1))
            sp.wait_ge(unit_out[1], 32 * ((NU - 1) // 2 + 1))


def node_groups():
    return [(q, 4 * q, min(4, NB - 4 * q)) for q in range((NB + 3) // 4)]


def first_network(nc, keep, layer=None):
    fast = layer is None
    with ExitStack() as ctx:
        m = Memory(nc, ctx, "" if fast else "layer_")
        parts = m.sb("parts", [P, NB, 3, H], BF16)
        rest = m.sb("rest", [P, 16 * H], F32)
        summed = m.sb("summed", [3 * H, 2, CH], F32)
        h1 = m.sb("h1", [H, NPAD], F32)
        h2 = m.sb("h2", [H, NPAD], F32)
        w1c = m.sb("w1c", [D, H], F32)
        w1e = m.sb("w1e", [D, H], F32)
        w2c = m.sb("w2c", [H, H], F32)
        w3c = m.sb("w3c", [H, D], F32)
        vec = m.sb("vec", [H, 6], F32)
        b3c = m.sb("b3c", [D, 1], F32)
        gain = m.sb("gain", [P, 1], F32)
        stats = m.sb("stats", [H, NCH, 6], F32)
        mv = m.sb("mv", [H, 2], F32)
        dev = m.sb("dev", [H, 2, 1], F32)
        root = m.sb("root", [H, 1], F32)
        scale = m.sb("scale", [H, 2, 1], F32)
        shift = m.sb("shift", [H, 2, 1], F32)
        junk = m.sb("junk", [P, 5, TPW * P], F32)
        big = m.ps("big", [P, 2, 512])
        small = m.ps("small", [P, 2, 512])
        yps = m.ps("yps", [P, 2, 512])

        x_turned = m.sem("x_turned")
        x_left = m.sem("x_left")
        cur_ready = m.sem("cur_ready")
        xt_ready = m.sem("xt_ready")
        y_done = m.sem("y_done")
        parts_ready = m.sem("parts_ready")
        dense_done = m.sem("dense_done")
        sum_left = m.sem("sum_left")
        h1_done = m.sem("h1_done")
        h1_left = m.sem("h1_left")
        var_ready = m.sem("var_ready")
        root_ready = m.sem("root_ready")
        norm_ready = m.sem("norm_ready")
        relu1 = m.sem("relu1")
        h2_done = m.sem("h2_done")
        h2_left = m.sem("h2_left")
        relu2 = m.sem("relu2")
        x_done = m.sem("x_done")
        chain = m.sem("chain")
        block = ctx.enter_context(nc.Block())

        spans = [(c, c * CH, chunk_width(c)) for c in range(NCH)]

        def layers(engine):
            return engine.Fori(0, L, 1) if fast else nullcontext(0)

        yb = [(0, 16), (16, NB - 16)]

        @block.tensor
        def _(pe):
            for q, b0, n in node_groups() if fast else ():
                if q >= 2:
                    pe.wait_ge(x_left, q - 1)
                for i in range(n):
                    last = nc.tensor.transpose(big[:, q % 2, i * P:(i + 1) * P], keep.x_nm[:, b0 + i, :], keep.ident[:, :])
                last.then_inc(x_turned, 1)
            with layers(pe) as l:
                pe.wait_ge(cur_ready, l + 1)
                pe.wait_ge(xt_ready, l * NCH + NCH)
                for q, (b0, n) in enumerate(yb if fast else ()):
                    for b in range(b0, b0 + n):
                        last = nc.tensor.matmul(yps[:, q, (b - b0) * H:(b - b0 + 1) * H], keep.xt[:, b * P:(b + 1) * P], w1c[:, :],
                                                start=True, stop=True)
                    last.then_inc(y_done, 1)

                def perceptron_in(c, at, w):
                    if fast:
                        pe.wait_ge(sum_left, l * NCH + (c + 1))
                    if c >= 2:
                        pe.wait_ge(h1_left, l * NCH + (c - 1))
                    if fast:
                        nc.tensor.matmul(small[0:H, c % 2, 0:w], keep.sum3[:, :], summed[:, c % 2, 0:w], start=True, stop=False)
                    else:
                        nc.tensor.matmul(small[0:H, c % 2, 0:w], w1c[:, :], keep.st[:, at:at + w], start=True, stop=False)
                    nc.tensor.matmul(small[0:H, c % 2, 0:w], w1e[:, :], keep.xt[:, at:at + w], start=False, stop=True).then_inc(h1_done, 1)

                if fast:
                    pe.wait_ge(parts_ready, l * 2 + 2)
                for c, at, w in spans if fast else ():
                    if c >= 2:
                        pe.wait_ge(sum_left, l * NCH + (c - 1))
                    pe.nop(nofuse=True)
                    for b in range(NB):
                        last = nc.tensor.matmul(big[0:3 * H, c % 2, 0:w], parts[:, b, :, :].rearrange("p s h -> p (s h)"),
                                                keep.adj[:, c * UPC:c * UPC + w // UD, b, :], start=(b == 0), stop=(b == NB - 1))
                    last.then_inc(dense_done, 1)
                    if c >= 1:
                        perceptron_in(*spans[c - 1])
                for span in spans[NCH - 1:] if fast else spans:
                    perceptron_in(*span)
                for c, at, w in spans:
                    pe.wait_ge(relu1, l * NCH + (c + 1))
                    if c >= 2:
                        pe.wait_ge(h2_left, l * NCH + (c - 1))
                    pe.nop(nofuse=True)
                    nc.tensor.matmul(small[0:H, c % 2, 0:w], w2c[:, :], h1[:, at:at + w], start=True, stop=True).then_inc(h2_done, 1)
                for c, at, w in spans:
                    pe.wait_ge(relu2, l * NCH + (c + 1))
                    if c >= 2:
                        pe.wait_ge(xt_ready, l * NCH + (NCH + c - 1))
                    nc.tensor.matmul(big[:, c % 2, 0:w], w3c[:, :], h2[:, at:at + w], start=True, stop=True).then_inc(x_done, 1)

        @block.scalar
        def _(act):
            for q, b0, n in node_groups() if fast else ():
                act.wait_ge(x_turned, q + 1)
                nc.scalar.activation(keep.xt[:, b0 * P:(b0 + n) * P], big[:, q % 2, 0:n * P], ACT.Copy).then_inc(x_left, 1)
            if fast:
                act.wait_ge(x_left, len(node_groups()))
            act.sem_inc(xt_ready, NCH)
            with layers(act) as l:
                def left1(c, at, w):
                    act.wait_ge(h1_done, l * NCH + (c + 1))
                    nc.scalar.activation(h1[:, at:at + w], small[0:H, c % 2, 0:w], ACT.Identity, bias=vec[:, 0:1]).then_inc(h1_left, 1)

                for c, at, w in spans if fast else ():
                    act.wait_ge(dense_done, l * NCH + (c + 1))
                    if c >= 2:
                        act.wait_ge(h1_done, l * NCH + (c - 1))
                    nc.scalar.activation(summed[:, c % 2, 0:w], big[0:3 * H, c % 2, 0:w], ACT.Copy).then_inc(sum_left, 1)
                    if c >= 1:
                        left1(*spans[c - 1])
                for span in spans[NCH - 1:] if fast else spans:
                    left1(*span)
                act.wait_ge(var_ready, l * 2 + 1)
                nc.scalar.activation(root[:, :], dev[:, 0, :], ACT.Sqrt).then_inc(root_ready, 1)
                act.wait_ge(norm_ready, l * 2 + 1)

                def left2(c, at, w):
                    act.wait_ge(h2_done, l * NCH + (c + 1))
                    nc.scalar.activation(h2[:, at:at + w], small[0:H, c % 2, 0:w], ACT.Identity, bias=vec[:, 3:4]).then_inc(h2_left, 1)

                for c, at, w in spans:
                    nc.scalar.activation(h1[:, at:at + w], h1[:, at:at + w], ACT.Relu, bias=shift[:, 0, :], scale=scale[:, 0, :]).then_inc(relu1, 1)
                    if c >= 1:
                        left2(*spans[c - 1])
                left2(*spans[NCH - 1])
                act.wait_ge(var_ready, l * 2 + 2)
                nc.scalar.activation(root[:, :], dev[:, 1, :], ACT.Sqrt).then_inc(root_ready, 1)
                act.wait_ge(norm_ready, l * 2 + 2)
                for c, at, w in spans:
                    nc.scalar.activation(h2[:, at:at + w], h2[:, at:at + w], ACT.Relu, bias=shift[:, 1, :], scale=scale[:, 1, :]).then_inc(relu2, 1)

        @block.vector
        def _(dve):
            ch = Chain(dve, chain)
            with layers(dve) as l:
                own = l if fast else layer
                ch.base, ch.n = l * LAYER_STEPS, 0
                dve.wait_ge(xt_ready, l * NCH + NCH)
                dve.nop(nofuse=True)
                nc.vector.tensor_copy(w1c[:, :], keep.w1t[:, bass.ds(own * H, H)]).then_inc(chain, 1)
                nc.vector.tensor_scalar(gain[:, :], keep.eps[:, bass.ds(own, 1)], 1.0, None, ALU.add).then_inc(chain, 1)
                for i, a in enumerate((keep.b1, keep.g1, keep.bt1, keep.b2, keep.g2, keep.bt2)):
                    nc.vector.tensor_copy(vec[:, i:i + 1], a[:, bass.ds(own, 1)])
                nc.vector.tensor_copy(b3c[:, :], keep.b3[:, bass.ds(own, 1)])
                nc.vector.tensor_copy(w2c[:, :], keep.w2t[:, bass.ds(own, 1), :].rearrange("p l o -> p (l o)"))
                nc.vector.tensor_copy(w3c[:, :], keep.w3t[:, bass.ds(own, 1), :].rearrange("p l o -> p (l o)")).then_inc(chain, 1)
                ch.n += 3
                dve.wait_ge(chain, ch.base + ch.n)
                nc.vector.tensor_scalar(w1e[:, :], w1c[:, :], gain[:, 0:1], None, ALU.mult).then_inc(cur_ready, 1)
                for q, (b0, n) in enumerate(yb if fast else ()):
                    dve.wait_ge(y_done, l * 2 + (q + 1))
                    y = yps[:, q, 0:n * H].rearrange("p (b h) -> p b h", h=H)
                    r = rest[:, 0:n * H].rearrange("p (b h) -> p b h", h=H)
                    part = [parts[:, b0:b0 + n, s, :] for s in range(3)]
                    ch.step(nc.vector.tensor_copy(part[0], y))
                    ch.step(nc.vector.tensor_tensor(r, y, part[0], ALU.subtract))
                    ch.step(nc.vector.tensor_copy(part[1], r))
                    ch.step(nc.vector.tensor_tensor(r, r, part[1], ALU.subtract))
                    nc.vector.tensor_copy(part[2], r).then_inc(parts_ready, 1)

                def statistics(h, c, at, w):
                    w = min(w, N - at)
                    return nc.vector.bn_stats(stats[:, c, :], h[:, at:at + w])

                def norm(i):
                    ch.step(nc.vector.bn_aggr(mv[:, :], stats[:, :, :].rearrange("p c s -> p (c s)")))
                    nc.vector.tensor_scalar(dev[:, i, :], mv[:, 1:2], EPS, None, ALU.add).then_inc(var_ready, 1)
                    dve.wait_ge(root_ready, l * 2 + (i + 1))
                    ch.step(nc.vector.reciprocal(root[:, :], root[:, :]))
                    ch.step(nc.vector.tensor_tensor(scale[:, i, :], root[:, :], vec[:, 3 * i + 1:3 * i + 2], ALU.mult))
                    ch.step(nc.vector.tensor_tensor(mv[:, 0:1], mv[:, 0:1], scale[:, i, :], ALU.mult))
                    nc.vector.tensor_tensor(shift[:, i, :], vec[:, 3 * i + 2:3 * i + 3], mv[:, 0:1], ALU.subtract).then_inc(norm_ready, 1)

                for c, at, w in spans:
                    for x in range(c * WC // NCH, (c + 1) * WC // NCH) if fast else ():
                        nc.vector.tensor_scalar(junk[:, x - c * WC // NCH, :], keep.dkey[:, bass.ds(l, 1), :].rearrange("p g e -> p (g e)"), float(x + 1), None,
                                                ALU.is_equal, ALU.add, accum_out=keep.deg[:, bass.ds(l * WC + x, 1)])
                    if fast:
                        ch.step(nc.vector.tensor_reduce(keep.largest[:, bass.ds(l * NCH + c, 1)],
                                                        keep.adj_bytes[:, bass.ds((l * NCH + c) * SLICE, SLICE)], AX.X, ALU.max))
                    dve.wait_ge(h1_left, l * NCH + (c + 1))
                    last = statistics(h1, c, at, w)
                ch.step(last)
                norm(0)
                for c, at, w in spans:
                    dve.wait_ge(h2_left, l * NCH + (c + 1))
                    last = statistics(h2, c, at, w)
                ch.step(last)
                norm(1)
                for c, at, w in spans:
                    dve.wait_ge(x_done, l * NCH + (c + 1))
                    nc.vector.tensor_scalar(keep.xt[:, at:at + w], big[:, c % 2, 0:w], b3c[:, 0:1], None, ALU.add).then_inc(xt_ready, 1)
                assert ch.n == LAYER_STEPS or not fast, ch.n


LAYER_STEPS = 3 + 8 + NCH + 2 * 5
SLICE = NU * NB * UD // (L * NCH)
assert SLICE * L * NCH == NU * NB * UD


def normalise(nc, keep, out, name):
    with ExitStack() as ctx:
        m = Memory(nc, ctx, name)
        stats = m.sb("n_stats", [P, NB, 6], F32)
        mv = m.sb("n_mv", [P, NB, 2], F32)
        root = m.sb("n_root", [P, NB], F32)
        ps = m.ps("n_ps", [P, 2, 512])
        ps2 = m.ps("n_ps2", [P, 2, 512])
        degs = m.ps("n_degs", [T, 2, 512])
        turned = m.sem("n_turned")
        added = m.sem("n_added")
        eps_added = m.sem("n_eps_added")
        rooted = m.sem("n_rooted")
        normed = m.sem("n_normed")
        back = m.sem("n_back")
        back_left = m.sem("n_back_left")
        hi_ready = m.sem("n_hi_ready")
        stored = m.sem("n_stored")
        deg_turned = m.sem("n_deg_turned")
        deg_left = m.sem("n_deg_left")
        chain = m.sem("n_chain")
        block = ctx.enter_context(nc.Block())
        groups = node_groups()

        @block.tensor
        def _(pe):
            for q, b0, n in groups:
                if q >= 2:
                    pe.wait_ge(added, q - 1)
                for i in range(n):
                    last = nc.tensor.transpose(ps[:, q % 2, i * P:(i + 1) * P], keep.xt[:, (b0 + i) * P:(b0 + i + 1) * P], keep.ident[:, :])
                last.then_inc(turned, 1)
            if out is None:
                for d in range(WD):
                    if d >= 2:
                        pe.wait_ge(deg_left, d - 1)
                    for g in range(NWG):
                        seen = keep.deg[:, g * WC:(g + 1) * WC].rearrange("p (t d) -> p t d", d=WD)[:, :, d]
                        last = nc.tensor.transpose(degs[:, d % 2, g * P:(g + 1) * P], seen, keep.ident[:, :])
                    last.then_inc(deg_turned, 1)
                for q, b0, n in groups:
                    pe.wait_ge(normed, q + 1)
                    if q >= 2:
                        pe.wait_ge(back_left, q - 1)
                    for i in range(n):
                        last = nc.tensor.transpose(ps2[:, q % 2, i * P:(i + 1) * P], keep.x_nm[:, b0 + i, :], keep.ident[:, :])
                    last.then_inc(back, 1)

        @block.vector
        def _(dve):
            ch = Chain(dve, chain)
            for q, b0, n in groups:
                dve.wait_ge(turned, q + 1)
                x = keep.x_nm[:, b0:b0 + n, :].rearrange("p b d -> p (b d)")
                nc.vector.tensor_tensor(x, ps[:, q % 2, 0:n * P], x, ALU.add).then_inc(added, 1)
                dve.wait_ge(added, q + 1)
                for b in range(b0, b0 + n):
                    last = nc.vector.bn_stats(stats[:, b, :], keep.x_nm[:, b, :])
                ch.step(last)
                for b in range(b0, b0 + n):
                    last = nc.vector.bn_aggr(mv[:, b, :], stats[:, b, :])
            ch.step(last)
            nc.vector.tensor_scalar(root[:, :], mv[:, :, 1], EPS, None, ALU.add).then_inc(eps_added, 1)
            dve.wait_ge(rooted, 1)
            ch.step(nc.vector.reciprocal(root[:, :], root[:, :]))
            for q, b0, n in groups:
                for b in range(b0, b0 + n):
                    last = nc.vector.tensor_scalar(keep.x_nm[:, b, :], keep.x_nm[:, b, :], mv[:, b, 0:1], root[:, b:b + 1],
                                                   ALU.subtract, ALU.mult)
                last.then_inc(normed, 1)
            if out is None:
                for d in range(WD):
                    dve.wait_ge(deg_turned, d + 1)
                    row = keep.deg_row[:, :].rearrange("t (w d) -> t w d", d=WD)[:, :, d]
                    nc.vector.tensor_copy(row, degs[:, d % 2, :]).then_inc(deg_left, 1)
                for q, b0, n in groups:
                    dve.wait_ge(hi_ready, q + 1)
                    nc.vector.scalar_tensor_tensor(out=keep.halves[:, 0, b0:b0 + n, 1, :], in0=keep.x_nm[:, b0:b0 + n, :], scalar=SPLIT,
                                                   in1=keep.halves[:, 0, b0:b0 + n, 0, :], op0=ALU.mult, op1=ALU.subtract)

        @block.scalar
        def _(act):
            act.wait_ge(eps_added, 1)
            nc.scalar.activation(root[:, :], root[:, :], ACT.Sqrt).then_inc(rooted, 1)
            if out is None:
                for q, b0, n in groups:
                    act.wait_ge(normed, q + 1)
                    nc.scalar.activation(keep.halves[:, 0, b0:b0 + n, 0, :], keep.x_nm[:, b0:b0 + n, :], ACT.Copy, scale=SPLIT).then_inc(hi_ready, 1)
                for q, b0, n in groups:
                    act.wait_ge(back, q + 1)
                    nc.scalar.activation(keep.xt[:, b0 * P:(b0 + n) * P], ps2[:, q % 2, 0:n * P], ACT.Copy).then_inc(back_left, 1)

        @block.sync
        def _(sp):
            if out is not None:
                sp.wait_ge(normed, len(groups))
                sp.dma_start(out[0:(NB - 1) * P, :].rearrange("(b p) d -> p b d", p=P), keep.x_nm[:, 0:NB - 1, :]).then_inc(stored, 16)
                sp.dma_start(out[(NB - 1) * P:N, :], keep.x_nm[0:LAST, NB - 1, :]).then_inc(stored, 16)
                sp.wait_ge(stored, 32)


def second_network(nc, keep, scratch):
    with ExitStack() as ctx:
        m = Memory(nc, ctx)
        ring = m.sb("ring", [P, T, UPC, NB * UD // 4], F32)
        ring8 = ring[:, :, :, :].rearrange("p t u f -> p (t u f)").bitcast(F8).rearrange(
            "p (t u b d) -> p t u b d", t=T, u=UPC, b=NB)
        near = m.sb("near", [D, T, CH], F32)
        a_sb = m.sb("a_sb", [D, CH], F32)
        r_sb = m.sb("r_sb", [D, CH], F32)
        z_sb = m.sb("z_sb", [D, CH], F32)
        n_sb = m.sb("n_sb", [D, CH], F32)
        u_sb = m.sb("u_sb", [D, CH], F32)
        h_new = m.sb("h_new", [D, CH], F32)
        b_rz = m.sb("b_rz", [D, 2], F32)
        near_ps = m.ps("near_ps", [D, 2, CH])
        a_ps = m.ps("a_ps", [D, CH])
        rz_ps = m.ps("rz_ps", [D, 2, CH])
        in_ps = m.ps("in_ps", [D, CH])
        hn_ps = m.ps("hn_ps", [D, CH])
        t_ps = m.ps("t_ps", [P, CH])

        tile_in = [m.sem(f"tile_in{t}") for t in range(T)]
        tile_done = m.sem("tile_done")
        near_left = m.sem("near_left")
        a_done = m.sem("a_done")
        a_left = m.sem("a_left")
        gates_done = m.sem("gates_done")
        rz_done = m.sem("rz_done")
        cand_done = m.sem("cand_done")
        n_done = m.sem("n_done")
        h_done = m.sem("h_done")
        t_done = m.sem("t_done")
        hi_done = m.sem("hi_done")
        lo_done = m.sem("lo_done")
        chain = m.sem("l1_chain")
        bias_ready = m.sem("bias_ready")
        block = ctx.enter_context(nc.Block())

        def steps(eng, chunk):
            with eng.Fori(0, STEPS, 2) as s0:
                for parity in range(2):
                    s = s0 + parity
                    chunk(s, 0, parity)
                    with eng.Fori(1, NCH - 1, 1) as c:
                        chunk(s, c, parity)
                    chunk(s, NCH - 1, parity)

        def cols(c, w):
            return slice(c * CH, c * CH + w) if isinstance(c, int) else bass.ds(c * CH, w)

        def is_first(c):
            return isinstance(c, int) and c == 0

        def is_last(c):
            return isinstance(c, int) and c == NCH - 1

        @block.sync
        def _(sp):
            def chunk(s, c, parity):
                k = s * NCH + c
                for t in range(T):
                    sp.wait_ge(tile_done, k * T + (t + 1))
                    sp.nop(nofuse=True)
                    u0, nu = (c * UPC, chunk_width(c) // UD)
                    of = scratch.adj[u0:u0 + nu, :, :] if isinstance(c, int) else scratch.adj[bass.ds(u0, nu), :, :]
                    sp.dma_start(ring[:, t, 0:nu, :], of[:, :, t * NB * UD // 4:(t + 1) * NB * UD // 4].rearrange("u p f -> p u f")
                                 ).then_inc(tile_in[t], 16)

            steps(sp, chunk)

        @block.tensor
        def _(pe):
            pe.sem_inc(tile_done, T)
            pe.sem_inc(a_done, 1)
            pe.sem_inc(gates_done, 1)
            pe.sem_inc(t_done, 1)
            pe.wait_ge(bias_ready, 1)

            def messages(k, c, w):
                pe.wait_ge(near_left, k * T + (T + 2))
                pe.wait_ge(a_left, k + 1)
                for t in range(T):
                    nc.tensor.matmul(a_ps[:, 0:w], keep.wet[:, t, :], near[:, t, 0:w], start=(t == 0), stop=False)
                nc.tensor.matmul(a_ps[:, 0:w], keep.b_edge[:, :], keep.deg_row[:, cols(c, w)], start=False, stop=True).then_inc(a_done, 1)

            def gates(k, c, w):
                pe.wait_ge(a_left, k + 2)
                pe.wait_ge(n_done, k + 1)
                h = keep.xt[:, cols(c, w)]
                for g in range(2):
                    nc.tensor.matmul(rz_ps[:, g, 0:w], keep.wht[:, g, :], h, start=True, stop=False)
                    nc.tensor.matmul(rz_ps[:, g, 0:w], keep.wit[:, g, :], a_sb[:, 0:w], start=False, stop=True)
                nc.tensor.matmul(hn_ps[:, 0:w], keep.wht[:, 2, :], h, start=True, stop=True)
                nc.tensor.matmul(in_ps[:, 0:w], keep.wit[:, 2, :], a_sb[:, 0:w], start=True, stop=True).then_inc(gates_done, 1)

            def turn(k, c, w):
                pe.wait_ge(h_done, k + 2)
                pe.wait_ge(hi_done, k + NCH)
                pe.wait_ge(lo_done, k + NCH)
                for i in range((w + P - 1) // P):
                    last = nc.tensor.transpose(t_ps[:, i * P:(i + 1) * P], h_new[:, i * P:(i + 1) * P], keep.ident[:, :])
                last.then_inc(t_done, 1)

            def chunk(s, c, parity):
                k = s * NCH + c
                w = chunk_width(c)
                for t in range(T):
                    pe.wait_ge(tile_in[t], k * 16 + 16)
                    pe.wait_ge(near_left, k * T + (t + 1))
                    pe.nop(nofuse=True)
                    for b in range(NB):
                        if is_first(c) and t == 0 and b % 4 == 0:
                            pe.wait_ge(hi_done, s * NCH + (b // 4 + 1))
                            pe.wait_ge(lo_done, s * NCH + (b // 4 + 1))
                            pe.nop(nofuse=True)
                        for half in range(2):
                            last = nc.tensor.matmul(near_ps[:, t % 2, 0:w], keep.halves[:, parity, b, half, :],
                                                    ring8[:, t, 0:w // UD, b, :], start=(b == 0 and half == 0),
                                                    stop=(b == NB - 1 and half == 1))
                    last.then_inc(tile_done, 1)
                    if not is_first(c) and t < 3:
                        (messages, gates, turn)[t](k - 1, c - 1, CH)
                if is_last(c):
                    messages(k, c, w)
                    gates(k, c, w)
                    turn(k, c, w)

            steps(pe, chunk)

        @block.scalar
        def _(act):
            act.sem_inc(near_left, 2)
            act.sem_inc(a_left, 1)
            act.sem_inc(n_done, 1)
            act.sem_inc(hi_done, NCH)
            act.wait_ge(bias_ready, 1)

            def sums(k, t, w):
                act.wait_ge(tile_done, k * T + (T + t + 1))
                act.wait_ge(a_done, k + 1)
                nc.scalar.activation(near[:, t, 0:w], near_ps[:, t % 2, 0:w], ACT.Copy, scale=1.0 / SPLIT).then_inc(near_left, 1)

            def messages(k, w):
                act.wait_ge(a_done, k + 2)
                act.wait_ge(gates_done, k + 1)
                nc.scalar.activation(a_sb[:, 0:w], a_ps[:, 0:w], ACT.Copy).then_inc(a_left, 1)

            def gates(k, w):
                act.wait_ge(gates_done, k + 2)
                act.wait_ge(h_done, k + 1)
                nc.scalar.activation(r_sb[:, 0:w], rz_ps[:, 0, 0:w], ACT.Sigmoid, bias=b_rz[:, 0:1]).then_inc(rz_done, 1)
                nc.scalar.activation(z_sb[:, 0:w], rz_ps[:, 1, 0:w], ACT.Sigmoid, bias=b_rz[:, 1:2])
                act.wait_ge(cand_done, k + 1)
                nc.scalar.activation(n_sb[:, 0:w], n_sb[:, 0:w], ACT.Tanh, bias=keep.b_ih[:, 2:3]).then_inc(n_done, 1)

            def turn(k, c, w, parity):
                nb = (w + P - 1) // P
                act.wait_ge(t_done, k + 2)
                at = keep.halves[:, 1 - parity, bass.ds(c * 4, nb), 0, :] if not isinstance(c, int) else keep.halves[:, 1 - parity, 4 * c:4 * c + nb, 0, :]
                nc.scalar.activation(at, t_ps[:, 0:nb * P].rearrange("p (b d) -> p b d", d=D), ACT.Copy, scale=SPLIT).then_inc(hi_done, 1)

            def chunk(s, c, parity):
                k = s * NCH + c
                w = chunk_width(c)
                sums(k, 0, w)
                if not is_first(c):
                    messages(k - 1, CH)
                sums(k, 1, w)
                if not is_first(c):
                    gates(k - 1, CH)
                sums(k, 2, w)
                if not is_first(c):
                    turn(k - 1, c - 1, CH, parity)
                sums(k, 3, w)
                if is_last(c):
                    messages(k, w)
                    gates(k, w)
                    turn(k, c, w, parity)

            steps(act, chunk)

        @block.vector
        def _(dve):
            dve.sem_inc(h_done, 1)
            dve.sem_inc(lo_done, NCH)
            nc.vector.tensor_tensor(b_rz[:, :], keep.b_ih[:, 0:2], keep.b_hh[:, 0:2], ALU.add)
            nc.vector.memset(h_new[:, :], 0.0).then_inc(bias_ready, 1)
            dve.wait_ge(bias_ready, 1)
            OWN = 4

            def unit(k, c, w):
                own = k * OWN
                dve.wait_ge(rz_done, k + 1)
                nc.vector.scalar_tensor_tensor(out=u_sb[:, 0:w], in0=hn_ps[:, 0:w], scalar=keep.b_hh[:, 2:3], in1=r_sb[:, 0:w],
                                               op0=ALU.add, op1=ALU.mult).then_inc(chain, 1)
                dve.wait_ge(chain, own + 1)
                nc.vector.tensor_tensor(n_sb[:, 0:w], in_ps[:, 0:w], u_sb[:, 0:w], ALU.add).then_inc(cand_done, 1)
                dve.wait_ge(n_done, k + 2)
                h = keep.xt[:, cols(c, w)]
                nc.vector.tensor_tensor(u_sb[:, 0:w], h, n_sb[:, 0:w], ALU.subtract).then_inc(chain, 1)
                dve.wait_ge(chain, own + 2)
                nc.vector.tensor_tensor(u_sb[:, 0:w], u_sb[:, 0:w], z_sb[:, 0:w], ALU.mult).then_inc(chain, 1)
                dve.wait_ge(chain, own + 3)
                dve.wait_ge(t_done, k + 1)
                nc.vector.tensor_tensor(h_new[:, 0:w], u_sb[:, 0:w], n_sb[:, 0:w], ALU.add).then_inc(h_done, 1)
                dve.wait_ge(h_done, k + 2)
                dve.nop(nofuse=True)
                nc.vector.tensor_copy(keep.xt[:, cols(c, w)], h_new[:, 0:w]).then_inc(chain, 1)

            def turn(k, c, w, parity):
                nb = (w + P - 1) // P
                dve.wait_ge(t_done, k + 2)
                dve.wait_ge(hi_done, k + (NCH + 1))

                def half(i):
                    return keep.halves[:, 1 - parity, bass.ds(c * 4, nb), i, :] if not isinstance(c, int) else keep.halves[:, 1 - parity, 4 * c:4 * c + nb, i, :]

                nc.vector.scalar_tensor_tensor(out=half(1), in0=t_ps[:, 0:nb * P].rearrange("p (b d) -> p b d", d=D), scalar=SPLIT,
                                               in1=half(0), op0=ALU.mult, op1=ALU.subtract).then_inc(lo_done, 1)

            def chunk(s, c, parity):
                k = s * NCH + c
                if not is_first(c):
                    unit(k - 1, c - 1, CH)
                    turn(k - 1, c - 1, CH, parity)
                if is_last(c):
                    unit(k, c, chunk_width(c))
                    turn(k, c, chunk_width(c), parity)

            steps(dve, chunk)


def verdict(nc, keep):
    FIFTEEN = 0x57
    with ExitStack() as ctx:
        m = Memory(nc, ctx, "verdict_")
        sums = m.sb("sums", [P, 2], F32)
        most = m.sb("most", [P, 1], F32)
        ones = m.sb("ones", [P, 1], F32)
        total = m.sb("total", [1, 4], F32)
        ps = m.ps("ps", [1, 2])
        ready = m.sem("ready")
        summed = m.sem("summed")
        chain = m.sem("chain")
        block = ctx.enter_context(nc.Block())

        @block.vector
        def _(dve):
            ch = Chain(dve, chain)
            nc.vector.memset(ones[:, :], 1.0)
            nc.vector.tensor_reduce(sums[:, 0:1], keep.deg[:, :], AX.X, ALU.add)
            ch.step(nc.vector.tensor_reduce(most[:, :], keep.largest[:, :], AX.X, ALU.max))
            nc.vector.tensor_scalar(sums[:, 1:2], most[:, :], float(FIFTEEN), None, ALU.is_gt).then_inc(ready, 1)
            dve.wait_ge(summed, 1)
            ch.step(nc.vector.tensor_copy(total[:, 0:2], ps[:, :]))
            ch.step(nc.vector.tensor_scalar(total[:, 2:3], total[:, 0:1], float(E), None, ALU.not_equal))
            ch.step(nc.vector.tensor_tensor(total[:, 3:4], total[:, 2:3], total[:, 1:2], ALU.add))
            ch.step(nc.vector.tensor_scalar(keep.amiss[:, :], total[:, 3:4], 0.0, None, ALU.is_gt))

        @block.tensor
        def _(pe):
            pe.wait_ge(ready, 1)
            nc.tensor.matmul(ps[:, :], ones[:, :], sums[:, :], start=True, stop=True).then_inc(summed, 1)


def reload(nc, ins, keep, scratch):
    with ExitStack() as ctx:
        m = Memory(nc, ctx, "reload_")
        fields = m.sb("fields", [EP, BPP, 4, EB], F32)
        sel_i = m.sb("sel_i", [T, T * P], I32)
        ps = m.ps("ps", [P, 2, 512])
        loaded = m.sem("loaded")
        cleared = m.sem("cleared")
        turned = m.sem("turned")
        left = m.sem("left")
        chain = m.sem("chain")
        block = ctx.enter_context(nc.Block())

        @block.sync
        def _(sp):
            sp.wait_ge(cleared, 1)
            sp.dma_start(keep.x_nm[:, 0:NB - 1, :], ins["x"][0:(NB - 1) * P, :].rearrange("(b p) d -> p b d", p=P)).then_inc(loaded, 16)
            sp.dma_start(keep.x_nm[0:LAST, NB - 1, :], ins["x"][(NB - 1) * P:N, :]).then_inc(loaded, 16)
            sp.dma_start(fields[:, :, :, :].rearrange("p b a e -> p b (a e)"),
                         scratch.fields[0:NEB, :].rearrange("(p b) f -> p b f", p=EP)).then_inc(loaded, 16)

        @block.gpsimd
        def _(pool):
            nc.gpsimd.memset(keep.x_nm[:, NB - 1, :], 0.0).then_inc(cleared, 1)
            nc.gpsimd.iota(keep.nodes[:, :], [[1, NCOL]], base=0, channel_multiplier=0).then_inc(cleared, 1)
            nc.gpsimd.iota(sel_i[:, :], [[1, T * P]], base=0, channel_multiplier=-P).then_inc(cleared, 1)

        @block.vector
        def _(dve):
            ch = Chain(dve, chain)
            dve.wait_ge(loaded, 48)
            dve.wait_ge(cleared, 3)

            def blocks(a):
                return a.rearrange("p (b e) -> p b e", e=EB)

            dv = blocks(keep.edge_dst[:, :])
            nc.vector.tensor_copy(dv, fields[:, :, 0, :])
            ch.step(nc.vector.scalar_tensor_tensor(out=blocks(keep.node_f[:, :]), in0=fields[:, :, 1, :], scalar=float(P) / WD,
                                                   in1=fields[:, :, 3, :], op0=ALU.mult, op1=ALU.add))
            nc.vector.tensor_copy(keep.src_row[:, 0, :], keep.node_f[:, :])
            nc.vector.scalar_tensor_tensor(out=blocks(keep.src_row[:, 1, :]), in0=fields[:, :, 2, :], scalar=float(NCOL) / TYW,
                                           in1=blocks(keep.node_f[:, :]), op0=ALU.mult, op1=ALU.add)
            ch.step(nc.vector.tensor_scalar(keep.select[:, :], sel_i[:, :], 0.0, None, ALU.is_ge))
            ch.step(nc.vector.scalar_tensor_tensor(out=keep.select[:, :], in0=sel_i[:, :], scalar=float(P), in1=keep.select[:, :],
                                                   op0=ALU.is_lt, op1=ALU.mult))

        @block.tensor
        def _(pe):
            pe.wait_ge(loaded, 48)
            for q, b0, n in node_groups():
                if q >= 2:
                    pe.wait_ge(left, q - 1)
                for i in range(n):
                    last = nc.tensor.transpose(ps[:, q % 2, i * P:(i + 1) * P], keep.x_nm[:, b0 + i, :], keep.ident[:, :])
                last.then_inc(turned, 1)

        @block.scalar
        def _(act):
            for q, b0, n in node_groups():
                act.wait_ge(turned, q + 1)
                nc.scalar.activation(keep.xt[:, b0 * P:(b0 + n) * P], ps[:, q % 2, 0:n * P], ACT.Copy).then_inc(left, 1)


def gather_sums(nc, keep, scratch, typed):
    with ExitStack() as ctx:
        m = Memory(nc, ctx, "typed_" if typed else "plain_")
        table = m.sb("table", [P, NB, D], F32)
        ps = m.ps("ps", [P, 7, 512])
        made = m.sem("made")
        left = m.sem("left")
        stored = m.sem("stored")
        row = m.sb("row", [EP, 1], U32)
        message = m.sb("message", [EP, D], F32)
        hot = m.sb("hot", [EP, NCOL], F32)
        total = m.sb("total", [P, NB * D], F32)
        row_ready = m.sem("row_ready")
        hot_ready = m.sem("hot_ready")
        gathered = m.sem("gathered")
        multiplied = m.sem("multiplied")
        added = m.sem("added")
        types = T if typed else 1
        SLICES = len(node_groups())
        block = ctx.enter_context(nc.Block())

        @block.tensor
        def _(pe):
            for t in range(types):
                if t:
                    pe.wait_ge(left, SLICES * t)
                for q, b0, n in node_groups():
                    for i in range(n):
                        cell = ps[:, q, i * P:(i + 1) * P]
                        nodes = keep.xt[:, (b0 + i) * P:(b0 + i + 1) * P]
                        if typed:
                            nc.tensor.matmul(cell, nodes, keep.wet[:, t, :], start=True, stop=False)
                            last = nc.tensor.matmul(cell, keep.select[:, t * P:(t + 1) * P], keep.b_edge[:, :], start=False, stop=True)
                        else:
                            last = nc.tensor.transpose(cell, nodes, keep.ident[:, :])
                    last.then_inc(made, 1)
            pe.wait_ge(left, SLICES * types)
            with pe.Fori(0, EF, 1) as j:
                pe.wait_ge(gathered, j * 16 + 16)
                pe.nop(nofuse=True)
                pe.wait_ge(hot_ready, j + 1)
                pe.nop(nofuse=True)
                for b in range(NB):
                    last = nc.tensor.matmul(ps[:, b // 4, (b % 4) * D:(b % 4 + 1) * D], hot[:, b * P:(b + 1) * P], message[:, :],
                                            start=True, stop=True)
                last.then_inc(multiplied, 1)
            pe.wait_ge(added, (EF + 1))
            for q, b0, n in node_groups():
                for i in range(n):
                    last = nc.tensor.transpose(ps[:, q, i * P:(i + 1) * P], total[:, (b0 + i) * D:(b0 + i + 1) * D], keep.ident[:, :])
                last.then_inc(made, 1)

        @block.scalar
        def _(act):
            for t in range(types):
                if t:
                    act.wait_ge(stored, 16 * t)
                for q, b0, n in node_groups():
                    act.wait_ge(made, SLICES * t + q + 1)
                    nc.scalar.activation(table[:, b0:b0 + n, :].rearrange("p b d -> p (b d)"), ps[:, q, 0:n * D], ACT.Copy).then_inc(left, 1)
            for q, b0, n in node_groups():
                act.wait_ge(made, SLICES * types + q + 1)
                nc.scalar.activation(keep.st[:, b0 * P:(b0 + n) * P], ps[:, q, 0:n * P], ACT.Copy)

        @block.sync
        def _(sp):
            for t in range(types):
                sp.wait_ge(left, SLICES * (t + 1))
                sp.dma_start(scratch.table[t * NCOL:(t + 1) * NCOL, :].rearrange("(b p) d -> p b d", p=P), table[:, :, :]).then_inc(stored, 16)

        @block.gpsimd
        def _(pool):
            pool.wait_ge(stored, 16 * types)
            with pool.Fori(0, EF, 1) as j:
                pool.wait_ge(row_ready, j + 1)
                pool.nop(nofuse=True)
                nc.gpsimd.indirect_dma_start(message[:, :], None, scratch.table,
                                             bass.IndirectOffsetOnAxis(ap=row[:, :], axis=0)).then_inc(gathered, 16)

        @block.vector
        def _(dve):
            nc.vector.memset(total[:, :], 0.0).then_inc(added, 1)
            with dve.Fori(0, EF, 1) as j:
                dve.wait_ge(added, j + 1)
                dve.nop(nofuse=True)
                nc.vector.tensor_copy(row[:, :], keep.src_row[:, 1 if typed else 0, bass.ds(j, 1)]).then_inc(row_ready, 1)
                nc.vector.tensor_scalar(hot[:, :], keep.nodes[0:EP, :], keep.edge_dst[:, bass.ds(j, 1)], None, ALU.is_equal).then_inc(hot_ready, 1)
                dve.wait_ge(multiplied, j + 1)
                dve.nop(nofuse=True)
                for q, b0, n in node_groups():
                    s = total[:, b0 * D:(b0 + n) * D]
                    last = nc.vector.tensor_tensor(s, ps[:, q, 0:n * D], s, ALU.add)
                last.then_inc(added, 1)


def gated_unit(nc, keep):
    with ExitStack() as ctx:
        m = Memory(nc, ctx, "unit_")
        r = m.sb("r", [D, CH], F32)
        z = m.sb("z", [D, CH], F32)
        n = m.sb("n", [D, CH], F32)
        u = m.sb("u", [D, CH], F32)
        b_rz = m.sb("b_rz", [D, 2], F32)
        rz_ps = m.ps("rz_ps", [D, 2, CH])
        in_ps = m.ps("in_ps", [D, CH])
        hn_ps = m.ps("hn_ps", [D, CH])
        gates = m.sem("gates")
        bias_ready = m.sem("bias_ready")
        rz = m.sem("rz")
        cand = m.sem("cand")
        act_n = m.sem("act_n")
        h_done = m.sem("h_done")
        chain = m.sem("chain")
        block = ctx.enter_context(nc.Block())

        @block.tensor
        def _(pe):
            for c in range(NCH):
                w = chunk_width(c)
                h, a = keep.xt[:, c * CH:c * CH + w], keep.st[:, c * CH:c * CH + w]
                if c:
                    pe.wait_ge(h_done, c)
                for g in range(2):
                    nc.tensor.matmul(rz_ps[:, g, 0:w], keep.wht[:, g, :], h, start=True, stop=False)
                    nc.tensor.matmul(rz_ps[:, g, 0:w], keep.wit[:, g, :], a, start=False, stop=True)
                nc.tensor.matmul(hn_ps[:, 0:w], keep.wht[:, 2, :], h, start=True, stop=True)
                nc.tensor.matmul(in_ps[:, 0:w], keep.wit[:, 2, :], a, start=True, stop=True).then_inc(gates, 1)

        @block.scalar
        def _(act):
            act.wait_ge(bias_ready, 1)
            for c in range(NCH):
                w = chunk_width(c)
                act.wait_ge(gates, c + 1)
                nc.scalar.activation(r[:, 0:w], rz_ps[:, 0, 0:w], ACT.Sigmoid, bias=b_rz[:, 0:1])
                nc.scalar.activation(z[:, 0:w], rz_ps[:, 1, 0:w], ACT.Sigmoid, bias=b_rz[:, 1:2]).then_inc(rz, 1)
                act.wait_ge(cand, c + 1)
                nc.scalar.activation(n[:, 0:w], n[:, 0:w], ACT.Tanh, bias=keep.b_ih[:, 2:3]).then_inc(act_n, 1)

        @block.vector
        def _(dve):
            ch = Chain(dve, chain)
            nc.vector.tensor_tensor(b_rz[:, :], keep.b_ih[:, 0:2], keep.b_hh[:, 0:2], ALU.add).then_inc(bias_ready, 1)
            for c in range(NCH):
                w = chunk_width(c)
                h = keep.xt[:, c * CH:c * CH + w]
                dve.wait_ge(rz, c + 1)
                ch.step(nc.vector.scalar_tensor_tensor(out=u[:, 0:w], in0=hn_ps[:, 0:w], scalar=keep.b_hh[:, 2:3], in1=r[:, 0:w],
                                                       op0=ALU.add, op1=ALU.mult))
                nc.vector.tensor_tensor(n[:, 0:w], in_ps[:, 0:w], u[:, 0:w], ALU.add).then_inc(cand, 1)
                dve.wait_ge(act_n, c + 1)
                ch.step(nc.vector.tensor_tensor(u[:, 0:w], h, n[:, 0:w], ALU.subtract))
                ch.step(nc.vector.tensor_tensor(u[:, 0:w], u[:, 0:w], z[:, 0:w], ALU.mult))
                nc.vector.tensor_tensor(h, u[:, 0:w], n[:, 0:w], ALU.add).then_inc(h_done, 1)


def general(nc, ins, keep, scratch, out):
    with ExitStack() as ctx:
        m = Memory(nc, ctx, "general_")
        keep.nodes = m.sb("nodes", [P, NCOL], I32)
        keep.edge_dst = m.sb("edge_dst", [EP, EF], F32)
        keep.node_f = m.sb("node_f", [EP, EF], F32)
        keep.src_row = m.sb("src_row", [EP, 2, EF], U32)
        keep.select = m.sb("select", [T, T * P], F32)
        keep.st = m.sb("st", [D, NCOL], F32)
        reload(nc, ins, keep, scratch)
        with nc.Fori(0, L, 1) as l:
            gather_sums(nc, keep, scratch, False)
            first_network(nc, keep, l)
        normalise(nc, keep, None, "general_middle_")
        with nc.Fori(0, STEPS, 1) as s:
            gather_sums(nc, keep, scratch, True)
            gated_unit(nc, keep)
        normalise(nc, keep, out, "general_end_")


class Kept:

    def __init__(self, m):
        self.ident = m.sb("ident", [P, P], F32)
        self.sum3 = m.sb("sum3", [3 * H, H], F32)
        self.iota = m.sb("iota", [P, T * TYW], F16)
        self.iota1 = m.sb("iota1", [P, P], F16)
        self.w1t = m.sb("w1t", [D, L * H], F32)
        self.w2t = m.sb("w2t", [H, L, H], F32)
        self.w3t = m.sb("w3t", [H, L, D], F32)
        self.wet = m.sb("wet", [D, T, D], F32)
        self.wit = m.sb("wit", [D, 3, D], F32)
        self.wht = m.sb("wht", [D, 3, D], F32)
        self.b_edge = m.sb("b_edge", [T, D], F32)
        self.b_ih = m.sb("b_ih", [D, 3], F32)
        self.b_hh = m.sb("b_hh", [D, 3], F32)
        self.eps = m.sb("eps", [P, L], F32)
        self.b1 = m.sb("b1", [H, L], F32)
        self.g1 = m.sb("g1", [H, L], F32)
        self.bt1 = m.sb("bt1", [H, L], F32)
        self.b2 = m.sb("b2", [H, L], F32)
        self.g2 = m.sb("g2", [H, L], F32)
        self.bt2 = m.sb("bt2", [H, L], F32)
        self.b3 = m.sb("b3", [D, L], F32)
        self.x_nm = m.sb("x_nm", [P, NB, D], F32)
        self.xt = m.sb("xt", [D, NCOL], F32)
        self.amiss = m.sb("amiss", [1, 1], I32)
        self.deg = m.sb("deg", [P, NWG * WC], F32)
        self.largest = m.sb("largest", [P, L * NCH], F32)


class Scratch:

    def __init__(self, nc):
        self.fields = nc.dram_tensor("edge_fields", (NEB + BPW - 1, 4 * EB), F32).ap()
        self.table = nc.dram_tensor("messages", (T * NCOL, D), F32).ap()
        self.adj = nc.dram_tensor("adjacency", (NU, P, T * NB * UD // 4), F32).ap()


def gnn(nc, ins, out):
    scratch = Scratch(nc)
    with ExitStack() as ctx:
        keep = Kept(Memory(nc, ctx))
        with ExitStack() as first:
            m = Memory(nc, first)
            keep.dkey = m.sb("dkey", [P, NWG, TPW * P], F32)
            keep.key = m.sb("key", [P, 3, TPW, NWG * P], F32)
            prepare(nc, ins, keep, scratch)
            keep.adj_words = m.sb("adj", [P, NU, NB * UD // 4], F32)
            words = keep.adj_words[:, :, :].rearrange("p u f -> p (u f)")
            keep.adj = words.bitcast(F8).rearrange("p (u b d) -> p u b d", u=NU, b=NB)
            keep.adj_bytes = words.bitcast(mybir.dt.uint8)
            build(nc, keep, scratch)
            first_network(nc, keep)
        with ExitStack() as second:
            m = Memory(nc, second)
            keep.deg_row = m.sb("deg_row", [T, NWG * P * WD], F32)
            keep.halves = m.sb("halves", [P, 2, NB, 2, D], F16)
            normalise(nc, keep, None, "middle_")
            second_network(nc, keep, scratch)
            normalise(nc, keep, out, "end_")
            verdict(nc, keep)
            amiss = nc.values_load(keep.amiss[0:1, 0:1], min_val=0, max_val=1)
            with nc.If(amiss > 0):
                general(nc, ins, keep, scratch, out)


def kernel(**inputs):
    import numpy as np
    import concourse.bacc as _bacc
    from concourse.bass_utils import run_bass_kernel_spmd as _run

    nc = _bacc.Bacc("TRN2", target_bir_lowering=False, num_devices=1)
    arrays, aps = {}, {}
    for name, a in inputs.items():
        a = np.ascontiguousarray(a)
        arrays["in_" + name] = a
        aps[name] = nc.dram_tensor("in_" + name, a.shape, mybir.dt.from_np(a.dtype), kind="ExternalInput").ap()
    out = nc.dram_tensor("out", (N, D), F32, kind="ExternalOutput").ap()
    gnn(nc, aps, out)
    r = _run(nc, [arrays], core_ids=[0])
    return r.results[0]["out"]
```

```python
from contextlib import ExitStack, nullcontext

import concourse.bass as bass
from concourse import mybir

F32 = mybir.dt.float32
F16 = mybir.dt.float16
BF16 = mybir.dt.bfloat16
F8 = mybir.dt.float8e4
I32 = mybir.dt.int32
U32 = mybir.dt.uint32
ALU = mybir.AluOpType
ACT = mybir.ActivationFunctionType
AX = mybir.AxisListType

P = 128
N = 3125
E = 100000
D = 128
H = 32
L = 4
T = 4
STEPS = 4
EPS = 1e-5

NB = (N + P - 1) // P
LAST = N - (NB - 1) * P
UD = 64
NU = (N + UD - 1) // UD
NPAD = NU * UD
NCOL = NB * P
WD = 8
WPU = UD // WD
WC = T * WD
NWG = 4
TPW = 3
EB = 32
BPW = TPW * P // EB
NEB = E // EB
EP = 125
EF = E // EP
BPP = EF // EB
TYW = NB * WD
CH = 512
UPC = CH // UD
NCH = (NPAD + CH - 1) // CH
TAIL = NPAD - (NCH - 1) * CH
SPLIT = 1024.0
FIFTEEN = 0x57
assert NEB * EB == E and EP * EF == E and TAIL == UD and NCH * 4 >= NB


def chunk_width(c):
    return CH if not isinstance(c, int) or c < NCH - 1 else TAIL


class Memory:

    def __init__(self, nc, ctx, prefix="", again=False):
        self.nc, self.ctx, self.prefix, self.again, self.sems = nc, ctx, prefix, again, []
        if again:
            ctx.callback(self.clear)

    def sb(self, name, shape, dt):
        return self.ctx.enter_context(self.nc.sbuf_tensor(self.prefix + name, shape, dt))

    def ps(self, name, shape, dt=F32):
        return self.ctx.enter_context(self.nc.psum_tensor(self.prefix + name, shape, dt))

    def sem(self, name):
        if not self.again:
            return self.ctx.enter_context(self.nc.semaphore(self.prefix + name))
        self.sems.append(self.nc.alloc_semaphore(self.prefix + name))
        return self.sems[-1]

    def clear(self):
        self.nc.clear_and_free_semaphores(self.sems)
        self.nc.all_engine_barrier()


class Chain:

    def __init__(self, engine, sem):
        self.engine, self.sem, self.n, self.base = engine, sem, 0, 0

    def step(self, instruction):
        self.n += 1
        instruction.then_inc(self.sem, 1)
        self.engine.wait_ge(self.sem, self.base + self.n)
        if not isinstance(self.base, int):
            self.engine.nop(nofuse=True)


def prepare(nc, ins, keep, scratch):
    with ExitStack() as ctx:
        m = Memory(nc, ctx)
        src_i = m.sb("src_i", [EP, EF], I32)
        dst_i = m.sb("dst_i", [EP, EF], I32)
        hi_i = m.sb("hi_i", [EP, EF], I32)
        lo_i = m.sb("lo_i", [EP, EF], I32)
        attr = m.sb("attr", [EP, EF, T], F32)
        dst_f = m.sb("dst_f", [EP, EF], F32)
        top01 = m.sb("top01", [EP, EF], F32)
        top = m.sb("top", [EP, EF], F32)
        not0 = m.sb("not0", [EP, EF], F32)
        not1 = m.sb("not1", [EP, EF], F32)
        not2 = top01
        fields = m.sb("fields", [EP, BPP, 4, EB], F32)
        filler = m.sb("filler", [BPW - 1, 4 * EB], F32)
        iota_i = m.sb("iota_i", [P, T * TYW], I32)
        thr = m.sb("thr", [EP, NWG * P], F16)
        below = m.sb("below", [EP, BPP, NWG * P], BF16)
        ones = m.sb("ones", [EP, 1], BF16)
        start = m.sb("start", [P, NWG], F32)
        step_i = m.sb("step_i", [P, NWG, BPW], I32)
        step_f = m.sb("step_f", [P, NWG, BPW], F32)
        w8_i = m.sb("w8_i", [P, NWG], I32)
        w1_raw = m.sb("w1_raw", [L * H, D], F32)
        w2_raw = m.sb("w2_raw", [H, L, H], F32)
        w3_raw = m.sb("w3_raw", [D, L, H], F32)
        we_raw = m.sb("we_raw", [D, T, D], F32)
        wi_raw = m.sb("wi_raw", [D, 3, D], F32)
        wh_raw = m.sb("wh_raw", [D, 3, D], F32)
        count_ps = m.ps("count_ps", [P, NWG])
        turn_ps = m.ps("turn_ps", [P, 2, 512])

        edges_in = m.sem("edges_in")
        weights_in = m.sem("weights_in")
        small_in = m.sem("small_in")
        iotas = m.sem("iotas")
        ident_set = m.sem("ident_set")
        dve_chain = m.sem("dve_chain")
        fields_ready = m.sem("fields_ready")
        filler_ready = m.sem("filler_ready")
        fields_out = m.sem("fields_out")
        compared = m.sem("compared")
        counted = m.sem("counted")
        turned = m.sem("turned")
        turned_out = m.sem("turned_out")
        block = ctx.enter_context(nc.Block())

        turns = [(w1_raw[:, :], keep.w1t[:, :])]
        turns += [(w2_raw[:, l, :], keep.w2t[:, l, :]) for l in range(L)]
        turns += [(w3_raw[:, l, :], keep.w3t[:, l, :]) for l in range(L)]
        turns += [(we_raw[:, t, :], keep.wet[:, t, :]) for t in range(T)]
        turns += [(wi_raw[:, g, :], keep.wit[:, g, :]) for g in range(3)]
        turns += [(wh_raw[:, g, :], keep.wht[:, g, :]) for g in range(3)]

        @block.sync
        def _(sp):
            sp.dma_start(dst_i[:, :], ins["dst"].rearrange("(p f) -> p f", p=EP)).then_inc(edges_in, 16)
            sp.dma_start(src_i[:, :], ins["src"].rearrange("(p f) -> p f", p=EP)).then_inc(edges_in, 16)
            sp.dma_start(attr[:, :, :], ins["edge_attr_4"].rearrange("(p f) t -> p f t", p=EP)).then_inc(edges_in, 16)
            sp.wait_ge(fields_ready, 1)
            sp.dma_start(scratch.fields[0:NEB, :].rearrange("(p b) f -> p b f", p=EP),
                         fields[:, :, :, :].rearrange("p b a e -> p b (a e)")).then_inc(fields_out, 16)
            sp.wait_ge(filler_ready, 1)
            sp.dma_start(scratch.fields[NEB:NEB + BPW - 1, :], filler[:, :]).then_inc(fields_out, 16)
            sp.wait_ge(fields_out, 32)

        @block.scalar
        def _(act):
            act.dma_start(w1_raw[:, :], ins["L0_gnn_W1"].rearrange("l h d -> (l h) d")).then_inc(weights_in, 16)
            act.dma_start(w2_raw[:, :, :], ins["L0_gnn_W2"].rearrange("l o i -> o l i")).then_inc(weights_in, 16)
            act.dma_start(w3_raw[:, :, :], ins["L0_gnn_W3"].rearrange("l o i -> o l i")).then_inc(weights_in, 16)
            act.dma_start(we_raw[:, :, :], ins["L1_gnn_W_edge"].rearrange("t o i -> o t i")).then_inc(weights_in, 16)
            act.dma_start(wi_raw[:, :, :], ins["L1_gnn_W_ih"].rearrange("(g o) i -> o g i", g=3)).then_inc(weights_in, 16)
            act.dma_start(wh_raw[:, :, :], ins["L1_gnn_W_hh"].rearrange("(g o) i -> o g i", g=3)).then_inc(weights_in, 16)
            small = [(keep.x_nm[:, 0:NB - 1, :], ins["x"][0:(NB - 1) * P, :].rearrange("(b p) d -> p b d", p=P)),
                     (keep.b_edge[:, :], ins["L1_gnn_b_edge"]),
                     (keep.b_ih[:, :], ins["L1_gnn_b_ih"].rearrange("(g o) -> o g", g=3)),
                     (keep.b_hh[:, :], ins["L1_gnn_b_hh"].rearrange("(g o) -> o g", g=3)),
                     (keep.eps[:, :], ins["L0_gnn_eps"].rearrange("(o l) -> o l", o=1).broadcast_to((P, L)))]
            for kept, name in ((keep.b1, "b1"), (keep.g1, "g1"), (keep.bt1, "bt1"),
                               (keep.b2, "b2"), (keep.g2, "g2"), (keep.bt2, "bt2"), (keep.b3, "b3")):
                small.append((kept[:, :], ins["L0_gnn_" + name].rearrange("l h -> h l")))
            for to, of in small:
                act.dma_start(to, of, allow_slow_non_contiguous=True).then_inc(small_in, 16)
            act.wait_ge(iotas, 1)
            act.dma_start(keep.x_nm[0:LAST, NB - 1, :], ins["x"][(NB - 1) * P:N, :]).then_inc(small_in, 16)
            for i, (raw, kept) in enumerate(turns):
                act.wait_ge(turned, i + 1)
                o, k = kept.shape[0], kept.shape[-1]
                nc.scalar.activation(kept, turn_ps[0:o, i % 2, 0:k], ACT.Copy).then_inc(turned_out, 1)
            act.wait_ge(small_in, 16 * (len(small) + 1))

        @block.gpsimd
        def _(pool):
            nc.gpsimd.memset(keep.x_nm[:, NB - 1, :], 0.0).then_inc(iotas, 1)
            nc.gpsimd.iota(w8_i[:, :], [[P * WD, NWG]], base=0, channel_multiplier=WD).then_inc(iotas, 1)
            nc.gpsimd.iota(step_i[:, :, :], [[0, NWG], [1, BPW]], base=0, channel_multiplier=0).then_inc(iotas, 1)
            nc.gpsimd.iota(iota_i[:, :], [[1, T * TYW]], base=0, channel_multiplier=0).then_inc(iotas, 1)
            nc.gpsimd.memset(keep.ident[:, :], 0.0).then_inc(ident_set, 1)
            nc.gpsimd.memset(keep.sum3[:, :], 0.0).then_inc(ident_set, 1)
            pool.wait_ge(ident_set, 2)
            nc.gpsimd.affine_select(out=keep.ident[:, :], in_=keep.ident[:, :], compare_op=ALU.not_equal, fill=1.0,
                                    base=0, pattern=[[-1, P]], channel_multiplier=1).then_inc(ident_set, 1)
            for s in range(3):
                pool.wait_ge(ident_set, 3 + s)
                nc.gpsimd.affine_select(out=keep.sum3[:, :], in_=keep.sum3[:, :], compare_op=ALU.not_equal, fill=1.0,
                                        base=-H * s, pattern=[[-1, H]], channel_multiplier=1).then_inc(ident_set, 1)

        @block.vector
        def _(dve):
            c = Chain(dve, dve_chain)
            nc.vector.memset(filler[:, :], -1.0).then_inc(filler_ready, 1)
            nc.vector.memset(keep.fifteen[:, :], -float(FIFTEEN))
            c.step(nc.vector.memset(ones[:, :], 1.0))
            dve.wait_ge(iotas, 4)
            nc.vector.tensor_scalar(thr[:, :], iota_i[0:EP, 0:NWG * P], float(WD), None, ALU.mult).then_inc(dve_chain, 1)
            nc.vector.tensor_copy(keep.iota[:, :], iota_i[:, :]).then_inc(dve_chain, 1)
            nc.vector.tensor_scalar(keep.iota1[:, :], iota_i[:, 0:P], 1.0, None, ALU.add).then_inc(dve_chain, 1)
            nc.vector.tensor_copy(step_f[:, :, :], step_i[:, :, :]).then_inc(dve_chain, 1)
            nc.vector.tensor_copy(keep.w8[:, :], w8_i[:, :]).then_inc(dve_chain, 1)
            c.n += 5
            dve.wait_ge(ident_set, 3)
            nc.vector.tensor_copy(keep.ident16[:, :], keep.ident[:, :])
            dve.wait_ge(edges_in, 48)
            c.step(nc.vector.tensor_copy(dst_f[:, :], dst_i[:, :]))
            for j in range(BPP):
                last = nc.vector.tensor_scalar(below[:, j, :], thr[:, :], dst_f[:, j * EB:j * EB + 1], None, ALU.is_gt)
            last.then_inc(compared, 1)
            nc.vector.tensor_tensor(top01[:, :], attr[:, :, 0], attr[:, :, 1], ALU.max).then_inc(dve_chain, 1)
            nc.vector.tensor_tensor(top[:, :], attr[:, :, 2], attr[:, :, 3], ALU.max).then_inc(dve_chain, 1)
            c.n += 2
            dve.wait_ge(dve_chain, c.n)
            c.step(nc.vector.tensor_tensor(top[:, :], top[:, :], top01[:, :], ALU.max))
            for i, (to) in enumerate((not0, not1, not2)):
                nc.vector.tensor_tensor(to[:, :], attr[:, :, i], top[:, :], ALU.not_equal).then_inc(dve_chain, 1)
            c.n += 3
            dve.wait_ge(dve_chain, c.n)
            c.step(nc.vector.scalar_tensor_tensor(out=not1[:, :], in0=not2[:, :], scalar=1.0, in1=not1[:, :], op0=ALU.add, op1=ALU.mult))
            c.step(nc.vector.scalar_tensor_tensor(out=not0[:, :], in0=not1[:, :], scalar=1.0, in1=not0[:, :], op0=ALU.add, op1=ALU.mult))
            nc.vector.tensor_scalar(hi_i[:, :], src_i[:, :], 7, None, ALU.arith_shift_right).then_inc(dve_chain, 1)
            nc.vector.tensor_scalar(lo_i[:, :], src_i[:, :], P - 1, None, ALU.bitwise_and).then_inc(dve_chain, 1)
            c.n += 2
            dve.wait_ge(dve_chain, c.n)

            def field(a):
                return fields[:, :, a, :]

            def blocks(a):
                return a[:, :].rearrange("p (b e) -> p b e", e=EB)

            nc.vector.tensor_copy(field(0), blocks(dst_f))
            nc.vector.tensor_scalar(field(1), blocks(hi_i), float(WD), None, ALU.mult)
            nc.vector.tensor_scalar(field(2), blocks(not0), float(TYW), None, ALU.mult)
            nc.vector.tensor_copy(field(3), blocks(lo_i)).then_inc(fields_ready, 1)
            dve.wait_ge(counted, 1)
            c.step(nc.vector.tensor_scalar(start[:, :], count_ps[:, :], -1.0, 0.0, ALU.add, ALU.max))
            for g in range(NWG):
                nc.vector.tensor_scalar(keep.row[:, g, :], step_f[:, g, :], start[:, g:g + 1], None, ALU.add)

        @block.tensor
        def _(pe):
            pe.wait_ge(ident_set, 3)
            pe.wait_ge(weights_in, 96)
            for i, (raw, kept) in enumerate(turns):
                if i >= 2:
                    pe.wait_ge(turned_out, i - 1)
                k, o = raw.shape[0], raw.shape[-1]
                nc.tensor.transpose(turn_ps[0:o, i % 2, 0:k], raw, keep.ident[0:k, 0:k]).then_inc(turned, 1)
            pe.wait_ge(compared, 1)
            for g in range(NWG):
                for j in range(BPP):
                    last = nc.tensor.matmul(count_ps[:, g:g + 1], below[:, j, g * P:(g + 1) * P], ones[:, :],
                                            start=(j == 0), stop=(j == BPP - 1))
            last.then_inc(counted, 1)


def build(nc, keep, scratch):
    R = 8
    QW = NB * UD // 4
    FG = P // WPU
    with ExitStack() as ctx:
        m = Memory(nc, ctx)
        got = m.sb("got", [P, NWG, BPW, 4 * EB], F32)
        dl = m.sb("dl", [P, BPW, EB], F32)
        inside = m.sb("inside", [P, BPW, EB], F32)
        wkey = m.sb("wkey", [P, 2, NWG, BPW, EB], F32)
        which = m.sb("which", [P, R, P], BF16)
        where = m.sb("where", [P, R, T * TYW], BF16)
        unit = m.sb("unit", [P, 2, T, NB, UD], F8)
        unit_all = m.sb("unit_all", [P, 2, NB, UD], F8)
        by_type = m.ps("by_type", [P, 2, 2, 512])
        sum_ps = m.ps("sum_ps", [P, 4, 512])

        gathered = [m.sem(f"gathered{g}") for g in range(NWG)]
        key_chain = m.sem("key_chain")
        wkeys_ready = m.sem("wkeys_ready")
        keys_turned = m.sem("keys_turned")
        keys_out = m.sem("keys_out")
        hot = m.sem("hot")
        hot_free = m.sem("hot_free")
        window_free = m.sem("window_free")
        sum_done = m.sem("sum_done")
        sum_left = m.sem("sum_left")
        unit_out = [m.sem("unit_out0"), m.sem("unit_out1")]
        block = ctx.enter_context(nc.Block())
        V = WPU * TPW

        def units(engine, keys, unit_of):
            keys(0)
            with engine.Fori(0, FG, 2) as u:
                unit_of(u, 0)
                unit_of(u + 1, 1)
            for g in range(1, NWG):
                keys(g)
            with engine.Fori(FG, NU - 1, 2) as u:
                unit_of(u, 0)
                unit_of(u + 1, 1)
            unit_of(NU - 1, 0)

        @block.gpsimd
        def _(pool):
            for g in range(NWG):
                for k in range(BPW):
                    nc.gpsimd.indirect_dma_start(
                        got[:, g, k, :], None, scratch.fields,
                        bass.IndirectOffsetOnAxis(ap=keep.row[:, g, k:k + 1], axis=0)).then_inc(gathered[g], 16)

        @block.vector
        def _(dve):
            c = Chain(dve, key_chain)

            def keys(g):
                dve.wait_ge(gathered[g], 16 * BPW)
                v = got[:, g, :, :].rearrange("p b (a e) -> p b a e", a=4)
                d, i, k = dl[:, :, :], inside[:, :, :], keep.dkey[:, g, :].rearrange("p (b e) -> p b e", e=EB)
                c.step(nc.vector.tensor_scalar(d, v[:, :, 0, :], keep.w8[:, g:g + 1], None, ALU.subtract))
                nc.vector.tensor_tensor(wkey[:, 1, g, :, :], v[:, :, 1, :], d, ALU.add).then_inc(key_chain, 1)
                nc.vector.tensor_scalar(i, d, 0.0, None, ALU.is_ge).then_inc(key_chain, 1)
                c.n += 2
                dve.wait_ge(key_chain, c.n)
                nc.vector.tensor_tensor(wkey[:, 1, g, :, :], wkey[:, 1, g, :, :], v[:, :, 2, :], ALU.add).then_inc(key_chain, 1)
                c.n += 1
                c.step(nc.vector.scalar_tensor_tensor(out=i, in0=d, scalar=float(WD), in1=i, op0=ALU.is_lt, op1=ALU.mult))
                nc.vector.scalar_tensor_tensor(out=wkey[:, 0, g, :, :], in0=v[:, :, 3, :], scalar=1.0, in1=i,
                                               op0=ALU.add, op1=ALU.mult).then_inc(wkeys_ready, 1)
                c.step(nc.vector.tensor_scalar(d, d, 1.0, None, ALU.add))
                c.step(nc.vector.scalar_tensor_tensor(out=k, in0=v[:, :, 2, :], scalar=float(WD) / TYW, in1=d,
                                                      op0=ALU.mult, op1=ALU.add))
                c.step(nc.vector.tensor_tensor(k, k, i, ALU.mult))
                if g in (0, NWG - 1):
                    dve.wait_ge(keys_out, 2 * (g + 1))

            def fill(u, parity):
                for i in range(WPU):
                    for j in range(TPW):
                        v = i * TPW + j
                        r = (parity * V + v) % R
                        dve.wait_ge(hot_free, (u * V + v) + 1)
                        w = u * WPU + i
                        nc.vector.tensor_scalar(which[:, r, :], keep.iota1[:, :], keep.key[:, 0, j, bass.ds(w, 1)], None, ALU.is_equal)
                        nc.vector.tensor_scalar(where[:, r, :], keep.iota[:, :], keep.key[:, 1, j, bass.ds(w, 1)], None,
                                                ALU.is_equal).then_inc(hot, 1)

            units(dve, keys, fill)

        @block.tensor
        def _(pe):
            pe.sem_inc(hot_free, R)

            def keys(g):
                if g:
                    pe.wait_ge(sum_left, 4 * FG + 4)
                    if g > 1:
                        pe.wait_ge(keys_out, 2 * g)
                pe.wait_ge(wkeys_ready, g + 1)
                for a in range(2):
                    for j in range(TPW):
                        seen = wkey[:, a, g, :, :].rearrange("p b e -> p (b e)")[:, j * P:(j + 1) * P]
                        last = nc.tensor.transpose(sum_ps[:, a, j * P:(j + 1) * P], seen, keep.ident[:, :])
                    last.then_inc(keys_turned, 1)

            def count(u, parity):
                for i in range(WPU):
                    pe.wait_ge(window_free, (u * WPU + i) + 1)
                    for j in range(TPW):
                        v = i * TPW + j
                        r = (parity * V + v) % R
                        pe.wait_ge(hot, (u * V + v) + 1)
                        for h in range(2):
                            last = nc.tensor.matmul(by_type[:, i % 2, h, 0:2 * TYW], which[:, r, :],
                                                    where[:, r, h * 2 * TYW:(h + 1) * 2 * TYW], start=(j == 0), stop=(j == TPW - 1))
                        last.then_inc(hot_free, 1)
                pe.wait_ge(sum_left, u * 4 + 4)
                pe.wait_ge(window_free, u * WPU + (WPU + 2))
                pe.nop(nofuse=True)
                for q in range(4):
                    for t in range(T):
                        of = unit[:, parity, t, :, :].rearrange("p b d -> p (b d)")[:, q * QW:(q + 1) * QW]
                        last = nc.tensor.matmul(sum_ps[:, q, 0:QW], keep.ident16[:, :], of, start=(t == 0), stop=(t == T - 1))
                    last.then_inc(sum_done, 1)

            units(pe, lambda g: (keys(g), pe.wait_ge(keys_out, 2 * (g + 1))), count)

        @block.scalar
        def _(act):
            act.sem_inc(window_free, 2)
            act.sem_inc(sum_left, 4)
            act.sem_inc(unit_out[0], 32)
            act.sem_inc(unit_out[1], 32)

            def keys(g):
                for a in range(2):
                    act.wait_ge(keys_turned, 2 * g + a + 1)
                    nc.scalar.activation(keep.key[:, a, :, g * P:(g + 1) * P],
                                         sum_ps[:, a, 0:TPW * P].rearrange("p (j w) -> p j w", w=P), ACT.Copy).then_inc(keys_out, 1)

            def leave(u, parity):
                act.wait_ge(unit_out[parity], (u - parity) * 16 + 32)
                act.nop(nofuse=True)
                for i in range(WPU):
                    act.wait_ge(hot_free, (u * WPU + i) * TPW + TPW + R)
                    act.nop(nofuse=True)
                    for h in range(2):
                        to = unit[:, parity, 2 * h:2 * h + 2, :, i * WD:(i + 1) * WD].rearrange("p t b d -> p (t b) d")
                        last = nc.scalar.activation(to, by_type[:, i % 2, h, 0:2 * TYW].rearrange("p (a d) -> p a d", d=WD),
                                                    ACT.Copy, saturate=False)
                    last.then_inc(window_free, 1)
                for q in range(4):
                    act.wait_ge(sum_done, u * 4 + q + 1)
                    act.nop(nofuse=True)
                    nc.scalar.activation(unit_all[:, parity, :, :].rearrange("p b d -> p (b d)")[:, q * QW:(q + 1) * QW],
                                         sum_ps[:, q, 0:QW], ACT.Copy, saturate=False).then_inc(sum_left, 1)

            units(act, keys, leave)

        @block.sync
        def _(sp):
            def store(u, parity):
                sp.wait_ge(sum_left, u * 4 + 8)
                sp.nop(nofuse=True)
                sp.dma_start(scratch.adj[bass.ds(u, 1), :, :].rearrange("u p f -> p (u f)"),
                             unit[:, parity, :, :, :].rearrange("p t b d -> p (t b d)").bitcast(F32)).then_inc(unit_out[parity], 16)
                sp.dma_start(keep.adj_words[:, bass.ds(u, 1), :].rearrange("p u f -> p (u f)"),
                             unit_all[:, parity, :, :].rearrange("p b d -> p (b d)").bitcast(F32)).then_inc(unit_out[parity], 16)

            with sp.Fori(0, NU - 1, 2) as u:
                store(u, 0)
                store(u + 1, 1)
            store(NU - 1, 0)
            sp.wait_ge(unit_out[0], 32 * ((NU + 1) // 2 + 1))
            sp.wait_ge(unit_out[1], 32 * ((NU - 1) // 2 + 1))


def node_groups():
    return [(q, 4 * q, min(4, NB - 4 * q)) for q in range((NB + 3) // 4)]


def first_network(nc, keep, layer=None):
    fast = layer is None
    with ExitStack() as ctx:
        m = Memory(nc, ctx, "" if fast else "layer_", again=not fast)
        parts = m.sb("parts", [P, NB, 3, H], BF16)
        rest = m.sb("rest", [P, 16 * H], F32)
        summed = m.sb("summed", [3 * H, 2, CH], F32)
        h1 = m.sb("h1", [H, NPAD], F32)
        h2 = m.sb("h2", [H, NPAD], F32)
        w1c = m.sb("w1c", [D, H], F32)
        w1e = m.sb("w1e", [D, H], F32)
        w2c = m.sb("w2c", [H, H], F32)
        w3c = m.sb("w3c", [H, D], F32)
        vec = m.sb("vec", [H, 6], F32)
        b3c = m.sb("b3c", [D, 1], F32)
        gain = m.sb("gain", [P, 1], F32)
        stats = m.sb("stats", [H, NCH, 6], F32)
        mv = m.sb("mv", [H, 2], F32)
        dev = m.sb("dev", [H, 2, 1], F32)
        root = m.sb("root", [H, 1], F32)
        scale = m.sb("scale", [H, 2, 1], F32)
        shift = m.sb("shift", [H, 2, 1], F32)
        excess = m.sb("excess", [P, SLICE], BF16)
        junk = m.sb("junk", [P, 5, TPW * P], F32)
        big = m.ps("big", [P, 2, 512])
        small = m.ps("small", [P, 2, 512])
        yps = m.ps("yps", [P, 2, 512])

        x_turned = m.sem("x_turned")
        x_left = m.sem("x_left")
        cur_ready = m.sem("cur_ready")
        xt_ready = m.sem("xt_ready")
        y_done = m.sem("y_done")
        parts_ready = m.sem("parts_ready")
        dense_done = m.sem("dense_done")
        sum_left = m.sem("sum_left")
        h1_done = m.sem("h1_done")
        h1_left = m.sem("h1_left")
        var_ready = m.sem("var_ready")
        root_ready = m.sem("root_ready")
        norm_ready = m.sem("norm_ready")
        relu1 = m.sem("relu1")
        h2_done = m.sem("h2_done")
        h2_left = m.sem("h2_left")
        relu2 = m.sem("relu2")
        x_done = m.sem("x_done")
        excess_done = m.sem("excess_done")
        chain = m.sem("chain")
        block = ctx.enter_context(nc.Block())

        spans = [(c, c * CH, chunk_width(c)) for c in range(NCH)]

        def layers(engine):
            return engine.Fori(0, L, 1) if fast else nullcontext(0)

        yb = [(0, 16), (16, NB - 16)]

        @block.tensor
        def _(pe):
            for q, b0, n in node_groups() if fast else ():
                if q >= 2:
                    pe.wait_ge(x_left, q - 1)
                for i in range(n):
                    last = nc.tensor.transpose(big[:, q % 2, i * P:(i + 1) * P], keep.x_nm[:, b0 + i, :], keep.ident[:, :])
                last.then_inc(x_turned, 1)
            with layers(pe) as l:
                pe.wait_ge(cur_ready, l + 1)
                pe.wait_ge(xt_ready, l * NCH + NCH)
                for q, (b0, n) in enumerate(yb if fast else ()):
                    for b in range(b0, b0 + n):
                        last = nc.tensor.matmul(yps[:, q, (b - b0) * H:(b - b0 + 1) * H], keep.xt[:, b * P:(b + 1) * P], w1c[:, :],
                                                start=True, stop=True)
                    last.then_inc(y_done, 1)

                def perceptron_in(c, at, w):
                    if fast:
                        pe.wait_ge(sum_left, l * NCH + (c + 1))
                    if c >= 2:
                        pe.wait_ge(h1_left, l * NCH + (c - 1))
                    if fast:
                        nc.tensor.matmul(small[0:H, c % 2, 0:w], keep.sum3[:, :], summed[:, c % 2, 0:w], start=True, stop=False)
                    else:
                        nc.tensor.matmul(small[0:H, c % 2, 0:w], w1c[:, :], keep.st[:, at:at + w], start=True, stop=False)
                    nc.tensor.matmul(small[0:H, c % 2, 0:w], w1e[:, :], keep.xt[:, at:at + w], start=False, stop=True).then_inc(h1_done, 1)

                if fast:
                    pe.wait_ge(parts_ready, l * 2 + 2)
                for c, at, w in spans if fast else ():
                    if c >= 2:
                        pe.wait_ge(sum_left, l * NCH + (c - 1))
                    pe.nop(nofuse=True)
                    for b in range(NB):
                        last = nc.tensor.matmul(big[0:3 * H, c % 2, 0:w], parts[:, b, :, :].rearrange("p s h -> p (s h)"),
                                                keep.adj[:, c * UPC:c * UPC + w // UD, b, :], start=(b == 0), stop=(b == NB - 1))
                    last.then_inc(dense_done, 1)
                    if c >= 1:
                        perceptron_in(*spans[c - 1])
                for span in spans[NCH - 1:] if fast else spans:
                    perceptron_in(*span)
                for c, at, w in spans:
                    pe.wait_ge(relu1, l * NCH + (c + 1))
                    if c >= 2:
                        pe.wait_ge(h2_left, l * NCH + (c - 1))
                    pe.nop(nofuse=True)
                    nc.tensor.matmul(small[0:H, c % 2, 0:w], w2c[:, :], h1[:, at:at + w], start=True, stop=True).then_inc(h2_done, 1)
                for c, at, w in spans:
                    pe.wait_ge(relu2, l * NCH + (c + 1))
                    if c >= 2:
                        pe.wait_ge(xt_ready, l * NCH + (NCH + c - 1))
                    nc.tensor.matmul(big[:, c % 2, 0:w], w3c[:, :], h2[:, at:at + w], start=True, stop=True).then_inc(x_done, 1)

        @block.scalar
        def _(act):
            for q, b0, n in node_groups() if fast else ():
                act.wait_ge(x_turned, q + 1)
                nc.scalar.activation(keep.xt[:, b0 * P:(b0 + n) * P], big[:, q % 2, 0:n * P], ACT.Copy).then_inc(x_left, 1)
            if fast:
                act.wait_ge(x_left, len(node_groups()))
            act.sem_inc(xt_ready, NCH)
            act.sem_inc(excess_done, 1)
            with layers(act) as l:
                def left1(c, at, w):
                    act.wait_ge(h1_done, l * NCH + (c + 1))
                    nc.scalar.activation(h1[:, at:at + w], small[0:H, c % 2, 0:w], ACT.Identity, bias=vec[:, 0:1]).then_inc(h1_left, 1)

                for c, at, w in spans if fast else ():
                    act.wait_ge(excess_done, l * NCH + (c + 1))
                    act.nop(nofuse=True)
                    nc.scalar.activation(excess[:, :], keep.adj_bytes[:, bass.ds((l * NCH + c) * SLICE, SLICE)], ACT.Relu,
                                         bias=keep.fifteen[:, :], accum_out=keep.excess[:, bass.ds(l * NCH + c, 1)]).then_inc(excess_done, 1)
                    act.wait_ge(dense_done, l * NCH + (c + 1))
                    if c >= 2:
                        act.wait_ge(h1_done, l * NCH + (c - 1))
                    nc.scalar.activation(summed[:, c % 2, 0:w], big[0:3 * H, c % 2, 0:w], ACT.Copy).then_inc(sum_left, 1)
                    if c >= 1:
                        left1(*spans[c - 1])
                for span in spans[NCH - 1:] if fast else spans:
                    left1(*span)
                act.wait_ge(var_ready, l * 2 + 1)
                nc.scalar.activation(root[:, :], dev[:, 0, :], ACT.Sqrt).then_inc(root_ready, 1)
                act.wait_ge(norm_ready, l * 2 + 1)

                def left2(c, at, w):
                    act.wait_ge(h2_done, l * NCH + (c + 1))
                    nc.scalar.activation(h2[:, at:at + w], small[0:H, c % 2, 0:w], ACT.Identity, bias=vec[:, 3:4]).then_inc(h2_left, 1)

                for c, at, w in spans:
                    nc.scalar.activation(h1[:, at:at + w], h1[:, at:at + w], ACT.Relu, bias=shift[:, 0, :], scale=scale[:, 0, :]).then_inc(relu1, 1)
                    if c >= 1:
                        left2(*spans[c - 1])
                left2(*spans[NCH - 1])
                act.wait_ge(var_ready, l * 2 + 2)
                nc.scalar.activation(root[:, :], dev[:, 1, :], ACT.Sqrt).then_inc(root_ready, 1)
                act.wait_ge(norm_ready, l * 2 + 2)
                for c, at, w in spans:
                    nc.scalar.activation(h2[:, at:at + w], h2[:, at:at + w], ACT.Relu, bias=shift[:, 1, :], scale=scale[:, 1, :]).then_inc(relu2, 1)

        @block.vector
        def _(dve):
            ch = Chain(dve, chain)
            with layers(dve) as l:
                own = l if fast else layer
                ch.base, ch.n = l * LAYER_STEPS, 0
                dve.wait_ge(xt_ready, l * NCH + NCH)
                dve.nop(nofuse=True)
                nc.vector.tensor_copy(w1c[:, :], keep.w1t[:, bass.ds(own * H, H)]).then_inc(chain, 1)
                nc.vector.tensor_scalar(gain[:, :], keep.eps[:, bass.ds(own, 1)], 1.0, None, ALU.add).then_inc(chain, 1)
                for i, a in enumerate((keep.b1, keep.g1, keep.bt1, keep.b2, keep.g2, keep.bt2)):
                    nc.vector.tensor_copy(vec[:, i:i + 1], a[:, bass.ds(own, 1)])
                nc.vector.tensor_copy(b3c[:, :], keep.b3[:, bass.ds(own, 1)])
                nc.vector.tensor_copy(w2c[:, :], keep.w2t[:, bass.ds(own, 1), :].rearrange("p l o -> p (l o)"))
                nc.vector.tensor_copy(w3c[:, :], keep.w3t[:, bass.ds(own, 1), :].rearrange("p l o -> p (l o)")).then_inc(chain, 1)
                ch.n += 3
                dve.wait_ge(chain, ch.base + ch.n)
                nc.vector.tensor_scalar(w1e[:, :], w1c[:, :], gain[:, 0:1], None, ALU.mult).then_inc(cur_ready, 1)
                for q, (b0, n) in enumerate(yb if fast else ()):
                    dve.wait_ge(y_done, l * 2 + (q + 1))
                    y = yps[:, q, 0:n * H].rearrange("p (b h) -> p b h", h=H)
                    r = rest[:, 0:n * H].rearrange("p (b h) -> p b h", h=H)
                    part = [parts[:, b0:b0 + n, s, :] for s in range(3)]
                    ch.step(nc.vector.tensor_copy(part[0], y))
                    ch.step(nc.vector.tensor_tensor(r, y, part[0], ALU.subtract))
                    ch.step(nc.vector.tensor_copy(part[1], r))
                    ch.step(nc.vector.tensor_tensor(r, r, part[1], ALU.subtract))
                    nc.vector.tensor_copy(part[2], r).then_inc(parts_ready, 1)

                def statistics(h, c, at, w):
                    w = min(w, N - at)
                    return nc.vector.bn_stats(stats[:, c, :], h[:, at:at + w])

                def norm(i):
                    ch.step(nc.vector.bn_aggr(mv[:, :], stats[:, :, :].rearrange("p c s -> p (c s)")))
                    nc.vector.tensor_scalar(dev[:, i, :], mv[:, 1:2], EPS, None, ALU.add).then_inc(var_ready, 1)
                    dve.wait_ge(root_ready, l * 2 + (i + 1))
                    ch.step(nc.vector.reciprocal(root[:, :], root[:, :]))
                    ch.step(nc.vector.tensor_tensor(scale[:, i, :], root[:, :], vec[:, 3 * i + 1:3 * i + 2], ALU.mult))
                    ch.step(nc.vector.tensor_tensor(mv[:, 0:1], mv[:, 0:1], scale[:, i, :], ALU.mult))
                    nc.vector.tensor_tensor(shift[:, i, :], vec[:, 3 * i + 2:3 * i + 3], mv[:, 0:1], ALU.subtract).then_inc(norm_ready, 1)

                for c, at, w in spans:
                    for x in range(c * WC // NCH, (c + 1) * WC // NCH) if fast else ():
                        last = nc.vector.tensor_scalar(junk[:, x - c * WC // NCH, :], keep.dkey[:, bass.ds(l, 1), :].rearrange("p g e -> p (g e)"), float(x + 1), None,
                                                       ALU.is_equal, ALU.add, accum_out=keep.deg[:, bass.ds(l * WC + x, 1)])
                    if fast:
                        ch.step(last)
                    dve.wait_ge(h1_left, l * NCH + (c + 1))
                    last = statistics(h1, c, at, w)
                ch.step(last)
                norm(0)
                for c, at, w in spans:
                    dve.wait_ge(h2_left, l * NCH + (c + 1))
                    last = statistics(h2, c, at, w)
                ch.step(last)
                norm(1)
                for c, at, w in spans:
                    dve.wait_ge(x_done, l * NCH + (c + 1))
                    nc.vector.tensor_scalar(keep.xt[:, at:at + w], big[:, c % 2, 0:w], b3c[:, 0:1], None, ALU.add).then_inc(xt_ready, 1)
                assert ch.n == LAYER_STEPS or not fast, ch.n


LAYER_STEPS = 3 + 8 + NCH + 2 * 5
SLICE = NU * NB * UD // (L * NCH)
assert SLICE * L * NCH == NU * NB * UD


def normalise(nc, keep, out, name):
    with ExitStack() as ctx:
        m = Memory(nc, ctx, name)
        stats = m.sb("n_stats", [P, NB, 6], F32)
        mv = m.sb("n_mv", [P, NB, 2], F32)
        root = m.sb("n_root", [P, NB], F32)
        ps = m.ps("n_ps", [P, 2, 512])
        ps2 = m.ps("n_ps2", [P, 2, 512])
        degs = m.ps("n_degs", [T, 2, 512])
        turned = m.sem("n_turned")
        added = m.sem("n_added")
        eps_added = m.sem("n_eps_added")
        rooted = m.sem("n_rooted")
        normed = m.sem("n_normed")
        back = m.sem("n_back")
        back_left = m.sem("n_back_left")
        hi_ready = m.sem("n_hi_ready")
        stored = m.sem("n_stored")
        deg_turned = m.sem("n_deg_turned")
        deg_left = m.sem("n_deg_left")
        chain = m.sem("n_chain")
        block = ctx.enter_context(nc.Block())
        groups = node_groups()

        @block.tensor
        def _(pe):
            for q, b0, n in groups:
                if q >= 2:
                    pe.wait_ge(added, q - 1)
                for i in range(n):
                    last = nc.tensor.transpose(ps[:, q % 2, i * P:(i + 1) * P], keep.xt[:, (b0 + i) * P:(b0 + i + 1) * P], keep.ident[:, :])
                last.then_inc(turned, 1)
            if out is None:
                for d in range(WD):
                    if d >= 2:
                        pe.wait_ge(deg_left, d - 1)
                    for g in range(NWG):
                        seen = keep.deg[:, g * WC:(g + 1) * WC].rearrange("p (t d) -> p t d", d=WD)[:, :, d]
                        last = nc.tensor.transpose(degs[:, d % 2, g * P:(g + 1) * P], seen, keep.ident[:, :])
                    last.then_inc(deg_turned, 1)
                for q, b0, n in groups:
                    pe.wait_ge(normed, q + 1)
                    if q >= 2:
                        pe.wait_ge(back_left, q - 1)
                    for i in range(n):
                        last = nc.tensor.transpose(ps2[:, q % 2, i * P:(i + 1) * P], keep.x_nm[:, b0 + i, :], keep.ident[:, :])
                    last.then_inc(back, 1)

        @block.vector
        def _(dve):
            ch = Chain(dve, chain)
            for q, b0, n in groups:
                dve.wait_ge(turned, q + 1)
                x = keep.x_nm[:, b0:b0 + n, :].rearrange("p b d -> p (b d)")
                nc.vector.tensor_tensor(x, ps[:, q % 2, 0:n * P], x, ALU.add).then_inc(added, 1)
                dve.wait_ge(added, q + 1)
                for b in range(b0, b0 + n):
                    last = nc.vector.bn_stats(stats[:, b, :], keep.x_nm[:, b, :])
                ch.step(last)
                for b in range(b0, b0 + n):
                    last = nc.vector.bn_aggr(mv[:, b, :], stats[:, b, :])
            ch.step(last)
            nc.vector.tensor_scalar(root[:, :], mv[:, :, 1], EPS, None, ALU.add).then_inc(eps_added, 1)
            dve.wait_ge(rooted, 1)
            ch.step(nc.vector.reciprocal(root[:, :], root[:, :]))
            for q, b0, n in groups:
                for b in range(b0, b0 + n):
                    last = nc.vector.tensor_scalar(keep.x_nm[:, b, :], keep.x_nm[:, b, :], mv[:, b, 0:1], root[:, b:b + 1],
                                                   ALU.subtract, ALU.mult)
                last.then_inc(normed, 1)
            if out is None:
                for d in range(WD):
                    dve.wait_ge(deg_turned, d + 1)
                    row = keep.deg_row[:, :].rearrange("t (w d) -> t w d", d=WD)[:, :, d]
                    nc.vector.tensor_copy(row, degs[:, d % 2, :]).then_inc(deg_left, 1)
                for q, b0, n in groups:
                    dve.wait_ge(hi_ready, q + 1)
                    nc.vector.scalar_tensor_tensor(out=keep.halves[:, 0, b0:b0 + n, 1, :], in0=keep.x_nm[:, b0:b0 + n, :], scalar=SPLIT,
                                                   in1=keep.halves[:, 0, b0:b0 + n, 0, :], op0=ALU.mult, op1=ALU.subtract)

        @block.scalar
        def _(act):
            act.wait_ge(eps_added, 1)
            nc.scalar.activation(root[:, :], root[:, :], ACT.Sqrt).then_inc(rooted, 1)
            if out is None:
                for q, b0, n in groups:
                    act.wait_ge(normed, q + 1)
                    nc.scalar.activation(keep.halves[:, 0, b0:b0 + n, 0, :], keep.x_nm[:, b0:b0 + n, :], ACT.Copy, scale=SPLIT).then_inc(hi_ready, 1)
                for q, b0, n in groups:
                    act.wait_ge(back, q + 1)
                    nc.scalar.activation(keep.xt[:, b0 * P:(b0 + n) * P], ps2[:, q % 2, 0:n * P], ACT.Copy).then_inc(back_left, 1)

        @block.sync
        def _(sp):
            if out is not None:
                sp.wait_ge(normed, len(groups))
                sp.dma_start(out[0:(NB - 1) * P, :].rearrange("(b p) d -> p b d", p=P), keep.x_nm[:, 0:NB - 1, :]).then_inc(stored, 16)
                sp.dma_start(out[(NB - 1) * P:N, :], keep.x_nm[0:LAST, NB - 1, :]).then_inc(stored, 16)
                sp.wait_ge(stored, 32)


FULL = 4
REST = -(-(NB - FULL * CH // P) // (NCH - FULL)) * P


def chunk_at(c):
    if not isinstance(c, int) or c < FULL:
        return c * CH, CH
    at = FULL * CH + (c - FULL) * REST
    return at, min(REST, NPAD - at)


assert sum(chunk_at(c)[1] for c in range(NCH)) == NPAD


def second_network(nc, keep, scratch):
    with ExitStack() as ctx:
        m = Memory(nc, ctx)
        ring = m.sb("ring", [P, T, UPC, NB * UD // 4], F32)
        ring8 = ring[:, :, :, :].rearrange("p t u f -> p (t u f)").bitcast(F8).rearrange(
            "p (t u b d) -> p t u b d", t=T, u=UPC, b=NB)
        near = m.sb("near", [D, T, CH], F32)
        a_bias = m.sb("a_bias", [D, NPAD], F32)
        a_sb = m.sb("a_sb", [D, CH], F32)
        r_sb = m.sb("r_sb", [D, CH], F32)
        z_sb = m.sb("z_sb", [D, CH], F32)
        n_sb = m.sb("n_sb", [D, CH], F32)
        u_sb = m.sb("u_sb", [D, CH], F32)
        h_new = m.sb("h_new", [D, CH], F32)
        b_rz = m.sb("b_rz", [D, 2], F32)
        near_ps = m.ps("near_ps", [D, 2, CH])
        a_ps = m.ps("a_ps", [D, CH])
        rz_ps = m.ps("rz_ps", [D, 2, CH])
        in_ps = m.ps("in_ps", [D, CH])
        hn_ps = m.ps("hn_ps", [D, CH])
        t_ps = m.ps("t_ps", [P, CH])

        tile_in = [m.sem(f"tile_in{t}") for t in range(T)]
        bias_done = m.sem("bias_done")
        bias_left = m.sem("bias_left")
        tile_done = m.sem("tile_done")
        near_left = m.sem("near_left")
        a_done = m.sem("a_done")
        a_left = m.sem("a_left")
        gates_done = m.sem("gates_done")
        rz_done = m.sem("rz_done")
        cand_done = m.sem("cand_done")
        n_done = m.sem("n_done")
        h_done = m.sem("h_done")
        t_done = m.sem("t_done")
        hi_done = m.sem("hi_done")
        lo_done = m.sem("lo_done")
        chain = m.sem("l1_chain")
        bias_ready = m.sem("bias_ready")
        block = ctx.enter_context(nc.Block())

        def steps(eng, chunk):
            with eng.Fori(0, STEPS, 2) as s0:
                for parity in range(2):
                    s = s0 + parity
                    chunk(s, 0, parity)
                    with eng.Fori(1, FULL, 1) as c:
                        chunk(s, c, parity)
                    for c in range(FULL, NCH):
                        chunk(s, c, parity)

        def steps_and_tails(eng, chunk, tail):
            def both(s, c, parity):
                k = s * NCH + c
                if not isinstance(c, int) or c:
                    chunk(s, c, parity, lambda i: tail(i, k - 1, c - 1, parity))
                elif parity:
                    chunk(s, c, parity, lambda i: tail(i, k - 1, NCH - 1, 1 - parity))
                else:
                    def guarded(i):
                        with eng.If(s > 0):
                            tail(i, k - 1, NCH - 1, 1 - parity)
                    chunk(s, c, parity, guarded)

            steps(eng, both)

        def cols(c):
            at, w = chunk_at(c)
            return slice(at, at + w) if isinstance(c, int) else bass.ds(at, w)

        def half(parity, c, i):
            at, w = chunk_at(c)
            nb = -(-w // P)
            return keep.halves[:, parity, bass.ds(c * (CH // P), nb), i, :] if not isinstance(c, int) else \
                keep.halves[:, parity, at // P:at // P + nb, i, :]

        @block.sync
        def _(sp):
            def chunk(s, c, parity):
                k = s * NCH + c
                for t in range(T):
                    sp.wait_ge(tile_done, k * T + (t + 1))
                    sp.nop(nofuse=True)
                    at, w = chunk_at(c)
                    of = scratch.adj[at // UD:(at + w) // UD, :, :] if isinstance(c, int) else scratch.adj[bass.ds(c * UPC, UPC), :, :]
                    sp.dma_start(ring[:, t, 0:w // UD, :], of[:, :, t * NB * UD // 4:(t + 1) * NB * UD // 4].rearrange("u p f -> p u f")
                                 ).then_inc(tile_in[t], 16)

            steps(sp, chunk)

        @block.tensor
        def _(pe):
            pe.sem_inc(tile_done, T)
            pe.sem_inc(a_done, 1)
            pe.sem_inc(gates_done, 1)
            pe.sem_inc(t_done, 1)
            pe.wait_ge(bias_ready, 1)
            for i in range(NCH):
                if i >= 2:
                    pe.wait_ge(bias_left, i - 1)
                w = chunk_width(i)
                nc.tensor.matmul(rz_ps[:, i % 2, 0:w], keep.b_edge[:, :], keep.deg_row[:, i * CH:i * CH + w], start=True, stop=True
                                 ).then_inc(bias_done, 1)
            pe.wait_ge(bias_left, NCH)

            def messages(k, c, parity):
                w = chunk_at(c)[1]
                pe.wait_ge(near_left, k * T + (T + 2))
                pe.wait_ge(a_left, k + 1)
                for t in range(T):
                    last = nc.tensor.matmul(a_ps[:, 0:w], keep.wet[:, t, :], near[:, t, 0:w], start=(t == 0), stop=(t == T - 1))
                last.then_inc(a_done, 1)

            def gates(k, c, parity):
                w = chunk_at(c)[1]
                pe.wait_ge(a_left, k + 2)
                pe.wait_ge(n_done, k + 1)
                h = keep.xt[:, cols(c)]
                for g in range(2):
                    nc.tensor.matmul(rz_ps[:, g, 0:w], keep.wht[:, g, :], h, start=True, stop=False)
                    nc.tensor.matmul(rz_ps[:, g, 0:w], keep.wit[:, g, :], a_sb[:, 0:w], start=False, stop=True)
                nc.tensor.matmul(hn_ps[:, 0:w], keep.wht[:, 2, :], h, start=True, stop=True)
                nc.tensor.matmul(in_ps[:, 0:w], keep.wit[:, 2, :], a_sb[:, 0:w], start=True, stop=True).then_inc(gates_done, 1)

            def turn(k, c, parity):
                w = chunk_at(c)[1]
                pe.wait_ge(h_done, k + 2)
                pe.wait_ge(hi_done, k + NCH)
                pe.wait_ge(lo_done, k + NCH)
                for i in range(-(-w // P)):
                    last = nc.tensor.transpose(t_ps[:, i * P:(i + 1) * P], h_new[:, i * P:(i + 1) * P], keep.ident[:, :])
                last.then_inc(t_done, 1)

            def tail(i, k, c, parity):
                (messages, gates, turn)[i](k, c, parity)

            def chunk(s, c, parity, tail):
                k = s * NCH + c
                w = chunk_at(c)[1]

                def tile(t, b0=0, b1=NB):
                    if b0 == 0:
                        pe.wait_ge(tile_in[t], k * 16 + 16)
                        pe.wait_ge(near_left, k * T + (t + 1))
                        pe.nop(nofuse=True)
                    for b in range(b0, b1):
                        if b in turned_at and isinstance(c, int) and c == 0:
                            pe.wait_ge(hi_done, s * NCH + (turned_at[b] + 1))
                            pe.wait_ge(lo_done, s * NCH + (turned_at[b] + 1))
                            pe.nop(nofuse=True)
                        for i in range(2):
                            last = nc.tensor.matmul(near_ps[:, t % 2, 0:w], keep.halves[:, parity, b, i, :],
                                                    ring8[:, t, 0:w // UD, b, :], start=(b == 0 and i == 0),
                                                    stop=(b == NB - 1 and i == 1))
                    if b1 == NB:
                        last.then_inc(tile_done, 1)

                if isinstance(c, int) and c == 0:
                    known = chunk_at(NCH - 1)[0] // P
                    tile(0, 0, 4)
                    tail(0)
                    tile(0, 4, 12)
                    tail(1)
                    tile(0, 12, known)
                    tile(1, 0, known - 6)
                    tail(2)
                    tile(1, known - 6, known)
                    tile(0, known)
                    tile(1, known)
                    tile(2)
                    tile(3)
                else:
                    for t in range(T):
                        tile(t)
                        if t < 3:
                            tail(t)

            turned_at = {chunk_at(c)[0] // P: c for c in range(NCH)}
            steps_and_tails(pe, chunk, tail)
            messages(STEPS * NCH - 1, NCH - 1, 1)
            gates(STEPS * NCH - 1, NCH - 1, 1)

        @block.scalar
        def _(act):
            act.sem_inc(near_left, 2)
            act.sem_inc(n_done, 1)
            act.sem_inc(hi_done, NCH)
            act.sem_inc(rz_done, 1)
            act.wait_ge(bias_ready, 1)
            for i in range(NCH):
                w = chunk_width(i)
                act.wait_ge(bias_done, i + 1)
                nc.scalar.activation(a_bias[:, i * CH:i * CH + w], rz_ps[:, i % 2, 0:w], ACT.Copy).then_inc(bias_left, 1)

            def sums(k, t, w):
                act.wait_ge(tile_done, k * T + (T + t + 1))
                act.wait_ge(a_done, k + 1)
                nc.scalar.activation(near[:, t, 0:w], near_ps[:, t % 2, 0:w], ACT.Copy, scale=1.0 / SPLIT).then_inc(near_left, 1)

            def gates(k, c, parity):
                w = chunk_at(c)[1]
                act.wait_ge(gates_done, k + 2)
                act.wait_ge(h_done, k + 1)
                nc.scalar.activation(r_sb[:, 0:w], rz_ps[:, 0, 0:w], ACT.Sigmoid, bias=b_rz[:, 0:1]).then_inc(rz_done, 1)
                nc.scalar.activation(z_sb[:, 0:w], rz_ps[:, 1, 0:w], ACT.Sigmoid, bias=b_rz[:, 1:2])
                act.wait_ge(cand_done, k + 2)
                nc.scalar.activation(n_sb[:, 0:w], n_sb[:, 0:w], ACT.Tanh, bias=keep.b_ih[:, 2:3]).then_inc(n_done, 1)

            def turn(k, c, parity):
                nb = -(-chunk_at(c)[1] // P)
                act.wait_ge(t_done, k + 2)
                nc.scalar.activation(half(1 - parity, c, 0), t_ps[:, 0:nb * P].rearrange("p (b d) -> p b d", d=D), ACT.Copy, scale=SPLIT
                                     ).then_inc(hi_done, 1)

            def tail(i, k, c, parity):
                (gates, turn)[i](k, c, parity)

            def chunk(s, c, parity, tail):
                k = s * NCH + c
                w = chunk_at(c)[1]
                if isinstance(c, int) and c == 0:
                    tail(0)
                    tail(1)
                    for t in range(T):
                        sums(k, t, w)
                else:
                    sums(k, 0, w)
                    sums(k, 1, w)
                    tail(0)
                    sums(k, 2, w)
                    tail(1)
                    sums(k, 3, w)

            steps_and_tails(act, chunk, tail)
            gates(STEPS * NCH - 1, NCH - 1, 1)

        @block.vector
        def _(dve):
            dve.sem_inc(a_left, 1)
            dve.sem_inc(h_done, 1)
            dve.sem_inc(lo_done, NCH)
            nc.vector.tensor_tensor(b_rz[:, :], keep.b_ih[:, 0:2], keep.b_hh[:, 0:2], ALU.add)
            nc.vector.memset(h_new[:, :], 0.0).then_inc(bias_ready, 1)
            dve.wait_ge(bias_ready, 1)
            OWN = 4
            dve.sem_inc(chain, OWN)
            dve.sem_inc(cand_done, 1)

            def messages(k, c, parity):
                w = chunk_at(c)[1]
                dve.wait_ge(a_done, k + 2)
                dve.wait_ge(gates_done, k + 1)
                dve.nop(nofuse=True)
                nc.vector.tensor_tensor(a_sb[:, 0:w], a_ps[:, 0:w], a_bias[:, cols(c)], ALU.add).then_inc(a_left, 1)

            def unit(k, c, parity):
                w = chunk_at(c)[1]
                own = (k + 1) * OWN
                dve.wait_ge(rz_done, k + 2)
                nc.vector.scalar_tensor_tensor(out=u_sb[:, 0:w], in0=hn_ps[:, 0:w], scalar=keep.b_hh[:, 2:3], in1=r_sb[:, 0:w],
                                               op0=ALU.add, op1=ALU.mult).then_inc(chain, 1)
                dve.wait_ge(chain, own + 1)
                nc.vector.tensor_tensor(n_sb[:, 0:w], in_ps[:, 0:w], u_sb[:, 0:w], ALU.add).then_inc(cand_done, 1)
                dve.wait_ge(n_done, k + 2)
                h = keep.xt[:, cols(c)]
                nc.vector.tensor_tensor(u_sb[:, 0:w], h, n_sb[:, 0:w], ALU.subtract).then_inc(chain, 1)
                dve.wait_ge(chain, own + 2)
                nc.vector.tensor_tensor(u_sb[:, 0:w], u_sb[:, 0:w], z_sb[:, 0:w], ALU.mult).then_inc(chain, 1)
                dve.wait_ge(chain, own + 3)
                dve.wait_ge(t_done, k + 1)
                nc.vector.tensor_tensor(h_new[:, 0:w], u_sb[:, 0:w], n_sb[:, 0:w], ALU.add).then_inc(h_done, 1)
                dve.wait_ge(h_done, k + 2)
                dve.nop(nofuse=True)
                nc.vector.tensor_copy(keep.xt[:, cols(c)], h_new[:, 0:w]).then_inc(chain, 1)

            def turn(k, c, parity):
                nb = -(-chunk_at(c)[1] // P)
                dve.wait_ge(t_done, k + 2)
                dve.wait_ge(hi_done, k + (NCH + 1))
                nc.vector.scalar_tensor_tensor(out=half(1 - parity, c, 1), in0=t_ps[:, 0:nb * P].rearrange("p (b d) -> p b d", d=D), scalar=SPLIT,
                                               in1=half(1 - parity, c, 0), op0=ALU.mult, op1=ALU.subtract).then_inc(lo_done, 1)

            def tail(i, k, c, parity):
                messages(k, c, parity)
                unit(k, c, parity)
                turn(k, c, parity)

            dve.wait_ge(bias_left, NCH)
            steps_and_tails(dve, lambda s, c, parity, tail: tail(0), tail)
            messages(STEPS * NCH - 1, NCH - 1, 1)
            unit(STEPS * NCH - 1, NCH - 1, 1)




def verdict(nc, keep):
    with ExitStack() as ctx:
        m = Memory(nc, ctx, "verdict_")
        sums = m.sb("sums", [P, 2], F32)
        ones = m.sb("ones", [P, 1], F32)
        total = m.sb("total", [1, 4], F32)
        ps = m.ps("ps", [1, 2])
        ready = m.sem("ready")
        summed = m.sem("summed")
        chain = m.sem("chain")
        block = ctx.enter_context(nc.Block())

        @block.vector
        def _(dve):
            ch = Chain(dve, chain)
            nc.vector.memset(ones[:, :], 1.0)
            nc.vector.tensor_reduce(sums[:, 0:1], keep.deg[:, :], AX.X, ALU.add)
            nc.vector.tensor_reduce(sums[:, 1:2], keep.excess[:, :], AX.X, ALU.add).then_inc(ready, 1)
            dve.wait_ge(summed, 1)
            ch.step(nc.vector.tensor_copy(total[:, 0:2], ps[:, :]))
            ch.step(nc.vector.tensor_scalar(total[:, 2:3], total[:, 0:1], float(E), None, ALU.not_equal))
            ch.step(nc.vector.tensor_tensor(total[:, 3:4], total[:, 2:3], total[:, 1:2], ALU.add))
            ch.step(nc.vector.tensor_scalar(keep.amiss[:, :], total[:, 3:4], 0.0, None, ALU.is_gt))

        @block.tensor
        def _(pe):
            pe.wait_ge(ready, 1)
            nc.tensor.matmul(ps[:, :], ones[:, :], sums[:, :], start=True, stop=True).then_inc(summed, 1)


def reload(nc, ins, keep, scratch):
    with ExitStack() as ctx:
        m = Memory(nc, ctx, "reload_")
        fields = m.sb("fields", [EP, BPP, 4, EB], F32)
        sel_i = m.sb("sel_i", [T, T * P], I32)
        ps = m.ps("ps", [P, 2, 512])
        loaded = m.sem("loaded")
        cleared = m.sem("cleared")
        turned = m.sem("turned")
        left = m.sem("left")
        chain = m.sem("chain")
        block = ctx.enter_context(nc.Block())

        @block.sync
        def _(sp):
            sp.wait_ge(cleared, 1)
            sp.dma_start(keep.x_nm[:, 0:NB - 1, :], ins["x"][0:(NB - 1) * P, :].rearrange("(b p) d -> p b d", p=P)).then_inc(loaded, 16)
            sp.dma_start(keep.x_nm[0:LAST, NB - 1, :], ins["x"][(NB - 1) * P:N, :]).then_inc(loaded, 16)
            sp.dma_start(fields[:, :, :, :].rearrange("p b a e -> p b (a e)"),
                         scratch.fields[0:NEB, :].rearrange("(p b) f -> p b f", p=EP)).then_inc(loaded, 16)

        @block.gpsimd
        def _(pool):
            nc.gpsimd.memset(keep.x_nm[:, NB - 1, :], 0.0).then_inc(cleared, 1)
            nc.gpsimd.iota(keep.nodes[:, :], [[1, NCOL]], base=0, channel_multiplier=0).then_inc(cleared, 1)
            nc.gpsimd.iota(sel_i[:, :], [[1, T * P]], base=0, channel_multiplier=-P).then_inc(cleared, 1)

        @block.vector
        def _(dve):
            ch = Chain(dve, chain)
            dve.wait_ge(loaded, 48)
            dve.wait_ge(cleared, 3)

            def blocks(a):
                return a.rearrange("p (b e) -> p b e", e=EB)

            dv = blocks(keep.edge_dst[:, :])
            nc.vector.tensor_copy(dv, fields[:, :, 0, :])
            ch.step(nc.vector.scalar_tensor_tensor(out=blocks(keep.node_f[:, :]), in0=fields[:, :, 1, :], scalar=float(P) / WD,
                                                   in1=fields[:, :, 3, :], op0=ALU.mult, op1=ALU.add))
            nc.vector.tensor_copy(keep.src_row[:, 0, :], keep.node_f[:, :])
            nc.vector.scalar_tensor_tensor(out=blocks(keep.src_row[:, 1, :]), in0=fields[:, :, 2, :], scalar=float(NCOL) / TYW,
                                           in1=blocks(keep.node_f[:, :]), op0=ALU.mult, op1=ALU.add)
            ch.step(nc.vector.tensor_scalar(keep.select[:, :], sel_i[:, :], 0.0, None, ALU.is_ge))
            ch.step(nc.vector.scalar_tensor_tensor(out=keep.select[:, :], in0=sel_i[:, :], scalar=float(P), in1=keep.select[:, :],
                                                   op0=ALU.is_lt, op1=ALU.mult))

        @block.tensor
        def _(pe):
            pe.wait_ge(loaded, 48)
            for q, b0, n in node_groups():
                if q >= 2:
                    pe.wait_ge(left, q - 1)
                for i in range(n):
                    last = nc.tensor.transpose(ps[:, q % 2, i * P:(i + 1) * P], keep.x_nm[:, b0 + i, :], keep.ident[:, :])
                last.then_inc(turned, 1)

        @block.scalar
        def _(act):
            for q, b0, n in node_groups():
                act.wait_ge(turned, q + 1)
                nc.scalar.activation(keep.xt[:, b0 * P:(b0 + n) * P], ps[:, q % 2, 0:n * P], ACT.Copy).then_inc(left, 1)


def gather_sums(nc, keep, scratch, typed):
    with ExitStack() as ctx:
        m = Memory(nc, ctx, "typed_" if typed else "plain_", again=True)
        table = m.sb("table", [P, NB, D], F32)
        ps = m.ps("ps", [P, 7, 512])
        made = m.sem("made")
        left = m.sem("left")
        stored = m.sem("stored")
        row = m.sb("row", [EP, 1], U32)
        message = m.sb("message", [EP, D], F32)
        hot = m.sb("hot", [EP, NCOL], F32)
        total = m.sb("total", [P, NB * D], F32)
        row_ready = m.sem("row_ready")
        hot_ready = m.sem("hot_ready")
        gathered = m.sem("gathered")
        multiplied = m.sem("multiplied")
        added = m.sem("added")
        types = T if typed else 1
        SLICES = len(node_groups())
        block = ctx.enter_context(nc.Block())

        @block.tensor
        def _(pe):
            for t in range(types):
                if t:
                    pe.wait_ge(left, SLICES * t)
                for q, b0, n in node_groups():
                    for i in range(n):
                        cell = ps[:, q, i * P:(i + 1) * P]
                        nodes = keep.xt[:, (b0 + i) * P:(b0 + i + 1) * P]
                        if typed:
                            nc.tensor.matmul(cell, nodes, keep.wet[:, t, :], start=True, stop=False)
                            last = nc.tensor.matmul(cell, keep.select[:, t * P:(t + 1) * P], keep.b_edge[:, :], start=False, stop=True)
                        else:
                            last = nc.tensor.transpose(cell, nodes, keep.ident[:, :])
                    last.then_inc(made, 1)
            pe.wait_ge(left, SLICES * types)
            with pe.Fori(0, EF, 1) as j:
                pe.wait_ge(gathered, j * 16 + 16)
                pe.nop(nofuse=True)
                pe.wait_ge(hot_ready, j + 1)
                pe.nop(nofuse=True)
                for b in range(NB):
                    last = nc.tensor.matmul(ps[:, b // 4, (b % 4) * D:(b % 4 + 1) * D], hot[:, b * P:(b + 1) * P], message[:, :],
                                            start=True, stop=True)
                last.then_inc(multiplied, 1)
            pe.wait_ge(added, (EF + 1))
            for q, b0, n in node_groups():
                for i in range(n):
                    last = nc.tensor.transpose(ps[:, q, i * P:(i + 1) * P], total[:, (b0 + i) * D:(b0 + i + 1) * D], keep.ident[:, :])
                last.then_inc(made, 1)

        @block.scalar
        def _(act):
            for t in range(types):
                if t:
                    act.wait_ge(stored, 16 * t)
                for q, b0, n in node_groups():
                    act.wait_ge(made, SLICES * t + q + 1)
                    nc.scalar.activation(table[:, b0:b0 + n, :].rearrange("p b d -> p (b d)"), ps[:, q, 0:n * D], ACT.Copy).then_inc(left, 1)
            for q, b0, n in node_groups():
                act.wait_ge(made, SLICES * types + q + 1)
                nc.scalar.activation(keep.st[:, b0 * P:(b0 + n) * P], ps[:, q, 0:n * P], ACT.Copy)

        @block.sync
        def _(sp):
            for t in range(types):
                sp.wait_ge(left, SLICES * (t + 1))
                sp.dma_start(scratch.table[t * NCOL:(t + 1) * NCOL, :].rearrange("(b p) d -> p b d", p=P), table[:, :, :]).then_inc(stored, 16)

        @block.gpsimd
        def _(pool):
            pool.wait_ge(stored, 16 * types)
            with pool.Fori(0, EF, 1) as j:
                pool.wait_ge(row_ready, j + 1)
                pool.nop(nofuse=True)
                nc.gpsimd.indirect_dma_start(message[:, :], None, scratch.table[0:types * NCOL, :],
                                             bass.IndirectOffsetOnAxis(ap=row[:, :], axis=0)).then_inc(gathered, 16)

        @block.vector
        def _(dve):
            nc.vector.memset(total[:, :], 0.0).then_inc(added, 1)
            with dve.Fori(0, EF, 1) as j:
                dve.wait_ge(added, j + 1)
                dve.nop(nofuse=True)
                nc.vector.tensor_copy(row[:, :], keep.src_row[:, 1 if typed else 0, bass.ds(j, 1)]).then_inc(row_ready, 1)
                nc.vector.tensor_scalar(hot[:, :], keep.nodes[0:EP, :], keep.edge_dst[:, bass.ds(j, 1)], None, ALU.is_equal).then_inc(hot_ready, 1)
                dve.wait_ge(multiplied, j + 1)
                dve.nop(nofuse=True)
                for q, b0, n in node_groups():
                    s = total[:, b0 * D:(b0 + n) * D]
                    last = nc.vector.tensor_tensor(s, ps[:, q, 0:n * D], s, ALU.add)
                last.then_inc(added, 1)


def gated_unit(nc, keep):
    with ExitStack() as ctx:
        m = Memory(nc, ctx, "unit_", again=True)
        r = m.sb("r", [D, CH], F32)
        z = m.sb("z", [D, CH], F32)
        n = m.sb("n", [D, CH], F32)
        u = m.sb("u", [D, CH], F32)
        b_rz = m.sb("b_rz", [D, 2], F32)
        rz_ps = m.ps("rz_ps", [D, 2, CH])
        in_ps = m.ps("in_ps", [D, CH])
        hn_ps = m.ps("hn_ps", [D, CH])
        gates = m.sem("gates")
        bias_ready = m.sem("bias_ready")
        rz = m.sem("rz")
        cand = m.sem("cand")
        act_n = m.sem("act_n")
        h_done = m.sem("h_done")
        chain = m.sem("chain")
        block = ctx.enter_context(nc.Block())

        @block.tensor
        def _(pe):
            for c in range(NCH):
                w = chunk_width(c)
                h, a = keep.xt[:, c * CH:c * CH + w], keep.st[:, c * CH:c * CH + w]
                if c:
                    pe.wait_ge(h_done, c)
                for g in range(2):
                    nc.tensor.matmul(rz_ps[:, g, 0:w], keep.wht[:, g, :], h, start=True, stop=False)
                    nc.tensor.matmul(rz_ps[:, g, 0:w], keep.wit[:, g, :], a, start=False, stop=True)
                nc.tensor.matmul(hn_ps[:, 0:w], keep.wht[:, 2, :], h, start=True, stop=True)
                nc.tensor.matmul(in_ps[:, 0:w], keep.wit[:, 2, :], a, start=True, stop=True).then_inc(gates, 1)

        @block.scalar
        def _(act):
            act.wait_ge(bias_ready, 1)
            for c in range(NCH):
                w = chunk_width(c)
                act.wait_ge(gates, c + 1)
                nc.scalar.activation(r[:, 0:w], rz_ps[:, 0, 0:w], ACT.Sigmoid, bias=b_rz[:, 0:1])
                nc.scalar.activation(z[:, 0:w], rz_ps[:, 1, 0:w], ACT.Sigmoid, bias=b_rz[:, 1:2]).then_inc(rz, 1)
                act.wait_ge(cand, c + 1)
                nc.scalar.activation(n[:, 0:w], n[:, 0:w], ACT.Tanh, bias=keep.b_ih[:, 2:3]).then_inc(act_n, 1)

        @block.vector
        def _(dve):
            ch = Chain(dve, chain)
            nc.vector.tensor_tensor(b_rz[:, :], keep.b_ih[:, 0:2], keep.b_hh[:, 0:2], ALU.add).then_inc(bias_ready, 1)
            for c in range(NCH):
                w = chunk_width(c)
                h = keep.xt[:, c * CH:c * CH + w]
                dve.wait_ge(rz, c + 1)
                ch.step(nc.vector.scalar_tensor_tensor(out=u[:, 0:w], in0=hn_ps[:, 0:w], scalar=keep.b_hh[:, 2:3], in1=r[:, 0:w],
                                                       op0=ALU.add, op1=ALU.mult))
                nc.vector.tensor_tensor(n[:, 0:w], in_ps[:, 0:w], u[:, 0:w], ALU.add).then_inc(cand, 1)
                dve.wait_ge(act_n, c + 1)
                ch.step(nc.vector.tensor_tensor(u[:, 0:w], h, n[:, 0:w], ALU.subtract))
                ch.step(nc.vector.tensor_tensor(u[:, 0:w], u[:, 0:w], z[:, 0:w], ALU.mult))
                nc.vector.tensor_tensor(h, u[:, 0:w], n[:, 0:w], ALU.add).then_inc(h_done, 1)


def general(nc, ins, keep, scratch, out):
    with ExitStack() as ctx:
        m = Memory(nc, ctx, "general_")
        keep.nodes = m.sb("nodes", [P, NCOL], I32)
        keep.edge_dst = m.sb("edge_dst", [EP, EF], F32)
        keep.node_f = m.sb("node_f", [EP, EF], F32)
        keep.src_row = m.sb("src_row", [EP, 2, EF], U32)
        keep.select = m.sb("select", [T, T * P], F32)
        keep.st = m.sb("st", [D, NCOL], F32)
        reload(nc, ins, keep, scratch)
        with nc.Fori(0, L, 1) as l:
            gather_sums(nc, keep, scratch, False)
            first_network(nc, keep, l)
        normalise(nc, keep, None, "general_middle_")
        with nc.Fori(0, STEPS, 1) as s:
            gather_sums(nc, keep, scratch, True)
            gated_unit(nc, keep)
        normalise(nc, keep, out, "general_end_")


class Kept:

    def __init__(self, m):
        self.ident = m.sb("ident", [P, P], F32)
        self.ident16 = m.sb("ident16", [P, P], BF16)
        self.sum3 = m.sb("sum3", [3 * H, H], F32)
        self.iota = m.sb("iota", [P, T * TYW], F16)
        self.iota1 = m.sb("iota1", [P, P], F16)
        self.w1t = m.sb("w1t", [D, L * H], F32)
        self.w2t = m.sb("w2t", [H, L, H], F32)
        self.w3t = m.sb("w3t", [H, L, D], F32)
        self.wet = m.sb("wet", [D, T, D], F32)
        self.wit = m.sb("wit", [D, 3, D], F32)
        self.wht = m.sb("wht", [D, 3, D], F32)
        self.b_edge = m.sb("b_edge", [T, D], F32)
        self.b_ih = m.sb("b_ih", [D, 3], F32)
        self.b_hh = m.sb("b_hh", [D, 3], F32)
        self.eps = m.sb("eps", [P, L], F32)
        self.b1 = m.sb("b1", [H, L], F32)
        self.g1 = m.sb("g1", [H, L], F32)
        self.bt1 = m.sb("bt1", [H, L], F32)
        self.b2 = m.sb("b2", [H, L], F32)
        self.g2 = m.sb("g2", [H, L], F32)
        self.bt2 = m.sb("bt2", [H, L], F32)
        self.b3 = m.sb("b3", [D, L], F32)
        self.x_nm = m.sb("x_nm", [P, NB, D], F32)
        self.xt = m.sb("xt", [D, NCOL], F32)
        self.fifteen = m.sb("fifteen", [P, 1], F32)
        self.amiss = m.sb("amiss", [1, 1], I32)
        self.deg = m.sb("deg", [P, NWG * WC], F32)
        self.excess = m.sb("excess_sum", [P, L * NCH], F32)


class Scratch:

    def __init__(self, nc):
        self.fields = nc.dram_tensor("edge_fields", (NEB + BPW - 1, 4 * EB), F32).ap()
        self.table = nc.dram_tensor("messages", (T * NCOL, D), F32).ap()
        self.adj = nc.dram_tensor("adjacency", (NU, P, T * NB * UD // 4), F32).ap()


def gnn(nc, ins, out):
    scratch = Scratch(nc)
    with ExitStack() as ctx:
        keep = Kept(Memory(nc, ctx))
        with ExitStack() as first:
            m = Memory(nc, first)
            keep.dkey = m.sb("dkey", [P, NWG, TPW * P], F32)
            keep.key = m.sb("key", [P, 2, TPW, NWG * P], F32)
            keep.row = m.sb("row", [P, NWG, BPW], U32)
            keep.w8 = m.sb("w8", [P, NWG], F32)
            prepare(nc, ins, keep, scratch)
            keep.adj_words = m.sb("adj", [P, NU, NB * UD // 4], F32)
            words = keep.adj_words[:, :, :].rearrange("p u f -> p (u f)")
            keep.adj = words.bitcast(F8).rearrange("p (u b d) -> p u b d", u=NU, b=NB)
            keep.adj_bytes = words.bitcast(mybir.dt.uint8)
            build(nc, keep, scratch)
            first_network(nc, keep)
        with ExitStack() as second:
            m = Memory(nc, second)
            keep.deg_row = m.sb("deg_row", [T, NWG * P * WD], F32)
            keep.halves = m.sb("halves", [P, 2, NB, 2, D], F16)
            normalise(nc, keep, None, "middle_")
            second_network(nc, keep, scratch)
            normalise(nc, keep, out, "end_")
            verdict(nc, keep)
            amiss = nc.values_load(keep.amiss[0:1, 0:1], min_val=0, max_val=1)
            with nc.If(amiss > 0):
                general(nc, ins, keep, scratch, out)


def kernel(**inputs):
    import numpy as np
    import concourse.bacc as _bacc
    from concourse.bass_utils import run_bass_kernel_spmd as _run

    nc = _bacc.Bacc("TRN2", target_bir_lowering=False, num_devices=1)
    arrays, aps = {}, {}
    for name, a in inputs.items():
        a = np.ascontiguousarray(a)
        arrays["in_" + name] = a
        aps[name] = nc.dram_tensor("in_" + name, a.shape, mybir.dt.from_np(a.dtype), kind="ExternalInput").ap()
    out = nc.dram_tensor("out", (N, D), F32, kind="ExternalOutput").ap()
    gnn(nc, aps, out)
    r = _run(nc, [arrays], core_ids=[0])
    return r.results[0]["out"]
```

```python
from contextlib import ExitStack

import concourse.bass as bass
from concourse import mybir

F32 = mybir.dt.float32
F16 = mybir.dt.float16
BF16 = mybir.dt.bfloat16
F8 = mybir.dt.float8e4
I32 = mybir.dt.int32
U32 = mybir.dt.uint32
ALU = mybir.AluOpType
ACT = mybir.ActivationFunctionType
AX = mybir.AxisListType

P = 128
N = 3125
E = 100000
D = 128
H = 32
L = 4
T = 4
STEPS = 4
EPS = 1e-5

NB = (N + P - 1) // P
LAST = N - (NB - 1) * P
UD = 64
NU = (N + UD - 1) // UD
NPAD = NU * UD
NCOL = NB * P
WD = 8
WPU = UD // WD
WC = T * WD
NWG = 4
TPW = 3
EB = 32
BPW = TPW * P // EB
NEB = E // EB
EP = 125
EF = E // EP
BPP = EF // EB
TYW = NB * WD
CH = 512
UPC = CH // UD
NCH = (NPAD + CH - 1) // CH
TAIL = NPAD - (NCH - 1) * CH
SPLIT = 1024.0
FIFTEEN = 0x57
assert NEB * EB == E and EP * EF == E and TAIL == UD and NCH * 4 >= NB and NB % 4 == 1


def chunk_width(c):
    return CH if not isinstance(c, int) or c < NCH - 1 else TAIL


class Memory:

    def __init__(self, nc, ctx, prefix="", again=False):
        self.nc, self.ctx, self.prefix, self.again, self.sems = nc, ctx, prefix, again, []
        if again:
            ctx.callback(self.clear)

    def sb(self, name, shape, dt):
        return self.ctx.enter_context(self.nc.sbuf_tensor(self.prefix + name, shape, dt))

    def ps(self, name, shape, dt=F32):
        return self.ctx.enter_context(self.nc.psum_tensor(self.prefix + name, shape, dt))

    def sem(self, name):
        if not self.again:
            return self.ctx.enter_context(self.nc.semaphore(self.prefix + name))
        self.sems.append(self.nc.alloc_semaphore(self.prefix + name))
        return self.sems[-1]

    def clear(self):
        self.nc.clear_and_free_semaphores(self.sems)
        self.nc.all_engine_barrier()


class Chain:

    def __init__(self, engine, sem):
        self.engine, self.sem, self.n, self.base = engine, sem, 0, 0

    def step(self, instruction):
        self.n += 1
        instruction.then_inc(self.sem, 1)
        self.engine.wait_ge(self.sem, self.base + self.n)
        if not isinstance(self.base, int):
            self.engine.nop(nofuse=True)


PIECES = [(0, 16, 0, 0), (16, NB - 17, 1, 16), (NB - 1, 1, 2, NB - 1)]


def split_piece(nc, ch, y_banks, rest, keep, i):
    b0, n, q, at = PIECES[i]
    y = y_banks[:, q, (b0 - at) * H:(b0 - at + n) * H].rearrange("p (b h) -> p b h", h=H)
    r = rest[:, 0:n * H].rearrange("p (b h) -> p b h", h=H)
    part = [keep.parts[:, b0:b0 + n, s, :] for s in range(3)]
    ch.step(nc.vector.tensor_copy(part[0], y))
    ch.step(nc.vector.tensor_tensor(r, y, part[0], ALU.subtract))
    ch.step(nc.vector.tensor_copy(part[1], r))
    ch.step(nc.vector.tensor_tensor(r, r, part[1], ALU.subtract))
    return nc.vector.tensor_copy(part[2], r)


def node_groups():
    return [(q, 4 * q, min(4, NB - 4 * q)) for q in range((NB + 3) // 4)]




def prepare(nc, ins, keep, scratch):
    with ExitStack() as ctx:
        m = Memory(nc, ctx)
        src_i = m.sb("src_i", [EP, EF], I32)
        dst_i = m.sb("dst_i", [EP, EF], I32)
        hi_i = m.sb("hi_i", [EP, EF], I32)
        lo_i = m.sb("lo_i", [EP, EF], I32)
        attr = m.sb("attr", [EP, EF, T], F32)
        dst_f = m.sb("dst_f", [EP, EF], F32)
        top01 = m.sb("top01", [EP, EF], F32)
        top = m.sb("top", [EP, EF], F32)
        not0 = m.sb("not0", [EP, EF], F32)
        not1 = m.sb("not1", [EP, EF], F32)
        not2 = top01
        fields = m.sb("fields", [EP, BPP, 4, EB], F32)
        filler = m.sb("filler", [BPW - 1, 4 * EB], F32)
        iota_i = m.sb("iota_i", [P, T * TYW], I32)
        thr = m.sb("thr", [EP, NWG * P], F16)
        below = m.sb("below", [EP, BPP, NWG * P], BF16)
        ones = m.sb("ones", [EP, 1], BF16)
        start = m.sb("start", [P, NWG], F32)
        step_i = m.sb("step_i", [P, NWG, BPW], I32)
        step_f = m.sb("step_f", [P, NWG, BPW], F32)
        w8_i = m.sb("w8_i", [P, NWG], I32)
        w1_raw = m.sb("w1_raw", [L * H, D], F32)
        w2_raw = m.sb("w2_raw", [H, L, H], F32)
        w3_raw = m.sb("w3_raw", [D, L, H], F32)
        we_raw = m.sb("we_raw", [D, T, D], F32)
        wi_raw = m.sb("wi_raw", [D, 3, D], F32)
        wh_raw = m.sb("wh_raw", [D, 3, D], F32)
        count_ps = m.ps("count_ps", [P, NWG])
        turn_ps = m.ps("turn_ps", [P, 2, 512])

        edges_in = m.sem("edges_in")
        weights_in = m.sem("weights_in")
        small_in = m.sem("small_in")
        iotas = m.sem("iotas")
        ident_set = m.sem("ident_set")
        dve_chain = m.sem("dve_chain")
        fields_ready = m.sem("fields_ready")
        filler_ready = m.sem("filler_ready")
        fields_out = m.sem("fields_out")
        compared = m.sem("compared")
        counted = m.sem("counted")
        turned = m.sem("turned")
        turned_out = m.sem("turned_out")
        block = ctx.enter_context(nc.Block())

        turns = [(w1_raw[:, :], keep.w1t[:, :])]
        turns += [(w2_raw[:, l, :], keep.w2t[:, l, :]) for l in range(L)]
        turns += [(w3_raw[:, l, :], keep.w3t[:, l, :]) for l in range(L)]
        turns += [(we_raw[:, t, :], keep.wet[:, t, :]) for t in range(T)]
        turns += [(wi_raw[:, g, :], keep.wit[:, g, :]) for g in range(3)]
        turns += [(wh_raw[:, g, :], keep.wht[:, g, :]) for g in range(3)]

        @block.sync
        def _(sp):
            sp.dma_start(dst_i[:, :], ins["dst"].rearrange("(p f) -> p f", p=EP)).then_inc(edges_in, 16)
            sp.dma_start(src_i[:, :], ins["src"].rearrange("(p f) -> p f", p=EP)).then_inc(edges_in, 16)
            sp.dma_start(attr[:, :, :], ins["edge_attr_4"].rearrange("(p f) t -> p f t", p=EP)).then_inc(edges_in, 16)
            sp.wait_ge(fields_ready, 1)
            sp.dma_start(scratch.fields[0:NEB, :].rearrange("(p b) f -> p b f", p=EP),
                         fields[:, :, :, :].rearrange("p b a e -> p b (a e)")).then_inc(fields_out, 16)
            sp.wait_ge(filler_ready, 1)
            sp.dma_start(scratch.fields[NEB:NEB + BPW - 1, :], filler[:, :]).then_inc(fields_out, 16)
            sp.wait_ge(fields_out, 32)

        @block.scalar
        def _(act):
            act.dma_start(w1_raw[:, :], ins["L0_gnn_W1"].rearrange("l h d -> (l h) d")).then_inc(weights_in, 16)
            act.dma_start(w2_raw[:, :, :], ins["L0_gnn_W2"].rearrange("l o i -> o l i")).then_inc(weights_in, 16)
            act.dma_start(w3_raw[:, :, :], ins["L0_gnn_W3"].rearrange("l o i -> o l i")).then_inc(weights_in, 16)
            act.dma_start(we_raw[:, :, :], ins["L1_gnn_W_edge"].rearrange("t o i -> o t i")).then_inc(weights_in, 16)
            act.dma_start(wi_raw[:, :, :], ins["L1_gnn_W_ih"].rearrange("(g o) i -> o g i", g=3)).then_inc(weights_in, 16)
            act.dma_start(wh_raw[:, :, :], ins["L1_gnn_W_hh"].rearrange("(g o) i -> o g i", g=3)).then_inc(weights_in, 16)
            small = [(keep.x_nm[:, 0:NB - 1, :], ins["x"][0:(NB - 1) * P, :].rearrange("(b p) d -> p b d", p=P)),
                     (keep.b_edge[:, :], ins["L1_gnn_b_edge"]),
                     (keep.b_ih[:, :], ins["L1_gnn_b_ih"].rearrange("(g o) -> o g", g=3)),
                     (keep.b_hh[:, :], ins["L1_gnn_b_hh"].rearrange("(g o) -> o g", g=3)),
                     (keep.eps[:, :], ins["L0_gnn_eps"].rearrange("(o l) -> o l", o=1).broadcast_to((P, L)))]
            for kept, name in ((keep.b1, "b1"), (keep.g1, "g1"), (keep.bt1, "bt1"),
                               (keep.b2, "b2"), (keep.g2, "g2"), (keep.bt2, "bt2"), (keep.b3, "b3")):
                small.append((kept[:, :], ins["L0_gnn_" + name].rearrange("l h -> h l")))
            for to, of in small:
                act.dma_start(to, of, allow_slow_non_contiguous=True).then_inc(small_in, 16)
            act.wait_ge(iotas, 1)
            act.dma_start(keep.x_nm[0:LAST, NB - 1, :], ins["x"][(NB - 1) * P:N, :]).then_inc(small_in, 16)
            for i, (raw, kept) in enumerate(turns):
                act.wait_ge(turned, i + 1)
                o, k = kept.shape[0], kept.shape[-1]
                nc.scalar.activation(kept, turn_ps[0:o, i % 2, 0:k], ACT.Copy).then_inc(turned_out, 1)
            act.wait_ge(small_in, 16 * (len(small) + 1))

        @block.gpsimd
        def _(pool):
            nc.gpsimd.memset(keep.x_nm[:, NB - 1, :], 0.0).then_inc(iotas, 1)
            nc.gpsimd.iota(w8_i[:, :], [[P * WD, NWG]], base=0, channel_multiplier=WD).then_inc(iotas, 1)
            nc.gpsimd.iota(step_i[:, :, :], [[0, NWG], [1, BPW]], base=0, channel_multiplier=0).then_inc(iotas, 1)
            nc.gpsimd.iota(iota_i[:, :], [[1, T * TYW]], base=0, channel_multiplier=0).then_inc(iotas, 1)
            nc.gpsimd.memset(keep.ident[:, :], 0.0).then_inc(ident_set, 1)
            nc.gpsimd.memset(keep.sum3[:, :], 0.0).then_inc(ident_set, 1)
            pool.wait_ge(ident_set, 2)
            nc.gpsimd.affine_select(out=keep.ident[:, :], in_=keep.ident[:, :], compare_op=ALU.not_equal, fill=1.0,
                                    base=0, pattern=[[-1, P]], channel_multiplier=1).then_inc(ident_set, 1)
            for s in range(3):
                pool.wait_ge(ident_set, 3 + s)
                nc.gpsimd.affine_select(out=keep.sum3[:, :], in_=keep.sum3[:, :], compare_op=ALU.not_equal, fill=1.0,
                                        base=-H * s, pattern=[[-1, H]], channel_multiplier=1).then_inc(ident_set, 1)

        @block.vector
        def _(dve):
            c = Chain(dve, dve_chain)
            nc.vector.memset(filler[:, :], -1.0).then_inc(filler_ready, 1)
            nc.vector.memset(keep.fifteen[:, :], -float(FIFTEEN))
            c.step(nc.vector.memset(ones[:, :], 1.0))
            dve.wait_ge(iotas, 4)
            nc.vector.tensor_scalar(thr[:, :], iota_i[0:EP, 0:NWG * P], float(WD), None, ALU.mult).then_inc(dve_chain, 1)
            nc.vector.tensor_copy(keep.iota[:, :], iota_i[:, :]).then_inc(dve_chain, 1)
            nc.vector.tensor_scalar(keep.iota1[:, :], iota_i[:, 0:P], 1.0, None, ALU.add).then_inc(dve_chain, 1)
            nc.vector.tensor_copy(step_f[:, :, :], step_i[:, :, :]).then_inc(dve_chain, 1)
            nc.vector.tensor_copy(keep.w8[:, :], w8_i[:, :]).then_inc(dve_chain, 1)
            c.n += 5
            dve.wait_ge(ident_set, 3)
            nc.vector.tensor_copy(keep.ident16[:, :], keep.ident[:, :])
            dve.wait_ge(edges_in, 48)
            c.step(nc.vector.tensor_copy(dst_f[:, :], dst_i[:, :]))
            for j in range(BPP):
                last = nc.vector.tensor_scalar(below[:, j, :], thr[:, :], dst_f[:, j * EB:j * EB + 1], None, ALU.is_gt)
            last.then_inc(compared, 1)
            nc.vector.tensor_tensor(top01[:, :], attr[:, :, 0], attr[:, :, 1], ALU.max).then_inc(dve_chain, 1)
            nc.vector.tensor_tensor(top[:, :], attr[:, :, 2], attr[:, :, 3], ALU.max).then_inc(dve_chain, 1)
            c.n += 2
            dve.wait_ge(dve_chain, c.n)
            c.step(nc.vector.tensor_tensor(top[:, :], top[:, :], top01[:, :], ALU.max))
            for i, (to) in enumerate((not0, not1, not2)):
                nc.vector.tensor_tensor(to[:, :], attr[:, :, i], top[:, :], ALU.not_equal).then_inc(dve_chain, 1)
            c.n += 3
            dve.wait_ge(dve_chain, c.n)
            c.step(nc.vector.scalar_tensor_tensor(out=not1[:, :], in0=not2[:, :], scalar=1.0, in1=not1[:, :], op0=ALU.add, op1=ALU.mult))
            c.step(nc.vector.scalar_tensor_tensor(out=not0[:, :], in0=not1[:, :], scalar=1.0, in1=not0[:, :], op0=ALU.add, op1=ALU.mult))
            nc.vector.tensor_scalar(hi_i[:, :], src_i[:, :], 7, None, ALU.arith_shift_right).then_inc(dve_chain, 1)
            nc.vector.tensor_scalar(lo_i[:, :], src_i[:, :], P - 1, None, ALU.bitwise_and).then_inc(dve_chain, 1)
            c.n += 2
            dve.wait_ge(dve_chain, c.n)

            def field(a):
                return fields[:, :, a, :]

            def blocks(a):
                return a[:, :].rearrange("p (b e) -> p b e", e=EB)

            nc.vector.tensor_copy(field(0), blocks(dst_f))
            nc.vector.tensor_scalar(field(1), blocks(hi_i), float(WD), None, ALU.mult)
            nc.vector.tensor_scalar(field(2), blocks(not0), float(TYW), None, ALU.mult)
            nc.vector.tensor_copy(field(3), blocks(lo_i)).then_inc(fields_ready, 1)
            dve.wait_ge(counted, 1)
            c.step(nc.vector.tensor_scalar(start[:, :], count_ps[:, :], -1.0, 0.0, ALU.add, ALU.max))
            for g in range(NWG):
                nc.vector.tensor_scalar(keep.row[:, g, :], step_f[:, g, :], start[:, g:g + 1], None, ALU.add)

        @block.tensor
        def _(pe):
            pe.wait_ge(ident_set, 3)
            pe.wait_ge(weights_in, 96)
            for i, (raw, kept) in enumerate(turns):
                if i >= 2:
                    pe.wait_ge(turned_out, i - 1)
                k, o = raw.shape[0], raw.shape[-1]
                nc.tensor.transpose(turn_ps[0:o, i % 2, 0:k], raw, keep.ident[0:k, 0:k]).then_inc(turned, 1)
            pe.wait_ge(compared, 1)
            for g in range(NWG):
                for j in range(BPP):
                    last = nc.tensor.matmul(count_ps[:, g:g + 1], below[:, j, g * P:(g + 1) * P], ones[:, :],
                                            start=(j == 0), stop=(j == BPP - 1))
            last.then_inc(counted, 1)


def build(nc, keep, scratch):
    R = 12
    QW = NB * UD // 4
    FG = P // WPU
    with ExitStack() as ctx:
        m = Memory(nc, ctx)
        got = m.sb("got", [P, NWG, BPW, 4 * EB], F32)
        dl = m.sb("dl", [P, BPW, EB], F32)
        inside = m.sb("inside", [P, BPW, EB], BF16)
        wkey = m.sb("wkey", [P, 2, NWG, BPW, EB], F32)
        which = m.sb("which", [P, R, P], BF16)
        where = m.sb("where", [P, R, T * TYW], BF16)
        unit = m.sb("unit", [P, 2, T, NB, UD], F8)
        unit_all = got[:, 0, :, :].rearrange("p b f -> p (b f)")[:, 0:2 * NB * UD // 4].bitcast(F8).rearrange("p (s b d) -> p s b d", s=2, b=NB)
        by_type = m.ps("by_type", [P, 2, 2, 512])
        sum_ps = m.ps("sum_ps", [P, 4, 512])

        rest = wkey[:, :, :, :, :].rearrange("p a g b e -> p (a g b e)")
        x_turned = m.sem("x_turned")
        x_left = m.sem("x_left")
        y_done = m.sem("y_done")
        parts_ready = m.sem("parts_ready")
        gathered = [m.sem(f"gathered{g}") for g in range(NWG)]
        key_chain = m.sem("key_chain")
        wkeys_ready = m.sem("wkeys_ready")
        keys_turned = m.sem("keys_turned")
        keys_out = m.sem("keys_out")
        hot = m.sem("hot")
        hot_free = m.sem("hot_free")
        window_free = m.sem("window_free")
        sum_done = m.sem("sum_done")
        sum_left = m.sem("sum_left")
        unit_out = [m.sem("unit_out0"), m.sem("unit_out1")]
        block = ctx.enter_context(nc.Block())
        V = WPU * TPW

        def units(engine, keys, unit_of):
            keys(0)
            with engine.Fori(0, FG, 2) as u:
                unit_of(u, 0)
                unit_of(u + 1, 1)
            for g in range(1, NWG):
                keys(g)
            with engine.Fori(FG, NU - 1, 2) as u:
                unit_of(u, 0)
                unit_of(u + 1, 1)
            unit_of(NU - 1, 0)

        @block.gpsimd
        def _(pool):
            for g in range(NWG):
                for k in range(BPW):
                    nc.gpsimd.indirect_dma_start(
                        got[:, g, k, :], None, scratch.fields,
                        bass.IndirectOffsetOnAxis(ap=keep.row[:, g, k:k + 1], axis=0)).then_inc(gathered[g], 16)

        @block.vector
        def _(dve):
            c = Chain(dve, key_chain)
            for i in range(3):
                dve.wait_ge(y_done, i + 1)
                split_piece(nc, c, sum_ps, rest, keep, i).then_inc(parts_ready, 1)
            dve.wait_ge(parts_ready, 3)

            def keys(g):
                dve.wait_ge(gathered[g], 16 * BPW)
                v = got[:, g, :, :].rearrange("p b (a e) -> p b a e", a=4)
                d, i, k = dl[:, :, :], inside[:, :, :], keep.dkey[:, g, :].rearrange("p (b e) -> p b e", e=EB)
                c.step(nc.vector.tensor_scalar(d, v[:, :, 0, :], keep.w8[:, g:g + 1], None, ALU.subtract))
                nc.vector.tensor_tensor(wkey[:, 1, g, :, :], v[:, :, 1, :], d, ALU.add).then_inc(key_chain, 1)
                nc.vector.tensor_scalar(i, d, 0.0, None, ALU.is_ge).then_inc(key_chain, 1)
                c.n += 2
                dve.wait_ge(key_chain, c.n)
                nc.vector.tensor_tensor(wkey[:, 1, g, :, :], wkey[:, 1, g, :, :], v[:, :, 2, :], ALU.add).then_inc(key_chain, 1)
                c.n += 1
                c.step(nc.vector.scalar_tensor_tensor(out=i, in0=d, scalar=float(WD), in1=i, op0=ALU.is_lt, op1=ALU.mult))
                nc.vector.scalar_tensor_tensor(out=wkey[:, 0, g, :, :], in0=v[:, :, 3, :], scalar=1.0, in1=i,
                                               op0=ALU.add, op1=ALU.mult).then_inc(wkeys_ready, 1)
                c.step(nc.vector.tensor_scalar(d, d, 1.0, None, ALU.add))
                c.step(nc.vector.scalar_tensor_tensor(out=k, in0=v[:, :, 2, :], scalar=float(WD) / TYW, in1=d,
                                                      op0=ALU.mult, op1=ALU.add))
                c.step(nc.vector.tensor_tensor(k, k, i, ALU.mult))
                if g in (0, NWG - 1):
                    dve.wait_ge(keys_out, 2 * (g + 1))

            def fill(u, parity):
                for i in range(WPU):
                    for j in range(TPW):
                        v = i * TPW + j
                        r = (parity * V + v) % R
                        dve.wait_ge(hot_free, (u * V + v) + 1)
                        w = u * WPU + i
                        nc.vector.tensor_scalar(which[:, r, :], keep.iota1[:, :], keep.key[:, 0, j, bass.ds(w, 1)], None, ALU.is_equal)
                        nc.vector.tensor_scalar(where[:, r, :], keep.iota[:, :], keep.key[:, 1, j, bass.ds(w, 1)], None,
                                                ALU.is_equal).then_inc(hot, 1)

            units(dve, keys, fill)

        @block.tensor
        def _(pe):
            pe.sem_inc(hot_free, R)
            for q, b0, n in node_groups():
                if q >= 2:
                    pe.wait_ge(x_left, q - 1)
                for i in range(n):
                    last = nc.tensor.transpose(by_type[:, q % 2, 0, i * P:(i + 1) * P], keep.x_nm[:, b0 + i, :], keep.ident[:, :])
                last.then_inc(x_turned, 1)
            for b0, n, q, at in PIECES:
                for b in range(b0, b0 + n):
                    if b % 4 == 0:
                        pe.wait_ge(x_left, b // 4 + 1)
                    last = nc.tensor.matmul(sum_ps[:, q, (b - at) * H:(b - at + 1) * H], keep.xt[:, b * P:(b + 1) * P], keep.w1t[:, 0:H],
                                            start=True, stop=True)
                last.then_inc(y_done, 1)
            pe.wait_ge(parts_ready, 3)

            def keys(g):
                if g:
                    pe.wait_ge(sum_left, 4 * FG + 4)
                pe.wait_ge(wkeys_ready, g + 1)
                for a in range(2):
                    for j in range(TPW):
                        seen = wkey[:, a, g, :, :].rearrange("p b e -> p (b e)")[:, j * P:(j + 1) * P]
                        last = nc.tensor.transpose(sum_ps[:, a, j * P:(j + 1) * P], seen, keep.ident[:, :])
                    last.then_inc(keys_turned, 1)
                pe.wait_ge(keys_out, 2 * (g + 1))

            def count(u, parity):
                for i in range(WPU):
                    pe.wait_ge(window_free, (u * WPU + i) + 1)
                    for j in range(TPW):
                        v = i * TPW + j
                        r = (parity * V + v) % R
                        pe.wait_ge(hot, (u * V + v) + 1)
                        for h in range(2):
                            last = nc.tensor.matmul(by_type[:, i % 2, h, 0:2 * TYW], which[:, r, :],
                                                    where[:, r, h * 2 * TYW:(h + 1) * 2 * TYW], start=(j == 0), stop=(j == TPW - 1))
                        last.then_inc(hot_free, 1)
                pe.wait_ge(sum_left, u * 4 + 4)
                pe.wait_ge(window_free, u * WPU + (WPU + 2))
                pe.nop(nofuse=True)
                for q in range(4):
                    for t in range(T):
                        of = unit[:, parity, t, :, :].rearrange("p b d -> p (b d)")[:, q * QW:(q + 1) * QW]
                        last = nc.tensor.matmul(sum_ps[:, q, 0:QW], keep.ident16[:, :], of, start=(t == 0), stop=(t == T - 1))
                    last.then_inc(sum_done, 1)

            units(pe, keys, count)

        @block.scalar
        def _(act):
            act.sem_inc(window_free, 2)
            act.sem_inc(sum_left, 4)
            act.sem_inc(unit_out[0], 32)
            act.sem_inc(unit_out[1], 32)
            for q, b0, n in node_groups():
                act.wait_ge(x_turned, q + 1)
                nc.scalar.activation(keep.xt[:, b0 * P:(b0 + n) * P], by_type[:, q % 2, 0, 0:n * P], ACT.Copy).then_inc(x_left, 1)

            def keys(g):
                for a in range(2):
                    act.wait_ge(keys_turned, 2 * g + a + 1)
                    nc.scalar.activation(keep.key[:, a, :, g * P:(g + 1) * P],
                                         sum_ps[:, a, 0:TPW * P].rearrange("p (j w) -> p j w", w=P), ACT.Copy).then_inc(keys_out, 1)

            def leave(u, parity):
                act.wait_ge(unit_out[parity], (u - parity) * 16 + 32)
                act.nop(nofuse=True)
                for i in range(WPU):
                    act.wait_ge(hot_free, (u * WPU + i) * TPW + TPW + R)
                    act.nop(nofuse=True)
                    for h in range(2):
                        to = unit[:, parity, 2 * h:2 * h + 2, :, i * WD:(i + 1) * WD].rearrange("p t b d -> p (t b) d")
                        last = nc.scalar.activation(to, by_type[:, i % 2, h, 0:2 * TYW].rearrange("p (a d) -> p a d", d=WD),
                                                    ACT.Copy, saturate=False)
                    last.then_inc(window_free, 1)
                for q in range(4):
                    act.wait_ge(sum_done, u * 4 + q + 1)
                    act.nop(nofuse=True)
                    nc.scalar.activation(unit_all[:, parity, :, :].rearrange("p b d -> p (b d)")[:, q * QW:(q + 1) * QW],
                                         sum_ps[:, q, 0:QW], ACT.Copy, saturate=False).then_inc(sum_left, 1)

            units(act, keys, leave)

        @block.sync
        def _(sp):
            def store(u, parity):
                sp.wait_ge(sum_left, u * 4 + 8)
                sp.nop(nofuse=True)
                sp.dma_start(scratch.adj[bass.ds(u, 1), :, :].rearrange("u p f -> p (u f)"),
                             unit[:, parity, :, :, :].rearrange("p t b d -> p (t b d)").bitcast(F32)).then_inc(unit_out[parity], 16)
                sp.dma_start(keep.adj_words[:, bass.ds(u, 1), :].rearrange("p u f -> p (u f)"),
                             unit_all[:, parity, :, :].rearrange("p b d -> p (b d)").bitcast(F32)).then_inc(unit_out[parity], 16)

            with sp.Fori(0, NU - 1, 2) as u:
                store(u, 0)
                store(u + 1, 1)
            store(NU - 1, 0)
            sp.wait_ge(unit_out[0], 32 * ((NU + 1) // 2 + 1))
            sp.wait_ge(unit_out[1], 32 * ((NU - 1) // 2 + 1))


def first_network(nc, keep, layer=None):
    fast = layer is None
    with ExitStack() as ctx:
        m = Memory(nc, ctx, "" if fast else "layer_", again=not fast)
        parts = keep.parts
        rest = m.sb("rest", [P, 16 * H], F32)
        summed = m.sb("summed", [3 * H, 2, CH], F32)
        h1 = m.sb("h1", [H, NPAD], F32)
        h2 = m.sb("h2", [H, NPAD], F32)
        w1c = m.sb("w1c", [D, H], F32)
        w1e = m.sb("w1e", [D, H], F32)
        w2c = m.sb("w2c", [H, H], F32)
        w3c = m.sb("w3c", [H, D], F32)
        vec = m.sb("vec", [H, 6], F32)
        b3c = m.sb("b3c", [D, 1], F32)
        gain = m.sb("gain", [P, 1], F32)
        stats = m.sb("stats", [H, NCH, 6], F32)
        mv = m.sb("mv", [H, 2], F32)
        dev = m.sb("dev", [H, 2, 1], F32)
        root = m.sb("root", [H, 1], F32)
        prime = m.sb("prime", [1, 1], F32)
        scale = m.sb("scale", [H, 2, 1], F32)
        shift = m.sb("shift", [H, 2, 1], F32)
        excess = m.sb("excess", [P, SLICE], BF16)
        junk = m.sb("junk", [P, -(-WC // (NCH - 1)), TPW * P], BF16)
        big = m.ps("big", [P, 2, 512])
        small = m.ps("small", [P, 2, 512])
        yps = m.ps("yps", [P, 3, 512])
        idle_ps = m.ps("idle_ps", [P, CH])

        cur_ready = m.sem("cur_ready")
        layer_ready = m.sem("layer_ready")
        xt_ready = m.sem("xt_ready")
        y_done = m.sem("y_done")
        parts_ready = m.sem("parts_ready")
        dense_done = m.sem("dense_done")
        sum_left = m.sem("sum_left")
        h1_done = m.sem("h1_done")
        h1_left = m.sem("h1_left")
        var_ready = m.sem("var_ready")
        root_ready = m.sem("root_ready")
        norm_ready = m.sem("norm_ready")
        primed = m.sem("primed")
        relu1 = m.sem("relu1")
        h2_done = m.sem("h2_done")
        h2_left = [m.sem("h2_left_even"), m.sem("h2_left_odd")]
        relu2 = m.sem("relu2")
        x_done = m.sem("x_done")
        excess_done = m.sem("excess_done")
        chain = m.sem("chain")
        block = ctx.enter_context(nc.Block())

        spans = [(c, c * CH, chunk_width(c)) for c in range(NCH)]

        LEFT = ((NCH + 1) // 2, NCH // 2)

        def layers(engine, layer_of):
            if fast:
                with engine.Fori(0, L - 1, 1) as l:
                    layer_of(l, False)
            layer_of(L - 1 if fast else 0, True)

        def with_before(spans):
            return zip(spans + [None], [None] + spans)


        @block.tensor
        def _(pe):
            def project(b0, n):
                for b in range(b0, b0 + n):
                    q, at = next((q, at) for p0, m, q, at in PIECES if p0 <= b < p0 + m)
                    last = nc.tensor.matmul(yps[:, q, (b - at) * H:(b - at + 1) * H], keep.xt[:, b * P:(b + 1) * P], w1c[:, :],
                                            start=True, stop=True)
                if any(b0 + n == p0 + m for p0, m, _, _ in PIECES):
                    last.then_inc(y_done, 1)

            def layer_of(l, is_last):
                pe.wait_ge(layer_ready, l + 1)
                pe.wait_ge(cur_ready, l + 1)
                if not fast:
                    pe.wait_ge(xt_ready, NCH)

                def keep_clock(products):
                    for _ in range(products if fast else 0):
                        nc.tensor.matmul(idle_ps[:, :], keep.ident16[:, :], keep.adj[:, 0:UPC, 0, :], start=True, stop=True)

                def perceptron_in(c, at, w):
                    if fast:
                        pe.wait_ge(sum_left, l * NCH + (c + 1))
                    if c >= 2:
                        pe.wait_ge(h1_left, l * NCH + (c - 1))
                    if fast:
                        nc.tensor.matmul(small[0:H, c % 2, 0:w], keep.sum3[:, :], summed[:, c % 2, 0:w], start=True, stop=False)
                    else:
                        nc.tensor.matmul(small[0:H, c % 2, 0:w], w1c[:, :], keep.st[:, at:at + w], start=True, stop=False)
                    nc.tensor.matmul(small[0:H, c % 2, 0:w], w1e[:, :], keep.xt[:, at:at + w], start=False, stop=True).then_inc(h1_done, 1)

                if fast:
                    pe.wait_ge(parts_ready, l * 3 + 3)
                for c, at, w in spans if fast else ():
                    if c >= 2:
                        pe.wait_ge(sum_left, l * NCH + (c - 1))
                    pe.nop(nofuse=True)
                    for b in range(NB):
                        last = nc.tensor.matmul(big[0:3 * H, c % 2, 0:w], parts[:, b, :, :].rearrange("p s h -> p (s h)"),
                                                keep.adj[:, c * UPC:c * UPC + w // UD, b, :], start=(b == 0), stop=(b == NB - 1))
                    last.then_inc(dense_done, 1)
                    if c >= 1:
                        perceptron_in(*spans[c - 1])
                for span in spans[NCH - 1:] if fast else spans:
                    perceptron_in(*span)
                keep_clock(IDLE[0])
                for c, at, w in spans:
                    pe.wait_ge(relu1, l * NCH + (c + 1))
                    if c >= 2:
                        pe.wait_ge(h2_left[c % 2], l * LEFT[c % 2] + c // 2)
                    pe.nop(nofuse=True)
                    nc.tensor.matmul(small[0:H, c % 2, 0:w], w2c[:, :], h1[:, at:at + w], start=True, stop=True).then_inc(h2_done, 1)
                keep_clock(IDLE[1])
                if not is_last:
                    pe.wait_ge(cur_ready, l + 2)
                for chunk, before in with_before(spans):
                    if chunk:
                        c, at, w = chunk
                        pe.wait_ge(relu2, l * NCH + (c + 1))
                        if c >= 2:
                            pe.wait_ge(xt_ready, l * NCH + (NCH + c - 1))
                        nc.tensor.matmul(big[:, c % 2, 0:w], w3c[:, :], h2[:, at:at + w], start=True, stop=True).then_inc(x_done, 1)
                    if before and not is_last:
                        c, at, w = before
                        pe.wait_ge(xt_ready, l * NCH + (NCH + c + 1))
                        project(at // P, -(-w // P))

            layers(pe, layer_of)

        @block.scalar
        def _(act):
            act.sem_inc(xt_ready, NCH)
            act.sem_inc(parts_ready, 3)
            act.sem_inc(excess_done, 1)
            act.sem_inc(primed, 1)
            def layer_of(l, is_last):
                def square_root(i):
                    act.wait_ge(primed, l * 2 + (i + 1))
                    act.nop(nofuse=True)
                    nc.scalar.activation(prime[:, :], keep.ident[0:1, 0:1], ACT.Sqrt).then_inc(primed, 1)
                    act.wait_ge(var_ready, l * 2 + (i + 1))
                    nc.scalar.activation(root[:, :], dev[:, i, :], ACT.Sqrt).then_inc(root_ready, 1)

                def left1(c, at, w):
                    act.wait_ge(h1_done, l * NCH + (c + 1))
                    nc.scalar.activation(h1[:, at:at + w], small[0:H, c % 2, 0:w], ACT.Identity, bias=vec[:, 0:1]).then_inc(h1_left, 1)

                for c, at, w in spans if fast else ():
                    act.wait_ge(excess_done, l * NCH + (c + 1))
                    act.nop(nofuse=True)
                    nc.scalar.activation(excess[:, :], keep.adj_bytes[:, bass.ds((l * NCH + c) * SLICE, SLICE)], ACT.Relu,
                                         bias=keep.fifteen[:, :], accum_out=keep.excess[:, bass.ds(l * NCH + c, 1)]).then_inc(excess_done, 1)
                    act.wait_ge(dense_done, l * NCH + (c + 1))
                    if c >= 2:
                        act.wait_ge(h1_done, l * NCH + (c - 1))
                    nc.scalar.activation(summed[:, c % 2, 0:w], big[0:3 * H, c % 2, 0:w], ACT.Copy).then_inc(sum_left, 1)
                    if c >= 1:
                        left1(*spans[c - 1])
                for span in spans[NCH - 1:] if fast else spans:
                    left1(*span)
                square_root(0)
                act.wait_ge(norm_ready, l * 2 + 1)

                def left2(c, at, w):
                    act.wait_ge(h2_done, l * NCH + (c + 1))
                    nc.scalar.activation(h2[:, at:at + w], small[0:H, c % 2, 0:w], ACT.Identity, bias=vec[:, 3:4]).then_inc(h2_left[1], 1)

                for c, at, w in spans:
                    nc.scalar.activation(h1[:, at:at + w], h1[:, at:at + w], ACT.Relu, bias=shift[:, 0, :], scale=scale[:, 0, :]).then_inc(relu1, 1)
                    if c >= 2 and c % 2 == 0:
                        left2(*spans[c - 1])
                square_root(1)
                act.wait_ge(norm_ready, l * 2 + 2)
                for c, at, w in spans:
                    nc.scalar.activation(h2[:, at:at + w], h2[:, at:at + w], ACT.Relu, bias=shift[:, 1, :], scale=scale[:, 1, :]).then_inc(relu2, 1)

            layers(act, layer_of)

        @block.gpsimd
        def _(pool):
            def other_weights(own):
                for i, a in enumerate((keep.b1, keep.g1, keep.bt1, keep.b2, keep.g2, keep.bt2)):
                    nc.gpsimd.tensor_copy(vec[:, i:i + 1], a[:, bass.ds(own, 1)])
                nc.gpsimd.tensor_copy(b3c[:, :], keep.b3[:, bass.ds(own, 1)])
                nc.gpsimd.tensor_copy(w2c[:, :], keep.w2t[:, bass.ds(own, 1), :].rearrange("p l o -> p (l o)"))
                nc.gpsimd.tensor_copy(w3c[:, :], keep.w3t[:, bass.ds(own, 1), :].rearrange("p l o -> p (l o)")).then_inc(layer_ready, 1)

            def layer_of(l, is_last):
                if not is_last:
                    pool.wait_ge(xt_ready, l * NCH + 2 * NCH)
                    pool.nop(nofuse=True)
                    other_weights(l + 1)

            other_weights(0 if fast else layer)
            layers(pool, layer_of)

        @block.vector
        def _(dve):
            ch = Chain(dve, chain)

            def first_weights(own):
                nc.vector.tensor_copy(w1c[:, :], keep.w1t[:, bass.ds(own * H, H)]).then_inc(chain, 1)
                nc.vector.tensor_scalar(gain[:, :], keep.eps[:, bass.ds(own, 1)], 1.0, None, ALU.add).then_inc(chain, 1)
                ch.n += 2
                dve.wait_ge(chain, ch.base + ch.n)
                if not isinstance(ch.base, int):
                    dve.nop(nofuse=True)
                nc.vector.tensor_scalar(w1e[:, :], w1c[:, :], gain[:, 0:1], None, ALU.mult).then_inc(cur_ready, 1)

            def split(l, i):
                dve.wait_ge(y_done, (l - 1) * 3 + (i + 1))
                split_piece(nc, ch, yps, rest, keep, i).then_inc(parts_ready, 1)

            first_weights(0 if fast else layer)
            dve.wait_ge(xt_ready, NCH)
            before = ch.n

            def layer_of(l, is_last):
                ch.base, ch.n = l * LAYER_STEPS + before, 0
                dve.wait_ge(layer_ready, l + 1)
                dve.nop(nofuse=True)

                def statistics(h, c, at, w):
                    w = min(w, N - at)
                    return nc.vector.bn_stats(stats[:, c, :], h[:, at:at + w])

                def norm(i):
                    ch.step(nc.vector.bn_aggr(mv[:, :], stats[:, :, :].rearrange("p c s -> p (c s)")))
                    nc.vector.tensor_scalar(dev[:, i, :], mv[:, 1:2], EPS, None, ALU.add).then_inc(var_ready, 1)
                    dve.wait_ge(root_ready, l * 2 + (i + 1))
                    ch.step(nc.vector.reciprocal(root[:, :], root[:, :]))
                    ch.step(nc.vector.tensor_tensor(scale[:, i, :], root[:, :], vec[:, 3 * i + 1:3 * i + 2], ALU.mult))
                    ch.step(nc.vector.tensor_tensor(mv[:, 0:1], mv[:, 0:1], scale[:, i, :], ALU.mult))
                    nc.vector.tensor_tensor(shift[:, i, :], vec[:, 3 * i + 2:3 * i + 3], mv[:, 0:1], ALU.subtract).then_inc(norm_ready, 1)

                for c, at, w in spans:
                    if fast and c < NCH - 1:
                        first, end = c * WC // (NCH - 1), (c + 1) * WC // (NCH - 1)
                        for x in range(first, end):
                            last = nc.vector.tensor_scalar(junk[:, x - first, :], keep.dkey[:, bass.ds(l, 1), :].rearrange("p g e -> p (g e)"),
                                                           float(x + 1), None, ALU.is_equal, ALU.add,
                                                           accum_out=keep.deg[:, bass.ds(l * WC + x, 1)])
                        ch.step(last)
                    dve.wait_ge(h1_left, l * NCH + (c + 1))
                    last = statistics(h1, c, at, w)
                ch.step(last)
                norm(0)
                if not is_last:
                    first_weights(l + 1)
                for c, at, w in spans:
                    if c % 2 == 0:
                        dve.wait_ge(h2_done, l * NCH + (c + 1))
                        nc.vector.tensor_scalar(h2[:, at:at + w], small[0:H, c % 2, 0:w], vec[:, 3:4], None, ALU.add).then_inc(h2_left[0], 1)
                    if c >= 1:
                        dve.wait_ge(h2_left[(c - 1) % 2], l * LEFT[(c - 1) % 2] + ((c - 1) // 2 + 1))
                        statistics(h2, *spans[c - 1])
                dve.wait_ge(h2_left[(NCH - 1) % 2], l * LEFT[(NCH - 1) % 2] + ((NCH - 1) // 2 + 1))
                ch.step(statistics(h2, *spans[NCH - 1]))
                norm(1)
                for c, at, w in spans:
                    dve.wait_ge(x_done, l * NCH + (c + 1))
                    nc.vector.tensor_scalar(keep.xt[:, at:at + w], big[:, c % 2, 0:w], b3c[:, 0:1], None, ALU.add).then_inc(xt_ready, 1)
                    if not is_last and c == 4:
                        split(l + 1, 0)
                if not is_last:
                    split(l + 1, 1)
                    split(l + 1, 2)
                    assert ch.n == LAYER_STEPS, ch.n

            layers(dve, layer_of)


IDLE = (18, 12)
LAYER_STEPS = 2 + 12 + NCH - 1 + 2 * 5
SLICE = NU * NB * UD // (L * NCH)
assert SLICE * L * NCH == NU * NB * UD


def load_tile(engine, keep, scratch, c, t):
    at, w = chunk_at(c)
    of = scratch.adj[at // UD:(at + w) // UD, :, :] if isinstance(c, int) else scratch.adj[bass.ds(c * UPC, UPC), :, :]
    engine.dma_start(keep.ring[:, t, 0:w // UD, :], of[:, :, t * NB * UD // 4:(t + 1) * NB * UD // 4].rearrange("u p f -> p u f")
                     ).then_inc(keep.tile_in[t], 16)


def normalise(nc, keep, out, name, scratch=None):
    with ExitStack() as ctx:
        m = Memory(nc, ctx, name)
        stats = m.sb("n_stats", [P, NB, 6], F32)
        mv = m.sb("n_mv", [P, NB, 2], F32)
        root = m.sb("n_root", [P, NB], F32)
        prime = m.sb("n_prime", [1, 1], F32)
        ps = m.ps("n_ps", [P, 2, 512])
        ps2 = m.ps("n_ps2", [P, 2, 512])
        degs = m.ps("n_degs", [T, 2, 512])
        turned = m.sem("n_turned")
        added = m.sem("n_added")
        normed = m.sem("n_normed")
        back = m.sem("n_back")
        back_left = m.sem("n_back_left")
        hi_ready = m.sem("n_hi_ready")
        stored = m.sem("n_stored")
        deg_turned = m.sem("n_deg_turned")
        deg_left = m.sem("n_deg_left")
        bias_ps = m.ps("n_bias_ps", [P, 2, 512])
        sums = m.sb("n_sums", [P, 2], F32)
        ones = m.sb("n_ones", [P, 1], F32)
        total = m.sb("n_total", [1, 4], F32)
        counted = m.sem("n_counted")
        totalled = m.sem("n_totalled")
        bias_done = m.sem("n_bias_done")
        bias_left = m.sem("n_bias_left")
        chain = m.sem("n_chain")
        eps_added = m.sem("n_eps_added")
        rooted = m.sem("n_rooted")
        block = ctx.enter_context(nc.Block())
        groups = node_groups()

        @block.tensor
        def _(pe):
            for q, b0, n in groups:
                if q >= 2:
                    pe.wait_ge(added, q - 1)
                for i in range(n):
                    last = nc.tensor.transpose(ps[:, q % 2, i * P:(i + 1) * P], keep.xt[:, (b0 + i) * P:(b0 + i + 1) * P], keep.ident[:, :])
                last.then_inc(turned, 1)
            if out is None:
                for d in range(WD):
                    if d >= 2:
                        pe.wait_ge(deg_left, d - 1)
                    for g in range(NWG):
                        seen = keep.deg[:, g * WC:(g + 1) * WC].rearrange("p (t d) -> p t d", d=WD)[:, :, d]
                        last = nc.tensor.transpose(degs[:, d % 2, g * P:(g + 1) * P], seen, keep.ident[:, :])
                    last.then_inc(deg_turned, 1)
            if scratch is not None:
                pe.wait_ge(deg_left, WD)
                for i in range(NCH):
                    if i >= 2:
                        pe.wait_ge(bias_left, i - 1)
                    w = chunk_width(i)
                    nc.tensor.matmul(bias_ps[:, i % 2, 0:w], keep.b_edge[:, :], keep.deg_row[:, i * CH:i * CH + w], start=True, stop=True
                                     ).then_inc(bias_done, 1)
            if out is None:
                for q, b0, n in groups:
                    pe.wait_ge(normed, q + 1)
                    if q >= 2:
                        pe.wait_ge(back_left, q - 1)
                    for i in range(n):
                        last = nc.tensor.transpose(ps2[:, q % 2, i * P:(i + 1) * P], keep.x_nm[:, b0 + i, :], keep.ident[:, :])
                    last.then_inc(back, 1)
            if scratch is not None:
                pe.wait_ge(counted, 1)
                nc.tensor.matmul(degs[0:1, 0, 0:2], ones[:, :], sums[:, :], start=True, stop=True).then_inc(totalled, 1)

        @block.vector
        def _(dve):
            ch = Chain(dve, chain)
            for q, b0, n in groups:
                dve.wait_ge(turned, q + 1)
                x = keep.x_nm[:, b0:b0 + n, :].rearrange("p b d -> p (b d)")
                nc.vector.tensor_tensor(x, ps[:, q % 2, 0:n * P], x, ALU.add).then_inc(added, 1)
                dve.wait_ge(added, q + 1)
                for b in range(b0, b0 + n):
                    last = nc.vector.bn_stats(stats[:, b, :], keep.x_nm[:, b, :])
                ch.step(last)
                for b in range(b0, b0 + n):
                    last = nc.vector.bn_aggr(mv[:, b, :], stats[:, b, :])
            ch.step(last)
            nc.vector.tensor_scalar(root[:, :], mv[:, :, 1], EPS, None, ALU.add).then_inc(eps_added, 1)
            dve.wait_ge(rooted, 1)
            ch.step(nc.vector.reciprocal(root[:, :], root[:, :]))
            for q, b0, n in groups:
                for b in range(b0, b0 + n):
                    last = nc.vector.tensor_scalar(keep.x_nm[:, b, :], keep.x_nm[:, b, :], mv[:, b, 0:1], root[:, b:b + 1],
                                                   ALU.subtract, ALU.mult)
                last.then_inc(normed, 1)
            if out is None:
                for q, b0, n in groups:
                    dve.wait_ge(hi_ready, q + 1)
                    nc.vector.scalar_tensor_tensor(out=keep.halves[:, 0, b0:b0 + n, 1, :], in0=keep.x_nm[:, b0:b0 + n, :], scalar=SPLIT,
                                                   in1=keep.halves[:, 0, b0:b0 + n, 0, :], op0=ALU.mult, op1=ALU.subtract)
            if scratch is not None:
                nc.vector.memset(ones[:, :], 1.0)
                nc.vector.tensor_reduce(sums[:, 0:1], keep.deg[:, :], AX.X, ALU.add)
                nc.vector.tensor_reduce(sums[:, 1:2], keep.excess[:, :], AX.X, ALU.add).then_inc(counted, 1)
                dve.wait_ge(totalled, 1)
                ch.step(nc.vector.tensor_copy(total[:, 0:2], degs[0:1, 0, 0:2]))
                ch.step(nc.vector.tensor_scalar(total[:, 2:3], total[:, 0:1], float(E), None, ALU.not_equal))
                ch.step(nc.vector.tensor_tensor(total[:, 3:4], total[:, 2:3], total[:, 1:2], ALU.add))
                ch.step(nc.vector.tensor_scalar(keep.amiss[:, :], total[:, 3:4], 0.0, None, ALU.is_gt))

        @block.scalar
        def _(act):
            if out is None:
                for d in range(WD):
                    act.wait_ge(deg_turned, d + 1)
                    row = keep.deg_row[:, :].rearrange("t (w d) -> t w d", d=WD)[:, :, d]
                    nc.scalar.activation(row, degs[:, d % 2, :], ACT.Copy).then_inc(deg_left, 1)
            nc.scalar.activation(prime[:, :], keep.ident[0:1, 0:1], ACT.Sqrt)
            act.wait_ge(eps_added, 1)
            nc.scalar.activation(root[:, :], root[:, :], ACT.Sqrt).then_inc(rooted, 1)
            if out is None:
                for q, b0, n in groups:
                    act.wait_ge(normed, q + 1)
                    nc.scalar.activation(keep.halves[:, 0, b0:b0 + n, 0, :], keep.x_nm[:, b0:b0 + n, :], ACT.Copy, scale=SPLIT).then_inc(hi_ready, 1)
                    if scratch is not None:
                        w = chunk_width(q)
                        act.wait_ge(bias_done, q + 1)
                        nc.scalar.activation(keep.a_bias[:, q * CH:q * CH + w], bias_ps[:, q % 2, 0:w], ACT.Copy).then_inc(bias_left, 1)
                for q, b0, n in groups:
                    act.wait_ge(back, q + 1)
                    nc.scalar.activation(keep.xt[:, b0 * P:(b0 + n) * P], ps2[:, q % 2, 0:n * P], ACT.Copy).then_inc(back_left, 1)

        @block.sync
        def _(sp):
            if scratch is not None:
                for t in range(T):
                    load_tile(sp, keep, scratch, 0, t)
            if out is not None:
                for q0, q1 in ((0, 4), (4, len(groups) - 1)):
                    sp.wait_ge(normed, q1)
                    sp.dma_start(out[q0 * 4 * P:q1 * 4 * P, :].rearrange("(b p) d -> p b d", p=P),
                                 keep.x_nm[:, 4 * q0:4 * q1, :]).then_inc(stored, 16)
                sp.wait_ge(normed, len(groups))
                sp.dma_start(out[(NB - 1) * P:N, :], keep.x_nm[0:LAST, NB - 1, :]).then_inc(stored, 16)
                sp.wait_ge(stored, 48)


FULL = 4
REST = -(-(NB - FULL * CH // P) // (NCH - FULL)) * P


def chunk_at(c):
    if not isinstance(c, int) or c < FULL:
        return c * CH, CH
    at = FULL * CH + (c - FULL) * REST
    return at, min(REST, NPAD - at)


assert sum(chunk_at(c)[1] for c in range(NCH)) == NPAD


def second_network(nc, keep, scratch):
    with ExitStack() as ctx:
        m = Memory(nc, ctx)
        ring = keep.ring
        ring8 = ring[:, :, :, :].rearrange("p t u f -> p (t u f)").bitcast(F8).rearrange(
            "p (t u b d) -> p t u b d", t=T, u=UPC, b=NB)
        near = m.sb("near", [D, T, CH], F32)
        a_sb = m.sb("a_sb", [D, CH], F32)
        r_sb = m.sb("r_sb", [D, CH], F32)
        z_sb = m.sb("z_sb", [D, CH], F32)
        n_sb = m.sb("n_sb", [D, CH], F32)
        u_sb = m.sb("u_sb", [D, CH], F32)
        h_new = m.sb("h_new", [D, CH], F32)
        b_rz = m.sb("b_rz", [D, 2], F32)
        near_ps = m.ps("near_ps", [D, 2, CH])
        a_ps = m.ps("a_ps", [D, CH])
        rz_ps = m.ps("rz_ps", [D, 2, CH])
        in_ps = m.ps("in_ps", [D, CH])
        hn_ps = m.ps("hn_ps", [D, CH])
        t_ps = m.ps("t_ps", [P, CH])

        tile_in = keep.tile_in
        tile_done = m.sem("tile_done")
        near_left = m.sem("near_left")
        a_done = m.sem("a_done")
        a_left = m.sem("a_left")
        gates_done = m.sem("gates_done")
        rz_done = m.sem("rz_done")
        cand_done = m.sem("cand_done")
        n_done = m.sem("n_done")
        h_done = m.sem("h_done")
        t_done = m.sem("t_done")
        hi_done = m.sem("hi_done")
        lo_done = m.sem("lo_done")
        chain = m.sem("l1_chain")
        bias_ready = m.sem("bias_ready")
        block = ctx.enter_context(nc.Block())

        def steps(eng, chunk):
            with eng.Fori(0, STEPS, 2) as s0:
                for parity in range(2):
                    s = s0 + parity
                    chunk(s, 0, parity)
                    with eng.Fori(1, FULL, 1) as c:
                        chunk(s, c, parity)
                    for c in range(FULL, NCH):
                        chunk(s, c, parity)

        def steps_and_tails(eng, chunk, tail):
            def both(s, c, parity):
                k = s * NCH + c
                if not isinstance(c, int) or c:
                    chunk(s, c, parity, lambda i: tail(i, k - 1, c - 1, parity))
                elif parity:
                    chunk(s, c, parity, lambda i: tail(i, k - 1, NCH - 1, 1 - parity))
                else:
                    def guarded(i):
                        with eng.If(s > 0):
                            tail(i, k - 1, NCH - 1, 1 - parity)
                    chunk(s, c, parity, guarded)

            steps(eng, both)

        def cols(c):
            at, w = chunk_at(c)
            return slice(at, at + w) if isinstance(c, int) else bass.ds(at, w)

        def half(parity, c, i):
            at, w = chunk_at(c)
            nb = -(-w // P)
            return keep.halves[:, parity, bass.ds(c * (CH // P), nb), i, :] if not isinstance(c, int) else \
                keep.halves[:, parity, at // P:at // P + nb, i, :]

        @block.sync
        def _(sp):
            def chunk(s, c, parity):
                k = s * NCH + c
                for t in range(T):
                    sp.wait_ge(tile_done, k * T + (t + 1))
                    sp.nop(nofuse=True)
                    load_tile(sp, keep, scratch, c, t)

            def all_but_first(s, c, parity):
                if isinstance(c, int) and c == 0 and parity == 0:
                    with sp.If(s > 0):
                        chunk(s, c, parity)
                else:
                    chunk(s, c, parity)

            steps(sp, all_but_first)

        @block.tensor
        def _(pe):
            pe.sem_inc(tile_done, T)
            pe.sem_inc(a_done, 1)
            pe.sem_inc(gates_done, 1)
            pe.sem_inc(t_done, 1)
            pe.wait_ge(bias_ready, 1)

            def messages(k, c, parity):
                w = chunk_at(c)[1]
                pe.wait_ge(near_left, k * T + (T + 2))
                pe.wait_ge(a_left, k + 1)
                for t in range(T):
                    last = nc.tensor.matmul(a_ps[:, 0:w], keep.wet[:, t, :], near[:, t, 0:w], start=(t == 0), stop=(t == T - 1))
                last.then_inc(a_done, 1)

            def gates(k, c, parity):
                w = chunk_at(c)[1]
                pe.wait_ge(a_left, k + 2)
                pe.wait_ge(n_done, k + 1)
                h = keep.xt[:, cols(c)]
                for g in range(2):
                    nc.tensor.matmul(rz_ps[:, g, 0:w], keep.wht[:, g, :], h, start=True, stop=False)
                    nc.tensor.matmul(rz_ps[:, g, 0:w], keep.wit[:, g, :], a_sb[:, 0:w], start=False, stop=True)
                nc.tensor.matmul(hn_ps[:, 0:w], keep.wht[:, 2, :], h, start=True, stop=True)
                nc.tensor.matmul(in_ps[:, 0:w], keep.wit[:, 2, :], a_sb[:, 0:w], start=True, stop=True).then_inc(gates_done, 1)

            def turn(k, c, parity):
                w = chunk_at(c)[1]
                pe.wait_ge(h_done, k + 2)
                pe.wait_ge(hi_done, k + NCH)
                pe.wait_ge(lo_done, k + NCH)
                for i in range(-(-w // P)):
                    last = nc.tensor.transpose(t_ps[:, i * P:(i + 1) * P], h_new[:, i * P:(i + 1) * P], keep.ident[:, :])
                last.then_inc(t_done, 1)

            def tail(i, k, c, parity):
                (messages, gates, turn)[i](k, c, parity)

            def chunk(s, c, parity, tail):
                k = s * NCH + c
                w = chunk_at(c)[1]

                def tile(t, b0=0, b1=NB):
                    if b0 == 0:
                        pe.wait_ge(tile_in[t], k * 16 + 16)
                        pe.wait_ge(near_left, k * T + (t + 1))
                        pe.nop(nofuse=True)
                    for b in range(b0, b1):
                        if b in turned_at and isinstance(c, int) and c == 0:
                            pe.wait_ge(hi_done, s * NCH + (turned_at[b] + 1))
                            pe.wait_ge(lo_done, s * NCH + (turned_at[b] + 1))
                            pe.nop(nofuse=True)
                        for i in range(2):
                            last = nc.tensor.matmul(near_ps[:, t % 2, 0:w], keep.halves[:, parity, b, i, :],
                                                    ring8[:, t, 0:w // UD, b, :], start=(b == 0 and i == 0),
                                                    stop=(b == NB - 1 and i == 1))
                    if b1 == NB:
                        last.then_inc(tile_done, 1)

                if isinstance(c, int) and c == 0:
                    known = chunk_at(NCH - 1)[0] // P
                    tile(0, 0, 4)
                    tail(0)
                    tile(0, 4, 12)
                    tail(1)
                    tile(0, 12, known)
                    tile(1, 0, known - 6)
                    tail(2)
                    tile(1, known - 6, known)
                    tile(0, known)
                    tile(1, known)
                    tile(2)
                    tile(3)
                else:
                    for t in range(T):
                        tile(t)
                        if t < 3:
                            tail(t)

            turned_at = {chunk_at(c)[0] // P: c for c in range(NCH)}
            steps_and_tails(pe, chunk, tail)
            messages(STEPS * NCH - 1, NCH - 1, 1)
            gates(STEPS * NCH - 1, NCH - 1, 1)

        @block.scalar
        def _(act):
            act.sem_inc(near_left, 2)
            act.sem_inc(n_done, 1)
            act.sem_inc(hi_done, NCH)
            act.sem_inc(rz_done, 1)
            act.wait_ge(bias_ready, 1)

            def sums(k, t, w):
                act.wait_ge(tile_done, k * T + (T + t + 1))
                act.wait_ge(a_done, k + 1)
                nc.scalar.activation(near[:, t, 0:w], near_ps[:, t % 2, 0:w], ACT.Copy, scale=1.0 / SPLIT).then_inc(near_left, 1)

            def gates(k, c, parity):
                w = chunk_at(c)[1]
                act.wait_ge(gates_done, k + 2)
                act.wait_ge(h_done, k + 1)
                nc.scalar.activation(r_sb[:, 0:w], rz_ps[:, 0, 0:w], ACT.Sigmoid, bias=b_rz[:, 0:1]).then_inc(rz_done, 1)
                nc.scalar.activation(z_sb[:, 0:w], rz_ps[:, 1, 0:w], ACT.Sigmoid, bias=b_rz[:, 1:2])
                act.wait_ge(cand_done, k + 2)
                nc.scalar.activation(n_sb[:, 0:w], n_sb[:, 0:w], ACT.Tanh, bias=keep.b_ih[:, 2:3]).then_inc(n_done, 1)

            def turn(k, c, parity):
                nb = -(-chunk_at(c)[1] // P)
                act.wait_ge(t_done, k + 2)
                nc.scalar.activation(half(1 - parity, c, 0), t_ps[:, 0:nb * P].rearrange("p (b d) -> p b d", d=D), ACT.Copy, scale=SPLIT
                                     ).then_inc(hi_done, 1)

            def tail(i, k, c, parity):
                (gates, turn)[i](k, c, parity)

            def chunk(s, c, parity, tail):
                k = s * NCH + c
                w = chunk_at(c)[1]
                if isinstance(c, int) and c == 0:
                    tail(0)
                    tail(1)
                    for t in range(T):
                        sums(k, t, w)
                else:
                    sums(k, 0, w)
                    sums(k, 1, w)
                    tail(0)
                    sums(k, 2, w)
                    tail(1)
                    sums(k, 3, w)

            steps_and_tails(act, chunk, tail)
            gates(STEPS * NCH - 1, NCH - 1, 1)

        @block.vector
        def _(dve):
            dve.sem_inc(a_left, 1)
            dve.sem_inc(h_done, 1)
            dve.sem_inc(lo_done, NCH)
            nc.vector.tensor_tensor(b_rz[:, :], keep.b_ih[:, 0:2], keep.b_hh[:, 0:2], ALU.add)
            nc.vector.memset(h_new[:, :], 0.0).then_inc(bias_ready, 1)
            dve.wait_ge(bias_ready, 1)
            OWN = 4
            dve.sem_inc(chain, OWN)
            dve.sem_inc(cand_done, 1)

            def messages(k, c, parity):
                w = chunk_at(c)[1]
                dve.wait_ge(a_done, k + 2)
                dve.wait_ge(gates_done, k + 1)
                dve.nop(nofuse=True)
                nc.vector.tensor_tensor(a_sb[:, 0:w], a_ps[:, 0:w], keep.a_bias[:, cols(c)], ALU.add).then_inc(a_left, 1)

            def unit(k, c, parity):
                w = chunk_at(c)[1]
                own = (k + 1) * OWN
                dve.wait_ge(rz_done, k + 2)
                nc.vector.scalar_tensor_tensor(out=u_sb[:, 0:w], in0=hn_ps[:, 0:w], scalar=keep.b_hh[:, 2:3], in1=r_sb[:, 0:w],
                                               op0=ALU.add, op1=ALU.mult).then_inc(chain, 1)
                dve.wait_ge(chain, own + 1)
                nc.vector.tensor_tensor(n_sb[:, 0:w], in_ps[:, 0:w], u_sb[:, 0:w], ALU.add).then_inc(cand_done, 1)
                dve.wait_ge(n_done, k + 2)
                h = keep.xt[:, cols(c)]
                nc.vector.tensor_tensor(u_sb[:, 0:w], h, n_sb[:, 0:w], ALU.subtract).then_inc(chain, 1)
                dve.wait_ge(chain, own + 2)
                nc.vector.tensor_tensor(u_sb[:, 0:w], u_sb[:, 0:w], z_sb[:, 0:w], ALU.mult).then_inc(chain, 1)
                dve.wait_ge(chain, own + 3)
                dve.wait_ge(t_done, k + 1)
                nc.vector.tensor_tensor(h_new[:, 0:w], u_sb[:, 0:w], n_sb[:, 0:w], ALU.add).then_inc(h_done, 1)
                dve.wait_ge(h_done, k + 2)
                dve.nop(nofuse=True)
                nc.vector.tensor_copy(keep.xt[:, cols(c)], h_new[:, 0:w]).then_inc(chain, 1)

            def turn(k, c, parity):
                nb = -(-chunk_at(c)[1] // P)
                dve.wait_ge(t_done, k + 2)
                dve.wait_ge(hi_done, k + (NCH + 1))
                nc.vector.scalar_tensor_tensor(out=half(1 - parity, c, 1), in0=t_ps[:, 0:nb * P].rearrange("p (b d) -> p b d", d=D), scalar=SPLIT,
                                               in1=half(1 - parity, c, 0), op0=ALU.mult, op1=ALU.subtract).then_inc(lo_done, 1)

            def tail(i, k, c, parity):
                messages(k, c, parity)
                unit(k, c, parity)
                turn(k, c, parity)

            steps_and_tails(dve, lambda s, c, parity, tail: tail(0), tail)
            messages(STEPS * NCH - 1, NCH - 1, 1)
            unit(STEPS * NCH - 1, NCH - 1, 1)




def reload(nc, ins, keep, scratch):
    with ExitStack() as ctx:
        m = Memory(nc, ctx, "reload_")
        fields = m.sb("fields", [EP, BPP, 4, EB], F32)
        sel_i = m.sb("sel_i", [T, T * P], I32)
        ps = m.ps("ps", [P, 2, 512])
        loaded = m.sem("loaded")
        cleared = m.sem("cleared")
        turned = m.sem("turned")
        left = m.sem("left")
        chain = m.sem("chain")
        block = ctx.enter_context(nc.Block())

        @block.sync
        def _(sp):
            sp.wait_ge(cleared, 1)
            sp.dma_start(keep.x_nm[:, 0:NB - 1, :], ins["x"][0:(NB - 1) * P, :].rearrange("(b p) d -> p b d", p=P)).then_inc(loaded, 16)
            sp.dma_start(keep.x_nm[0:LAST, NB - 1, :], ins["x"][(NB - 1) * P:N, :]).then_inc(loaded, 16)
            sp.dma_start(fields[:, :, :, :].rearrange("p b a e -> p b (a e)"),
                         scratch.fields[0:NEB, :].rearrange("(p b) f -> p b f", p=EP)).then_inc(loaded, 16)

        @block.gpsimd
        def _(pool):
            nc.gpsimd.memset(keep.x_nm[:, NB - 1, :], 0.0).then_inc(cleared, 1)
            nc.gpsimd.iota(keep.nodes[:, :], [[1, NCOL]], base=0, channel_multiplier=0).then_inc(cleared, 1)
            nc.gpsimd.iota(sel_i[:, :], [[1, T * P]], base=0, channel_multiplier=-P).then_inc(cleared, 1)

        @block.vector
        def _(dve):
            ch = Chain(dve, chain)
            dve.wait_ge(loaded, 48)
            dve.wait_ge(cleared, 3)

            def blocks(a):
                return a.rearrange("p (b e) -> p b e", e=EB)

            dv = blocks(keep.edge_dst[:, :])
            nc.vector.tensor_copy(dv, fields[:, :, 0, :])
            ch.step(nc.vector.scalar_tensor_tensor(out=blocks(keep.node_f[:, :]), in0=fields[:, :, 1, :], scalar=float(P) / WD,
                                                   in1=fields[:, :, 3, :], op0=ALU.mult, op1=ALU.add))
            nc.vector.tensor_copy(keep.src_row[:, 0, :], keep.node_f[:, :])
            nc.vector.scalar_tensor_tensor(out=blocks(keep.src_row[:, 1, :]), in0=fields[:, :, 2, :], scalar=float(NCOL) / TYW,
                                           in1=blocks(keep.node_f[:, :]), op0=ALU.mult, op1=ALU.add)
            ch.step(nc.vector.tensor_scalar(keep.select[:, :], sel_i[:, :], 0.0, None, ALU.is_ge))
            ch.step(nc.vector.scalar_tensor_tensor(out=keep.select[:, :], in0=sel_i[:, :], scalar=float(P), in1=keep.select[:, :],
                                                   op0=ALU.is_lt, op1=ALU.mult))

        @block.tensor
        def _(pe):
            pe.wait_ge(loaded, 48)
            for q, b0, n in node_groups():
                if q >= 2:
                    pe.wait_ge(left, q - 1)
                for i in range(n):
                    last = nc.tensor.transpose(ps[:, q % 2, i * P:(i + 1) * P], keep.x_nm[:, b0 + i, :], keep.ident[:, :])
                last.then_inc(turned, 1)

        @block.scalar
        def _(act):
            for q, b0, n in node_groups():
                act.wait_ge(turned, q + 1)
                nc.scalar.activation(keep.xt[:, b0 * P:(b0 + n) * P], ps[:, q % 2, 0:n * P], ACT.Copy).then_inc(left, 1)


def gather_sums(nc, keep, scratch, typed):
    with ExitStack() as ctx:
        m = Memory(nc, ctx, "typed_" if typed else "plain_", again=True)
        table = m.sb("table", [P, NB, D], F32)
        ps = m.ps("ps", [P, 7, 512])
        made = m.sem("made")
        left = m.sem("left")
        stored = m.sem("stored")
        row = m.sb("row", [EP, 1], U32)
        message = m.sb("message", [EP, D], F32)
        hot = m.sb("hot", [EP, NCOL], F32)
        total = m.sb("total", [P, NB * D], F32)
        row_ready = m.sem("row_ready")
        hot_ready = m.sem("hot_ready")
        gathered = m.sem("gathered")
        multiplied = m.sem("multiplied")
        added = m.sem("added")
        types = T if typed else 1
        SLICES = len(node_groups())
        block = ctx.enter_context(nc.Block())

        @block.tensor
        def _(pe):
            for t in range(types):
                if t:
                    pe.wait_ge(left, SLICES * t)
                for q, b0, n in node_groups():
                    for i in range(n):
                        cell = ps[:, q, i * P:(i + 1) * P]
                        nodes = keep.xt[:, (b0 + i) * P:(b0 + i + 1) * P]
                        if typed:
                            nc.tensor.matmul(cell, nodes, keep.wet[:, t, :], start=True, stop=False)
                            last = nc.tensor.matmul(cell, keep.select[:, t * P:(t + 1) * P], keep.b_edge[:, :], start=False, stop=True)
                        else:
                            last = nc.tensor.transpose(cell, nodes, keep.ident[:, :])
                    last.then_inc(made, 1)
            pe.wait_ge(left, SLICES * types)
            with pe.Fori(0, EF, 1) as j:
                pe.wait_ge(gathered, j * 16 + 16)
                pe.nop(nofuse=True)
                pe.wait_ge(hot_ready, j + 1)
                pe.nop(nofuse=True)
                for b in range(NB):
                    last = nc.tensor.matmul(ps[:, b // 4, (b % 4) * D:(b % 4 + 1) * D], hot[:, b * P:(b + 1) * P], message[:, :],
                                            start=True, stop=True)
                last.then_inc(multiplied, 1)
            pe.wait_ge(added, (EF + 1))
            for q, b0, n in node_groups():
                for i in range(n):
                    last = nc.tensor.transpose(ps[:, q, i * P:(i + 1) * P], total[:, (b0 + i) * D:(b0 + i + 1) * D], keep.ident[:, :])
                last.then_inc(made, 1)

        @block.scalar
        def _(act):
            for t in range(types):
                if t:
                    act.wait_ge(stored, 16 * t)
                for q, b0, n in node_groups():
                    act.wait_ge(made, SLICES * t + q + 1)
                    nc.scalar.activation(table[:, b0:b0 + n, :].rearrange("p b d -> p (b d)"), ps[:, q, 0:n * D], ACT.Copy).then_inc(left, 1)
            for q, b0, n in node_groups():
                act.wait_ge(made, SLICES * types + q + 1)
                nc.scalar.activation(keep.st[:, b0 * P:(b0 + n) * P], ps[:, q, 0:n * P], ACT.Copy)

        @block.sync
        def _(sp):
            for t in range(types):
                sp.wait_ge(left, SLICES * (t + 1))
                sp.dma_start(scratch.table[t * NCOL:(t + 1) * NCOL, :].rearrange("(b p) d -> p b d", p=P), table[:, :, :]).then_inc(stored, 16)

        @block.gpsimd
        def _(pool):
            pool.wait_ge(stored, 16 * types)
            with pool.Fori(0, EF, 1) as j:
                pool.wait_ge(row_ready, j + 1)
                pool.nop(nofuse=True)
                nc.gpsimd.indirect_dma_start(message[:, :], None, scratch.table[0:types * NCOL, :],
                                             bass.IndirectOffsetOnAxis(ap=row[:, :], axis=0)).then_inc(gathered, 16)

        @block.vector
        def _(dve):
            nc.vector.memset(total[:, :], 0.0).then_inc(added, 1)
            with dve.Fori(0, EF, 1) as j:
                dve.wait_ge(added, j + 1)
                dve.nop(nofuse=True)
                nc.vector.tensor_copy(row[:, :], keep.src_row[:, 1 if typed else 0, bass.ds(j, 1)]).then_inc(row_ready, 1)
                nc.vector.tensor_scalar(hot[:, :], keep.nodes[0:EP, :], keep.edge_dst[:, bass.ds(j, 1)], None, ALU.is_equal).then_inc(hot_ready, 1)
                dve.wait_ge(multiplied, j + 1)
                dve.nop(nofuse=True)
                for q, b0, n in node_groups():
                    s = total[:, b0 * D:(b0 + n) * D]
                    last = nc.vector.tensor_tensor(s, ps[:, q, 0:n * D], s, ALU.add)
                last.then_inc(added, 1)


def gated_unit(nc, keep):
    with ExitStack() as ctx:
        m = Memory(nc, ctx, "unit_", again=True)
        r = m.sb("r", [D, CH], F32)
        z = m.sb("z", [D, CH], F32)
        n = m.sb("n", [D, CH], F32)
        u = m.sb("u", [D, CH], F32)
        b_rz = m.sb("b_rz", [D, 2], F32)
        rz_ps = m.ps("rz_ps", [D, 2, CH])
        in_ps = m.ps("in_ps", [D, CH])
        hn_ps = m.ps("hn_ps", [D, CH])
        gates = m.sem("gates")
        bias_ready = m.sem("bias_ready")
        rz = m.sem("rz")
        cand = m.sem("cand")
        act_n = m.sem("act_n")
        h_done = m.sem("h_done")
        chain = m.sem("chain")
        block = ctx.enter_context(nc.Block())

        @block.tensor
        def _(pe):
            for c in range(NCH):
                w = chunk_width(c)
                h, a = keep.xt[:, c * CH:c * CH + w], keep.st[:, c * CH:c * CH + w]
                if c:
                    pe.wait_ge(h_done, c)
                for g in range(2):
                    nc.tensor.matmul(rz_ps[:, g, 0:w], keep.wht[:, g, :], h, start=True, stop=False)
                    nc.tensor.matmul(rz_ps[:, g, 0:w], keep.wit[:, g, :], a, start=False, stop=True)
                nc.tensor.matmul(hn_ps[:, 0:w], keep.wht[:, 2, :], h, start=True, stop=True)
                nc.tensor.matmul(in_ps[:, 0:w], keep.wit[:, 2, :], a, start=True, stop=True).then_inc(gates, 1)

        @block.scalar
        def _(act):
            act.wait_ge(bias_ready, 1)
            for c in range(NCH):
                w = chunk_width(c)
                act.wait_ge(gates, c + 1)
                nc.scalar.activation(r[:, 0:w], rz_ps[:, 0, 0:w], ACT.Sigmoid, bias=b_rz[:, 0:1])
                nc.scalar.activation(z[:, 0:w], rz_ps[:, 1, 0:w], ACT.Sigmoid, bias=b_rz[:, 1:2]).then_inc(rz, 1)
                act.wait_ge(cand, c + 1)
                nc.scalar.activation(n[:, 0:w], n[:, 0:w], ACT.Tanh, bias=keep.b_ih[:, 2:3]).then_inc(act_n, 1)

        @block.vector
        def _(dve):
            ch = Chain(dve, chain)
            nc.vector.tensor_tensor(b_rz[:, :], keep.b_ih[:, 0:2], keep.b_hh[:, 0:2], ALU.add).then_inc(bias_ready, 1)
            for c in range(NCH):
                w = chunk_width(c)
                h = keep.xt[:, c * CH:c * CH + w]
                dve.wait_ge(rz, c + 1)
                ch.step(nc.vector.scalar_tensor_tensor(out=u[:, 0:w], in0=hn_ps[:, 0:w], scalar=keep.b_hh[:, 2:3], in1=r[:, 0:w],
                                                       op0=ALU.add, op1=ALU.mult))
                nc.vector.tensor_tensor(n[:, 0:w], in_ps[:, 0:w], u[:, 0:w], ALU.add).then_inc(cand, 1)
                dve.wait_ge(act_n, c + 1)
                ch.step(nc.vector.tensor_tensor(u[:, 0:w], h, n[:, 0:w], ALU.subtract))
                ch.step(nc.vector.tensor_tensor(u[:, 0:w], u[:, 0:w], z[:, 0:w], ALU.mult))
                nc.vector.tensor_tensor(h, u[:, 0:w], n[:, 0:w], ALU.add).then_inc(h_done, 1)


def general(nc, ins, keep, scratch, out):
    with ExitStack() as ctx:
        m = Memory(nc, ctx, "general_")
        keep.nodes = m.sb("nodes", [P, NCOL], I32)
        keep.edge_dst = m.sb("edge_dst", [EP, EF], F32)
        keep.node_f = m.sb("node_f", [EP, EF], F32)
        keep.src_row = m.sb("src_row", [EP, 2, EF], U32)
        keep.select = m.sb("select", [T, T * P], F32)
        keep.st = m.sb("st", [D, NCOL], F32)
        reload(nc, ins, keep, scratch)
        with nc.Fori(0, L, 1) as l:
            gather_sums(nc, keep, scratch, False)
            first_network(nc, keep, l)
        normalise(nc, keep, None, "general_middle_")
        with nc.Fori(0, STEPS, 1):
            gather_sums(nc, keep, scratch, True)
            gated_unit(nc, keep)
        normalise(nc, keep, out, "general_end_")


class Kept:

    def __init__(self, m):
        self.ident = m.sb("ident", [P, P], F32)
        self.ident16 = m.sb("ident16", [P, P], BF16)
        self.sum3 = m.sb("sum3", [3 * H, H], F32)
        self.iota = m.sb("iota", [P, T * TYW], F16)
        self.iota1 = m.sb("iota1", [P, P], F16)
        self.w1t = m.sb("w1t", [D, L * H], F32)
        self.w2t = m.sb("w2t", [H, L, H], F32)
        self.w3t = m.sb("w3t", [H, L, D], F32)
        self.wet = m.sb("wet", [D, T, D], F32)
        self.wit = m.sb("wit", [D, 3, D], F32)
        self.wht = m.sb("wht", [D, 3, D], F32)
        self.b_edge = m.sb("b_edge", [T, D], F32)
        self.b_ih = m.sb("b_ih", [D, 3], F32)
        self.b_hh = m.sb("b_hh", [D, 3], F32)
        self.eps = m.sb("eps", [P, L], F32)
        self.b1 = m.sb("b1", [H, L], F32)
        self.g1 = m.sb("g1", [H, L], F32)
        self.bt1 = m.sb("bt1", [H, L], F32)
        self.b2 = m.sb("b2", [H, L], F32)
        self.g2 = m.sb("g2", [H, L], F32)
        self.bt2 = m.sb("bt2", [H, L], F32)
        self.b3 = m.sb("b3", [D, L], F32)
        self.x_nm = m.sb("x_nm", [P, NB, D], F32)
        self.xt = m.sb("xt", [D, NCOL], F32)
        self.fifteen = m.sb("fifteen", [P, 1], F32)
        self.amiss = m.sb("amiss", [1, 1], I32)
        self.deg = m.sb("deg", [P, NWG * WC], F32)
        self.excess = m.sb("excess_sum", [P, L * NCH], F32)


class Scratch:

    def __init__(self, nc):
        self.fields = nc.dram_tensor("edge_fields", (NEB + BPW - 1, 4 * EB), F32).ap()
        self.table = nc.dram_tensor("messages", (T * NCOL, D), F32).ap()
        self.adj = nc.dram_tensor("adjacency", (NU, P, T * NB * UD // 4), F32).ap()


def gnn(nc, ins, out):
    scratch = Scratch(nc)
    with ExitStack() as ctx:
        keep = Kept(Memory(nc, ctx))
        with ExitStack() as first:
            m = Memory(nc, first)
            keep.dkey = m.sb("dkey", [P, NWG, TPW * P], F16)
            keep.key = m.sb("key", [P, 2, TPW, NWG * P], F32)
            keep.row = m.sb("row", [P, NWG, BPW], U32)
            keep.w8 = m.sb("w8", [P, NWG], F32)
            keep.parts = m.sb("parts", [P, NB, 3, H], BF16)
            prepare(nc, ins, keep, scratch)
            keep.adj_words = m.sb("adj", [P, NU, NB * UD // 4], F32)
            words = keep.adj_words[:, :, :].rearrange("p u f -> p (u f)")
            keep.adj = words.bitcast(F8).rearrange("p (u b d) -> p u b d", u=NU, b=NB)
            keep.adj_bytes = words.bitcast(mybir.dt.uint8)
            build(nc, keep, scratch)
            first_network(nc, keep)
        with ExitStack() as second:
            m = Memory(nc, second)
            keep.deg_row = m.sb("deg_row", [T, NWG * P * WD], F32)
            keep.halves = m.sb("halves", [P, 2, NB, 2, D], F16)
            with ExitStack() as fast:
                m = Memory(nc, fast)
                keep.a_bias = m.sb("a_bias", [D, NPAD], F32)
                keep.ring = m.sb("ring", [P, T, UPC, NB * UD // 4], F32)
                keep.tile_in = [m.sem(f"tile_in{t}") for t in range(T)]
                normalise(nc, keep, None, "middle_", scratch)
                second_network(nc, keep, scratch)
            normalise(nc, keep, out, "end_")
            amiss = nc.values_load(keep.amiss[0:1, 0:1], min_val=0, max_val=1)
            with nc.If(amiss > 0):
                general(nc, ins, keep, scratch, out)


def kernel(**inputs):
    import numpy as np
    import concourse.bacc as _bacc
    from concourse.bass_utils import run_bass_kernel_spmd as _run

    nc = _bacc.Bacc("TRN2", target_bir_lowering=False, num_devices=1)
    arrays, aps = {}, {}
    for name, a in inputs.items():
        a = np.ascontiguousarray(a)
        arrays["in_" + name] = a
        aps[name] = nc.dram_tensor("in_" + name, a.shape, mybir.dt.from_np(a.dtype), kind="ExternalInput").ap()
    out = nc.dram_tensor("out", (N, D), F32, kind="ExternalOutput").ap()
    gnn(nc, aps, out)
    r = _run(nc, [arrays], core_ids=[0])
    return r.results[0]["out"]
```
